# Optimizing a Trainium2 kernel written in Bass

```python
import numpy as np
import jax
import jax.numpy as jnp

def _softmax(x, axis=-1):
    return jax.nn.softmax(x, axis=axis)

def _gelu(x):
    return jax.nn.gelu(x, approximate=True)

def _silu(x):
    return jax.nn.silu(x)

def _sigmoid(x):
    return jax.nn.sigmoid(x)

def _layernorm(x, axis=-1, eps=1e-05):
    m = jnp.mean(x, axis=axis, keepdims=True)
    v = jnp.var(x, axis=axis, keepdims=True)
    return (x - m) / jnp.sqrt(v + eps)

def _scatter_add(tgt, idx, src, axis=0):
    return tgt.at[idx].add(src)

def _segment_sum(src, seg, n):
    return jax.ops.segment_sum(src, seg, n)
kernel_name = 'mk_gnn_resnorm_d4_gnn_r32_1d32cd'

def setup_inputs(seed: int=0):
    np.random.seed(seed)
    _w = jnp.asarray

    def _rec_inputs():
        import jax
        import jax.numpy as jnp
        _gk = jax.random.key(seed)
        x = -0.0003713 + 1 * jax.random.normal(jax.random.fold_in(_gk, 1), (3125, 128), jnp.float32)
        src = jax.random.randint(jax.random.fold_in(_gk, 2), (50000,), 0, 3125, jnp.int32)
        dst = jax.random.randint(jax.random.fold_in(_gk, 3), (50000,), 0, 3125, jnp.int32)
        _o = jnp.argsort(dst, stable=True)
        src = src[_o]
        dst = dst[_o]
        edge_attr_64 = 0.000102155 + 1.00015 * jax.random.normal(jax.random.fold_in(_gk, 12), (50000, 64), jnp.float32)
        edge_type_32 = jax.random.randint(jax.random.fold_in(_gk, 14), (50000,), 0, 32, jnp.int32)
        edge_type_8 = jax.random.randint(jax.random.fold_in(_gk, 15), (50000,), 0, 8, jnp.int32)
        edge_weight = jax.random.uniform(jax.random.fold_in(_gk, 16), (50000,), jnp.float32, 0.0, 0.999999)
        node_type_16 = jax.random.randint(jax.random.fold_in(_gk, 17), (3125,), 0, 16, jnp.int32)
        return (x, src, dst, edge_attr_64, edge_type_32, edge_type_8, edge_weight, node_type_16)
    x, src, dst, edge_attr_64, edge_type_32, edge_type_8, edge_weight, node_type_16 = _rec_inputs()

    def _L0_gnn_setup():
        import jax, jax.numpy as jnp
        import numpy as np
        N = 3125
        E = 50000
        H = 128
        L = 3
        EPS = 1e-05

        def _layer(h, src, dst, e_w, w_neigh, w_root, b_root, g, b):
            msg = e_w[:, None] * h[src]
            agg = jax.ops.segment_sum(msg, dst, num_segments=N)
            sum_w = jnp.clip(jax.ops.segment_sum(e_w, dst, num_segments=N), 1.0, None)
            out = agg / sum_w[:, None]
            out = out @ w_neigh.T + h @ w_root.T + b_root
            out = jax.nn.relu(out)
            mu = jnp.mean(out, axis=-1, keepdims=True)
            var = jnp.var(out, axis=-1, keepdims=True)
            out = (out - mu) * jax.lax.rsqrt(var + EPS) * g + b
            return out
        key = jax.random.key(seed)
        ks = jax.random.split(key, 8)
        x = jax.random.normal(ks[0], (N, H), dtype=jnp.float32)
        edge_index = jax.random.randint(ks[1], (2, E), 0, N, dtype=jnp.int64)
        edge_weight = jax.random.uniform(ks[2], (E,), dtype=jnp.float32)
        s = 1.0 / np.sqrt(H)
        lin_neigh_w = jax.random.uniform(ks[3], (L, H, H), minval=-s, maxval=s, dtype=jnp.float32)
        lin_root_w = jax.random.uniform(ks[4], (L, H, H), minval=-s, maxval=s, dtype=jnp.float32)
        lin_root_b = jax.random.uniform(ks[5], (L, H), minval=-s, maxval=s, dtype=jnp.float32)
        ln_w = jnp.ones((L, H), dtype=jnp.float32)
        ln_b = jnp.zeros((L, H), dtype=jnp.float32)
        return {'x': x, 'edge_index': edge_index, 'edge_weight': edge_weight, 'lin_neigh_w': lin_neigh_w, 'lin_root_w': lin_root_w, 'lin_root_b': lin_root_b, 'ln_w': ln_w, 'ln_b': ln_b}
    _L0_gnn_all = _L0_gnn_setup()
    _L0_gnn_in = {k: v for k, v in _L0_gnn_all.items() if k in ('lin_neigh_w', 'lin_root_w', 'lin_root_b', 'ln_w', 'ln_b')}
    del _L0_gnn_all

    def _L1_gnn_setup():
        import jax, jax.numpy as jnp
        import numpy as np
        N_NODES = 3125
        N_EDGES = 15625
        IN_CH = 128
        EDGE_CH = 64

        def _glorot(key, shape):
            fan_in, fan_out = (shape[0], shape[1])
            lim = (6.0 / (fan_in + fan_out)) ** 0.5
            return jax.random.uniform(key, shape, jnp.float32, -lim, lim)
        key = jax.random.key(seed)
        ks = jax.random.split(key, 14)
        x = jax.random.normal(ks[0], (N_NODES, IN_CH), jnp.float32)
        edge_index = jax.random.randint(ks[1], (2, N_EDGES), 0, N_NODES, jnp.int64)
        edge_attr = jax.random.normal(ks[2], (N_EDGES, EDGE_CH), jnp.float32)
        timestamps = jax.random.uniform(ks[3], (N_EDGES,), jnp.float32)
        We1 = _glorot(ks[4], (EDGE_CH, 2 * EDGE_CH))
        be1 = jnp.zeros((2 * EDGE_CH,), jnp.float32)
        We2 = _glorot(ks[5], (2 * EDGE_CH, IN_CH))
        be2 = jnp.zeros((IN_CH,), jnp.float32)
        Wt = _glorot(ks[6], (1, IN_CH))
        bt = jnp.zeros((IN_CH,), jnp.float32)
        Wn1 = _glorot(ks[7], (2 * IN_CH, IN_CH))
        bn1 = jnp.zeros((IN_CH,), jnp.float32)
        Wn2 = _glorot(ks[8], (IN_CH, IN_CH))
        bn2 = jnp.zeros((IN_CH,), jnp.float32)
        return {'x': x, 'edge_index': edge_index, 'edge_attr': edge_attr, 'timestamps': timestamps, 'We1': We1, 'be1': be1, 'We2': We2, 'be2': be2, 'Wt': Wt, 'bt': bt, 'Wn1': Wn1, 'bn1': bn1, 'Wn2': Wn2, 'bn2': bn2}
    _L1_gnn_all = _L1_gnn_setup()
    _L1_gnn_in = {k: v for k, v in _L1_gnn_all.items() if k in ('We1', 'be1', 'We2', 'be2', 'Wt', 'bt', 'Wn1', 'bn1', 'Wn2', 'bn2')}
    del _L1_gnn_all

    def _L2_gnn_setup():
        import jax, jax.numpy as jnp
        import numpy as np
        N = 50000
        E = 31250
        R = 8
        IN = 128
        H = 128
        OUT = 128

        def rel_graph_conv(x, W, Wl, b, src, dst, etypes):
            xt = jnp.einsum('ni,rio->nro', x, W)
            msg = xt[src, etypes]
            agg = jax.ops.segment_sum(msg, dst, num_segments=x.shape[0])
            return agg + x @ Wl + b
        key = jax.random.key(seed)
        ks = jax.random.split(key, 12)
        feats = jax.random.normal(ks[0], (N, IN), dtype=jnp.float32)
        src = jax.random.randint(ks[1], (E,), 0, N, dtype=jnp.int32)
        dst = jax.random.randint(ks[2], (E,), 0, N, dtype=jnp.int32)
        etypes = jax.random.randint(ks[3], (E,), 0, R, dtype=jnp.int32)
        s_in = 1.0 / np.sqrt(IN)
        s_h = 1.0 / np.sqrt(H)
        W1 = jax.random.normal(ks[4], (R, IN, H), dtype=jnp.float32) * s_in
        Wl1 = jax.random.normal(ks[5], (IN, H), dtype=jnp.float32) * s_in
        b1 = jnp.zeros((H,), dtype=jnp.float32)
        W2 = jax.random.normal(ks[6], (R, H, OUT), dtype=jnp.float32) * s_h
        Wl2 = jax.random.normal(ks[7], (H, OUT), dtype=jnp.float32) * s_h
        b2 = jnp.zeros((OUT,), dtype=jnp.float32)
        return dict(feats=feats, W1=W1, Wl1=Wl1, b1=b1, W2=W2, Wl2=Wl2, b2=b2, src=src, dst=dst, etypes=etypes)
    _L2_gnn_all = _L2_gnn_setup()
    _L2_gnn_in = {k: v for k, v in _L2_gnn_all.items() if k in ('W1', 'Wl1', 'b1', 'W2', 'Wl2', 'b2')}
    del _L2_gnn_all

    def _L3_gnn_setup():
        import jax, jax.numpy as jnp
        import numpy as np
        N = 625
        E = 10000
        DIN = 128
        HID = 128
        H = 8
        HS = HID // H
        NT = 16
        RT = 32
        L = 2
        OUT = 128
        SQRT_D = float(np.sqrt(HS))

        def typed_linear(x, t, W):
            y_all = jnp.einsum('nd,tdo->nto', x, W)
            return jnp.take_along_axis(y_all, t[:, None, None], axis=1)[:, 0]

        def edge_softmax(a, dst, n):
            amax = jax.ops.segment_max(a, dst, num_segments=n)
            ex = jnp.exp(a - amax[dst])
            s = jax.ops.segment_sum(ex, dst, num_segments=n)
            return ex / s[dst]

        def gt_layer(x, ntype, etype, src, dst, Wk, Wq, Wv, Wa, Watt, Wmsg, pri, skip, g, b):
            n = x.shape[0]
            k = typed_linear(x, ntype, Wk).reshape(n, H, HS)
            q = typed_linear(x, ntype, Wq).reshape(n, H, HS)
            v = typed_linear(x, ntype, Wv).reshape(n, H, HS)
            kT = jnp.einsum('nhd,htdo->nhto', k, Watt)
            vT = jnp.einsum('nhd,htdo->nhto', v, Wmsg)
            kw = kT[src, :, etype]
            m = vT[src, :, etype]
            a = jnp.einsum('ehd,ehd->eh', kw, q[dst]) * pri[:, etype].T / SQRT_D
            att = edge_softmax(a, dst, n)
            msg = (m * att[:, :, None]).reshape(-1, H * HS)
            hag = jax.ops.segment_sum(msg, dst, num_segments=n)
            h = jax.nn.silu(typed_linear(hag, ntype, Wa))
            alpha = jax.nn.sigmoid(skip[ntype])[:, None]
            h = h * alpha + x * (1.0 - alpha)
            mu = jnp.mean(h, axis=-1, keepdims=True)
            var = jnp.mean((h - mu) ** 2, axis=-1, keepdims=True)
            return (h - mu) * jax.lax.rsqrt(var + 1e-05) * g + b
        key = jax.random.key(seed)
        ks = jax.random.split(key, 16)
        f32 = jnp.float32
        return {'x': jax.random.normal(ks[0], (N, DIN), f32), 'ntype': jax.random.randint(ks[1], (N,), 0, NT), 'etype': jax.random.randint(ks[2], (E,), 0, RT), 'src': jax.random.randint(ks[3], (E,), 0, N), 'dst': jax.random.randint(ks[4], (E,), 0, N), 'Wk': jax.random.normal(ks[5], (L, NT, DIN, HID), f32) / np.sqrt(DIN), 'Wq': jax.random.normal(ks[6], (L, NT, DIN, HID), f32) / np.sqrt(DIN), 'Wv': jax.random.normal(ks[7], (L, NT, DIN, HID), f32) / np.sqrt(DIN), 'Wa': jax.random.normal(ks[8], (L, NT, HID, HID), f32) / np.sqrt(HID), 'Watt': jax.random.normal(ks[9], (L, H, RT, HS, HS), f32) / np.sqrt(HS), 'Wmsg': jax.random.normal(ks[10], (L, H, RT, HS, HS), f32) / np.sqrt(HS), 'pri': jnp.ones((L, H, RT), f32), 'skip': jnp.ones((L, NT), f32), 'ln_g': jnp.ones((L, HID), f32), 'ln_b': jnp.zeros((L, HID), f32), 'ff_w': jax.random.normal(ks[11], (HID, OUT), f32) / np.sqrt(HID), 'ff_b': jnp.zeros((OUT,), f32)}
    _L3_gnn_all = _L3_gnn_setup()
    _L3_gnn_in = {k: v for k, v in _L3_gnn_all.items() if k in ('Wk', 'Wq', 'Wv', 'Wa', 'Watt', 'Wmsg', 'pri', 'skip', 'ln_g', 'ln_b', 'ff_w', 'ff_b')}
    del _L3_gnn_all
    return {'x': x, 'src': src, 'dst': dst, 'edge_attr_64': edge_attr_64, 'edge_type_32': edge_type_32, 'edge_type_8': edge_type_8, 'edge_weight': edge_weight, 'node_type_16': node_type_16, 'L0_gnn_lin_neigh_w': _L0_gnn_in['lin_neigh_w'], 'L0_gnn_lin_root_w': _L0_gnn_in['lin_root_w'], 'L0_gnn_lin_root_b': _L0_gnn_in['lin_root_b'], 'L0_gnn_ln_w': _L0_gnn_in['ln_w'], 'L0_gnn_ln_b': _L0_gnn_in['ln_b'], 'L1_gnn_We1': _L1_gnn_in['We1'], 'L1_gnn_be1': _L1_gnn_in['be1'], 'L1_gnn_We2': _L1_gnn_in['We2'], 'L1_gnn_be2': _L1_gnn_in['be2'], 'L1_gnn_Wt': _L1_gnn_in['Wt'], 'L1_gnn_bt': _L1_gnn_in['bt'], 'L1_gnn_Wn1': _L1_gnn_in['Wn1'], 'L1_gnn_bn1': _L1_gnn_in['bn1'], 'L1_gnn_Wn2': _L1_gnn_in['Wn2'], 'L1_gnn_bn2': _L1_gnn_in['bn2'], 'L2_gnn_W1': _L2_gnn_in['W1'], 'L2_gnn_Wl1': _L2_gnn_in['Wl1'], 'L2_gnn_b1': _L2_gnn_in['b1'], 'L2_gnn_W2': _L2_gnn_in['W2'], 'L2_gnn_Wl2': _L2_gnn_in['Wl2'], 'L2_gnn_b2': _L2_gnn_in['b2'], 'L3_gnn_Wk': _L3_gnn_in['Wk'], 'L3_gnn_Wq': _L3_gnn_in['Wq'], 'L3_gnn_Wv': _L3_gnn_in['Wv'], 'L3_gnn_Wa': _L3_gnn_in['Wa'], 'L3_gnn_Watt': _L3_gnn_in['Watt'], 'L3_gnn_Wmsg': _L3_gnn_in['Wmsg'], 'L3_gnn_pri': _L3_gnn_in['pri'], 'L3_gnn_skip': _L3_gnn_in['skip'], 'L3_gnn_ln_g': _L3_gnn_in['ln_g'], 'L3_gnn_ln_b': _L3_gnn_in['ln_b'], 'L3_gnn_ff_w': _L3_gnn_in['ff_w'], 'L3_gnn_ff_b': _L3_gnn_in['ff_b']}

def reference(x, src, dst, edge_attr_64, edge_type_32, edge_type_8, edge_weight, node_type_16, L0_gnn_lin_neigh_w, L0_gnn_lin_root_w, L0_gnn_lin_root_b, L0_gnn_ln_w, L0_gnn_ln_b, L1_gnn_We1, L1_gnn_be1, L1_gnn_We2, L1_gnn_be2, L1_gnn_Wt, L1_gnn_bt, L1_gnn_Wn1, L1_gnn_bn1, L1_gnn_Wn2, L1_gnn_bn2, L2_gnn_W1, L2_gnn_Wl1, L2_gnn_b1, L2_gnn_W2, L2_gnn_Wl2, L2_gnn_b2, L3_gnn_Wk, L3_gnn_Wq, L3_gnn_Wv, L3_gnn_Wa, L3_gnn_Watt, L3_gnn_Wmsg, L3_gnn_pri, L3_gnn_skip, L3_gnn_ln_g, L3_gnn_ln_b, L3_gnn_ff_w, L3_gnn_ff_b):
    import jax
    import jax.numpy as jnp

    def _L0_gnn_ref(x, edge_index, edge_weight, lin_neigh_w, lin_root_w, lin_root_b, ln_w, ln_b):
        import jax, jax.numpy as jnp
        import numpy as np
        N = 3125
        E = 50000
        H = 128
        L = 3
        EPS = 1e-05

        def _layer(h, src, dst, e_w, w_neigh, w_root, b_root, g, b):
            msg = e_w[:, None] * h[src]
            agg = jax.ops.segment_sum(msg, dst, num_segments=N)
            sum_w = jnp.clip(jax.ops.segment_sum(e_w, dst, num_segments=N), 1.0, None)
            out = agg / sum_w[:, None]
            out = out @ w_neigh.T + h @ w_root.T + b_root
            out = jax.nn.relu(out)
            mu = jnp.mean(out, axis=-1, keepdims=True)
            var = jnp.var(out, axis=-1, keepdims=True)
            out = (out - mu) * jax.lax.rsqrt(var + EPS) * g + b
            return out
        src, dst = (edge_index[0], edge_index[1])
        h = x
        for l in range(L):
            h = _layer(h, src, dst, edge_weight, lin_neigh_w[l], lin_root_w[l], lin_root_b[l], ln_w[l], ln_b[l])
        return h

    def _L1_gnn_ref(x, edge_index, edge_attr, timestamps, We1, be1, We2, be2, Wt, bt, Wn1, bn1, Wn2, bn2):
        import jax, jax.numpy as jnp
        import numpy as np
        N_NODES = 3125
        N_EDGES = 15625
        IN_CH = 128
        EDGE_CH = 64

        def _glorot(key, shape):
            fan_in, fan_out = (shape[0], shape[1])
            lim = (6.0 / (fan_in + fan_out)) ** 0.5
            return jax.random.uniform(key, shape, jnp.float32, -lim, lim)
        ts = timestamps[:, None]
        ef = jax.nn.relu(edge_attr @ We1 + be1) @ We2 + be2
        tw = jax.nn.sigmoid(ts @ Wt + bt)
        ef = ef * tw
        row, col = (edge_index[0], edge_index[1])
        combined = jnp.concatenate([x[row], ef], axis=1)
        msg = jax.nn.relu(combined @ Wn1 + bn1) @ Wn2 + bn2
        out = jax.ops.segment_sum(msg, col, num_segments=x.shape[0])
        return out + x

    def _L2_gnn_ref(feats, W1, Wl1, b1, W2, Wl2, b2, src, dst, etypes):
        import jax, jax.numpy as jnp
        import numpy as np
        N = 50000
        E = 31250
        R = 8
        IN = 128
        H = 128
        OUT = 128

        def rel_graph_conv(x, W, Wl, b, src, dst, etypes):
            xt = jnp.einsum('ni,rio->nro', x, W)
            msg = xt[src, etypes]
            agg = jax.ops.segment_sum(msg, dst, num_segments=x.shape[0])
            return agg + x @ Wl + b
        x = jax.nn.relu(rel_graph_conv(feats, W1, Wl1, b1, src, dst, etypes))
        return rel_graph_conv(x, W2, Wl2, b2, src, dst, etypes)

    def _L3_gnn_ref(x, ntype, etype, src, dst, Wk, Wq, Wv, Wa, Watt, Wmsg, pri, skip, ln_g, ln_b, ff_w, ff_b):
        import jax, jax.numpy as jnp
        import numpy as np
        N = 625
        E = 10000
        DIN = 128
        HID = 128
        H = 8
        HS = HID // H
        NT = 16
        RT = 32
        L = 2
        OUT = 128
        SQRT_D = float(np.sqrt(HS))

        def typed_linear(x, t, W):
            y_all = jnp.einsum('nd,tdo->nto', x, W)
            return jnp.take_along_axis(y_all, t[:, None, None], axis=1)[:, 0]

        def edge_softmax(a, dst, n):
            amax = jax.ops.segment_max(a, dst, num_segments=n)
            ex = jnp.exp(a - amax[dst])
            s = jax.ops.segment_sum(ex, dst, num_segments=n)
            return ex / s[dst]

        def gt_layer(x, ntype, etype, src, dst, Wk, Wq, Wv, Wa, Watt, Wmsg, pri, skip, g, b):
            n = x.shape[0]
            k = typed_linear(x, ntype, Wk).reshape(n, H, HS)
            q = typed_linear(x, ntype, Wq).reshape(n, H, HS)
            v = typed_linear(x, ntype, Wv).reshape(n, H, HS)
            kT = jnp.einsum('nhd,htdo->nhto', k, Watt)
            vT = jnp.einsum('nhd,htdo->nhto', v, Wmsg)
            kw = kT[src, :, etype]
            m = vT[src, :, etype]
            a = jnp.einsum('ehd,ehd->eh', kw, q[dst]) * pri[:, etype].T / SQRT_D
            att = edge_softmax(a, dst, n)
            msg = (m * att[:, :, None]).reshape(-1, H * HS)
            hag = jax.ops.segment_sum(msg, dst, num_segments=n)
            h = jax.nn.silu(typed_linear(hag, ntype, Wa))
            alpha = jax.nn.sigmoid(skip[ntype])[:, None]
            h = h * alpha + x * (1.0 - alpha)
            mu = jnp.mean(h, axis=-1, keepdims=True)
            var = jnp.mean((h - mu) ** 2, axis=-1, keepdims=True)
            return (h - mu) * jax.lax.rsqrt(var + 1e-05) * g + b
        h = x
        for l in range(L):
            h = gt_layer(h, ntype, etype, src, dst, Wk[l], Wq[l], Wv[l], Wa[l], Watt[l], Wmsg[l], pri[l], skip[l], ln_g[l], ln_b[l])
        return h @ ff_w + ff_b
    edge_index = jnp.stack([src, dst])
    x = _layernorm(x + _L0_gnn_ref(x, edge_index, edge_weight, L0_gnn_lin_neigh_w, L0_gnn_lin_root_w, L0_gnn_lin_root_b, L0_gnn_ln_w, L0_gnn_ln_b), axis=-1)
    x = _layernorm(x + _L1_gnn_ref(x, edge_index, edge_attr_64, edge_weight, L1_gnn_We1, L1_gnn_be1, L1_gnn_We2, L1_gnn_be2, L1_gnn_Wt, L1_gnn_bt, L1_gnn_Wn1, L1_gnn_bn1, L1_gnn_Wn2, L1_gnn_bn2), axis=-1)
    x = _layernorm(x + _L2_gnn_ref(x, L2_gnn_W1, L2_gnn_Wl1, L2_gnn_b1, L2_gnn_W2, L2_gnn_Wl2, L2_gnn_b2, src, dst, edge_type_8), axis=-1)
    x = _layernorm(x + _L3_gnn_ref(x, node_type_16, edge_type_32, src, dst, L3_gnn_Wk, L3_gnn_Wq, L3_gnn_Wv, L3_gnn_Wa, L3_gnn_Watt, L3_gnn_Wmsg, L3_gnn_pri, L3_gnn_skip, L3_gnn_ln_g, L3_gnn_ln_b, L3_gnn_ff_w, L3_gnn_ff_b), axis=-1)
    return x

_drawn_inputs = setup_inputs


def setup_inputs(seed=0):
    import zlib

    import numpy as np

    out = dict(_drawn_inputs(seed))
    spreads = {'L0_gnn_ln_w': (1.0, 0.2),
     'L0_gnn_ln_b': (0.0, 0.1),
     'L1_gnn_be1': (0.0, 0.323),
     'L1_gnn_be2': (0.0, 0.1),
     'L1_gnn_bt': (0.0, 0.628),
     'L1_gnn_bn1': (0.0, 0.1),
     'L1_gnn_bn2': (0.0, 0.1),
     'L2_gnn_b1': (0.0, 0.41),
     'L2_gnn_b2': (0.0, 0.8),
     'L3_gnn_pri': (1.0, 0.2),
     'L3_gnn_skip': (1.0, 0.2),
     'L3_gnn_ln_g': (1.0, 0.2),
     'L3_gnn_ln_b': (0.0, 0.1),
     'L3_gnn_ff_b': (0.0, 0.1)}
    factors = {'L1_gnn_Wt': 6.708}
    for name, (base, spread) in spreads.items():
        noise = np.random.default_rng([zlib.crc32(name.encode()), seed]).standard_normal(out[name].shape)
        drawn = base * np.exp(spread * noise) if base else spread * noise
        out[name] = jnp.asarray(drawn.astype(out[name].dtype))
    for name, factor in factors.items():
        out[name] = (out[name] * factor).astype(out[name].dtype)
    return out
```

```python
from contextlib import ExitStack

import concourse.bass as bass
from concourse import mybir

ALU = mybir.AluOpType
ACT = mybir.ActivationFunctionType
AX = mybir.AxisListType
F32 = mybir.dt.float32
I32 = mybir.dt.int32
ds = bass.ds

P = 128
N = 3125
E = 50000
H = 128
NB = -(-N // P)
NP = NB * P
LAST = N - (NB - 1) * P
BANKS = -(-NB // 4)
U = 16
HALF = U // 2
TILES = 4 * -(-E // (4 * P))
STEPS = -(-(-(-E // P) + NB - 1) // U) * U
TRIPS = STEPS // U
EP = TILES * P
TCH = 4
TROWS = TILES // TCH
CROWS = 125
CCOLS = E // CROWS
L0 = 3
R8 = 8
T32 = 32
NT = 16
HEADS = 8
HS = H // HEADS
EDIM = 64
CHUNKS = P // HEADS
GSTEPS = STEPS // CHUNKS
BIG = 1e30
EPS = 1e-5
STAGE = 4


class Signal:

    def __init__(self, sem):
        self.sem, self.base = sem, 0

    def at(self, count):
        return count + self.base


class Chain:

    def __init__(self, eng, mark):
        self.eng, self.mark, self.n = eng, mark, 0

    def __call__(self, inst):
        self.n += 1
        inst.then_inc(self.mark.sem, 1)
        self.eng.wait_ge(self.mark.sem, self.mark.at(self.n))

    def close(self):
        self.mark.base += self.n


def trips(eng, body, n=TRIPS):
    body(0, True)
    with eng.Fori(1, n) as i:
        body(i, False)


def span(k):
    return 512 * k, min(NP, 512 * k + 512), range(4 * k, min(NB, 4 * k + 4))


def build(nc, A, out):
    ctx = ExitStack()
    with ctx:
        def sb(name, shape, dt=F32):
            return ctx.enter_context(nc.sbuf_tensor(name, shape, dt))

        def signal(name):
            return Signal(ctx.enter_context(nc.semaphore(name)))

        def dram(name, shape, dt=F32):
            return nc.dram_tensor(name, shape, dt, kind="Internal").ap()

        table = dram("table", [NP, H])
        table8 = dram("table8", [NP * R8, H])
        table32 = dram("table32", [NP * T32, 2 * H])
        edge_part = dram("edge_part", [TILES, P, H])
        values = dram("values", [STEPS, P, H])

        ident = sb("ident", [P, P])
        iota_row = sb("iota_row", [P, P])
        zeros = sb("zeros", [P, 512])
        ones = sb("ones", [P, P])
        shift = sb("shift", [P, 2, P])
        head_mask = sb("head_mask", [P, HEADS])
        blk_i = sb("blk_i", [P, STEPS], I32)
        tile_i = sb("tile_i", [P, STEPS], I32)
        src_s = sb("src_s", [P, STEPS])
        dl_s = sb("dl_s", [P, STEPS])
        t32_s = sb("t32_s", [P, STEPS])
        t8_s = sb("t8_s", [P, STEPS])
        w_s = sb("w_s", [P, STEPS])
        dv_s = sb("dv_s", [P, STEPS])
        idx_s = sb("idx_s", [P, STEPS], I32)
        rsum = sb("rsum", [P, NB])
        deg = sb("deg", [P, NB])
        Xn = sb("Xn", [P, NB, H])
        Lx = sb("Lx", [P, NB, H])
        XT = sb("XT", [P, NP])
        Hn = sb("Hn", [P, NB, H])
        HF = sb("HF", [P, NP])
        G = sb("G", [P, U, 2 * H])
        gidx = sb("gidx", [P, U], I32)
        onehot = sb("onehot", [P, HALF, P])
        red = sb("red", [P, 4, NB])
        wts = sb("wts", [P, 6, H])
        vecs = sb("vecs", [P, 16])
        bc = sb("bc", [P, 2, H])
        brow = sb("brow", [1, H])
        arena = sb("arena", [P, 24500])

        ps = ctx.enter_context(nc.psum_tensor("ps", [P, 8, 512], F32))
        acc, misc = ps[:, 0:7, :], ps[:, 7, :]
        accf = acc.rearrange("p a b -> p (a b)")
        acc_nodes = accf[:, 0:NP].rearrange("p (b f) -> p b f", f=H)

        loaded = signal("loaded")
        stored = signal("stored")
        consts = signal("consts")
        vdone = signal("vdone")
        adone = signal("adone")
        pdone = signal("pdone")
        idx_ready = signal("idx_ready")
        go = signal("go")
        gathered = [signal(f"gathered{u}") for u in range(U)]
        onehot_ready = signal("onehot_ready")
        step_done = signal("step_done")
        turned = signal("turned")
        evac = signal("evac")
        made = signal("made")
        copied = signal("copied")
        mixed = signal("mixed")
        centred = signal("centred")
        squared = signal("squared")
        varied = signal("varied")
        rooted = signal("rooted")
        ring_in = [signal(f"ring_in{u}") for u in range(HALF)]
        ring_out = [signal(f"ring_out{u}") for u in range(U)]

        edge_out = [signal(f"edge_out{u}") for u in range(2)]

        cube = arena[:, 0:STEPS * NB]
        dst_i = Hn[0:CROWS, 0:4, :].rearrange("p a b -> p (a b)").bitcast(I32)[:, 0:CCOLS]
        dst_f = Hn[0:CROWS, 4:8, :].rearrange("p a b -> p (a b)")[:, 0:CCOLS]
        cnt = red[:, 0, :]
        jrow_i = XT[:, 0:STEPS].bitcast(I32)
        jrow = XT[:, 512:512 + STEPS]
        blk_f = XT[:, 1024:1024 + STEPS]
        tile_f = XT[:, 1536:1536 + STEPS]
        blk128 = XT[:, 2048:2048 + STEPS]
        valid = XT[:, 2560:2560 + STEPS]
        sm = HF[:, 0:12 * 32].rearrange("p (a b) -> p a b", b=32)
        smi = HF[:, 512:512 + 64].bitcast(I32)
        chunk_i = HF[:, 600:604].bitcast(I32)
        chunk_f = HF[:, 604:608]
        start_f, n_f, first_f, last_f, tiles_f, base_f, delta_f, dd_f, thr = (sm[:, r, 0:NB + 1] for r in range(9))
        fields_i = Hn[:, 8:24, :].rearrange("p a b -> p (a b)")[0:TROWS, :].bitcast(I32).rearrange("p (c e k) -> p c e k", c=TCH, k=4)
        fields_f = Lx[:, 0:16, :].rearrange("p a b -> p (a b)")[0:TROWS, :].rearrange("p (c e k) -> p c e k", c=TCH, k=4)
        fields_w = Lx[:, 16:20, :].rearrange("p a b -> p (a b)")[0:TROWS, :].rearrange("p (c e) -> p c e", c=TCH)
        select = arena[0:TROWS, 12000:12000 + TCH * STEPS].rearrange("p (c s) -> p c s", c=TCH)
        dests = [src_s, dl_s, t32_s, t8_s, w_s]

        with nc.Block() as block:
            @block.gpsimd
            def _(pool):
                ch = Chain(pool, pdone)
                pool.memset(zeros[:, :], 0.0).then_inc(consts.sem, 1)
                pool.memset(ones[:, :], 1.0).then_inc(consts.sem, 1)
                pool.memset(red[:, :, :], 0.0).then_inc(consts.sem, 1)
                ch(pool.memset(ident[:, :], 0.0))
                pool.affine_select(out=ident[:, :], in_=ident[:, :], compare_op=ALU.not_equal, fill=1.0,
                                   base=0, pattern=[[-1, P]], channel_multiplier=1).then_inc(consts.sem, 1)
                pool.iota(jrow_i, pattern=[[1, STEPS]], base=0, channel_multiplier=0).then_inc(consts.sem, 1)
                pool.iota(chunk_i, pattern=[[TROWS, TCH]], base=0, channel_multiplier=1).then_inc(consts.sem, 1)
                ch(pool.memset(shift[:, :, :], 0.0))
                pool.affine_select(out=shift[:, 0, :], in_=shift[:, 0, :], compare_op=ALU.not_equal, fill=1.0,
                                   base=HEADS, pattern=[[-1, P]], channel_multiplier=1).then_inc(consts.sem, 1)
                pool.affine_select(out=shift[:, 1, :], in_=shift[:, 1, :], compare_op=ALU.not_equal, fill=1.0,
                                   base=-HEADS, pattern=[[-1, P]], channel_multiplier=1).then_inc(consts.sem, 1)
                ch(pool.memset(head_mask[:, :], 1.0))
                ch(pool.affine_select(out=head_mask[:, :], in_=head_mask[:, :], compare_op=ALU.is_ge, fill=0.0,
                                      base=0, pattern=[[-HS, HEADS]], channel_multiplier=1))
                pool.affine_select(out=head_mask[:, :], in_=head_mask[:, :], compare_op=ALU.is_ge, fill=0.0,
                                   base=HS - 1, pattern=[[HS, HEADS]], channel_multiplier=-1).then_inc(consts.sem, 1)
                ch.close()

            @block.sync
            def _(sp):
                sp.dma_start(dst_i, A["dst"].rearrange("(p c) -> p c", p=CROWS)).then_inc(loaded.sem, 16)
                sp.dma_start(fields_i.rearrange("p c e k -> p c (e k)"),
                             A["edge_ints"].rearrange("(c p) k -> p c k", c=TCH)).then_inc(stored.sem, 16)
                sp.dma_start(fields_w, A["edge_w"].rearrange("(c p) k -> p c k", c=TCH)).then_inc(stored.sem, 16)
                sp.dma_start(Xn[:, 0:NB - 1, :], A["x"][0:(NB - 1) * P, :].rearrange("(b p) f -> p b f", p=P)).then_inc(stored.sem, 16)
                sp.wait_ge(copied.sem, 1)
                sp.dma_start(Xn[0:LAST, NB - 1, :], A["x"][(NB - 1) * P:N, :]).then_inc(stored.sem, 16)
                sp.wait_ge(stored.sem, 64)

            @block.tensor
            def _(pe):
                pe.wait_ge(consts.sem, 9)
                pe.wait_ge(made.sem, 1)
                pe.matmul(misc[:, 0:NB], ones[0:CROWS, :], cnt[0:CROWS, :], start=True, stop=True).then_inc(turned.sem, 1)
                pe.wait_ge(mixed.sem, 1)
                for f in range(5):
                    for c in range(TCH):
                        rows = fields_f[:, c, :, f] if f < 4 else fields_w[:, c, :]
                        mm = pe.matmul(acc[:, f, 0:STEPS], rows, select[:, c, :], start=(c == 0), stop=(c == TCH - 1))
                    mm.then_inc(turned.sem, 1)

            @block.vector
            def _(dve):
                ch = Chain(dve, vdone)
                dve.memset(Xn[:, NB - 1, :], 0.0).then_inc(copied.sem, 1)
                dve.wait_ge(consts.sem, 9)
                ch(dve.tensor_copy(jrow, jrow_i))
                ch(dve.tensor_copy(chunk_f, chunk_i))
                ch(dve.tensor_copy(iota_row[:, :], jrow[:, 0:P]))
                ch(dve.tensor_scalar(thr, jrow[:, 0:NB + 1], float(P), None, ALU.mult))
                dve.wait_ge(loaded.sem, 16)
                ch(dve.tensor_copy(dst_f, dst_i))
                below = cube[0:CROWS, 0:NB * CCOLS].rearrange("p (b c) -> p b c", b=NB)
                ch(dve.tensor_tensor(below, dst_f.unsqueeze(1).to_broadcast([CROWS, NB, CCOLS]),
                                     thr[0:CROWS, 0:NB].unsqueeze(2).to_broadcast([CROWS, NB, CCOLS]), ALU.is_lt))
                dve.tensor_reduce(cnt[0:CROWS, :], below, AX.X, ALU.add).then_inc(made.sem, 1)
                dve.wait_ge(turned.sem, 1)
                ch(dve.tensor_copy(start_f[:, 0:NB], misc[:, 0:NB]))
                ch(dve.memset(start_f[:, NB:NB + 1], float(E)))
                ch(dve.tensor_tensor(n_f[:, 0:NB], start_f[:, 1:NB + 1], start_f[:, 0:NB], ALU.subtract))
                ch(dve.tensor_copy(smi[:, 0:NB], start_f[:, 0:NB]))
                ch(dve.tensor_scalar(n_f[:, 0:NB], n_f[:, 0:NB], 0.0, None, ALU.is_gt))
                ch(dve.tensor_scalar(last_f[:, 0:NB], start_f[:, 1:NB + 1], float(P - 1), None, ALU.add))
                ch(dve.tensor_copy(smi[:, 32:32 + NB], last_f[:, 0:NB]))
                ch(dve.tensor_scalar(smi[:, 0:NB], smi[:, 0:NB], 7, None, ALU.arith_shift_right))
                ch(dve.tensor_scalar(smi[:, 32:32 + NB], smi[:, 32:32 + NB], 7, None, ALU.arith_shift_right))
                ch(dve.tensor_copy(first_f[:, 0:NB], smi[:, 0:NB]))
                ch(dve.tensor_copy(last_f[:, 0:NB], smi[:, 32:32 + NB]))
                ch(dve.tensor_tensor(tiles_f[:, 0:NB], last_f[:, 0:NB], first_f[:, 0:NB], ALU.subtract))
                ch(dve.tensor_tensor(tiles_f[:, 0:NB], tiles_f[:, 0:NB], n_f[:, 0:NB], ALU.mult))
                ch(dve.tensor_tensor_scan(base_f[:, 0:NB], tiles_f[:, 0:NB], zeros[:, 0:NB], 0.0, ALU.add, ALU.add))
                ch(dve.tensor_tensor(base_f[:, 0:NB], base_f[:, 0:NB], tiles_f[:, 0:NB], ALU.subtract))
                ch(dve.tensor_tensor(delta_f[:, 0:NB], first_f[:, 0:NB], base_f[:, 0:NB], ALU.subtract))
                ch(dve.tensor_copy(dd_f[:, 0:1], delta_f[:, 0:1]))
                ch(dve.tensor_tensor(dd_f[:, 1:NB], delta_f[:, 1:NB], delta_f[:, 0:NB - 1], ALU.subtract))
                reached = cube.rearrange("p (j b) -> p j b", b=NB)
                ch(dve.tensor_tensor(reached, jrow.unsqueeze(2).to_broadcast([P, STEPS, NB]),
                                     base_f[:, 0:NB].unsqueeze(1).to_broadcast([P, STEPS, NB]), ALU.is_ge))
                ch(dve.tensor_reduce(blk_f, reached, AX.X, ALU.add))
                ch(dve.tensor_scalar(blk_f, blk_f, 1.0, None, ALU.subtract))
                ch(dve.tensor_tensor(reached, reached, dd_f[:, 0:NB].unsqueeze(1).to_broadcast([P, STEPS, NB]), ALU.mult))
                ch(dve.tensor_reduce(tile_f, reached, AX.X, ALU.add))
                ch(dve.tensor_tensor(tile_f, jrow, tile_f, ALU.add))
                ch(dve.tensor_scalar(valid, tile_f, float(TILES) - 0.5, None, ALU.is_lt))
                ch(dve.tensor_scalar(tile_f, tile_f, float(TILES - 1), None, ALU.min))
                ch(dve.tensor_copy(blk_i[:, :], blk_f))
                ch(dve.tensor_copy(tile_i[:, :], tile_f))
                ch(dve.tensor_scalar(blk128, blk_f, float(P), None, ALU.mult))
                for c in range(TCH):
                    ch(dve.tensor_scalar(select[:, c, :], tile_f[0:TROWS, :], chunk_f[0:TROWS, c:c + 1], None, ALU.is_equal))
                dve.wait_ge(stored.sem, 64)
                dve.tensor_copy(fields_f.rearrange("p c e k -> p (c e k)"), fields_i.rearrange("p c e k -> p (c e k)")).then_inc(mixed.sem, 1)
                for f in range(5):
                    dve.wait_ge(turned.sem, f + 2)
                    ch(dve.tensor_copy(dests[f][:, :], acc[:, f, 0:STEPS]))
                ch(dve.tensor_scalar(dv_s[:, :], dl_s[:, :], 1.0, None, ALU.add))
                ch(dve.tensor_tensor(dl_s[:, :], dl_s[:, :], blk128, ALU.subtract))
                ch(dve.scalar_tensor_tensor(valid, dl_s[:, :], 0.0, valid, ALU.is_ge, ALU.mult))
                ch(dve.scalar_tensor_tensor(valid, dl_s[:, :], float(P), valid, ALU.is_lt, ALU.mult))
                ch(dve.tensor_tensor(dv_s[:, :], dv_s[:, :], valid, ALU.mult))
                ch(dve.scalar_tensor_tensor(dl_s[:, :], dl_s[:, :], 1.0, valid, ALU.add, ALU.mult))
                ch(dve.tensor_scalar(dl_s[:, :], dl_s[:, :], 1.0, None, ALU.subtract))
                ch(dve.tensor_copy(idx_s[:, :], src_s[:, :]))
                ch.close()
        loaded.base, stored.base, consts.base, made.base, turned.base, mixed.base, copied.base = 16, 64, 9, 1, 6, 1, 1

        def onehots(dve, weight, after=None):
            def body(i, first):
                for u in range(U):
                    j = i * U + u
                    if not (first and u < HALF):
                        dve.wait_ge(step_done.sem, step_done.at(j - HALF + 1))
                    o = onehot[:, u % HALF, :]
                    if weight is None:
                        inst = dve.tensor_scalar(o, iota_row[:, :], dl_s[:, ds(j, 1)], None, ALU.is_equal)
                    else:
                        inst = dve.tensor_scalar(o, iota_row[:, :], dl_s[:, ds(j, 1)], weight[:, ds(j, 1)],
                                                 ALU.is_equal, ALU.mult)
                    inst.then_inc(onehot_ready.sem, 1)
                    if after is not None:
                        after(i, u, first)
            trips(dve, body)

        def gathers(pool, tab, width, free=None):
            def body(i, first):
                for h in range(2):
                    if not first:
                        if free is None:
                            pool.wait_ge(step_done.sem, step_done.at(i * U - U + (h + 1) * HALF))
                        else:
                            free(pool, i, h)
                    pool.tensor_copy(gidx[:, h * HALF:(h + 1) * HALF],
                                     idx_s[:, ds(i * U + h * HALF, HALF)]).then_inc(idx_ready.sem, 1)
                    pool.wait_ge(idx_ready.sem, idx_ready.at(2 * i + h + 1))
                    pool.sem_inc(go.sem, 1)
                    for u in range(h * HALF, (h + 1) * HALF):
                        pool.indirect_dma_start(G[:, u, 0:width], None, tab,
                                                bass.IndirectOffsetOnAxis(ap=gidx[:, u:u + 1], axis=0)).then_inc(gathered[u].sem, 16)
            trips(pool, body)

        def step_block(pe, j):
            return pe.value_load(blk_i[0:1, ds(j, 1)], min_val=0, max_val=NB - 1)

        def step_pass_over():
            onehot_ready.base += STEPS
            step_done.base += STEPS

        def gather_pass_over():
            step_pass_over()
            idx_ready.base += 2 * TRIPS
            go.base += 2 * TRIPS
            for s in gathered:
                s.base += 16 * TRIPS

        def fill_rows(pe, row):
            for k in range(BANKS):
                a, b, blocks = span(k)
                if row is None:
                    pe.matmul(accf[:, a:b], ident[:, :], zeros[:, 0:b - a], start=True, stop=False, skip_group_check=True)
                else:
                    pe.matmul(accf[:, a:b].rearrange("p (b f) -> p b f", f=H), ones[0:1, :],
                              row.unsqueeze(1).to_broadcast([1, len(blocks), H]), start=True, stop=False, skip_group_check=True)

        def turn_nodes(pe, source, need):
            for k in range(BANKS):
                need(k)
                for b in span(k)[2]:
                    mm = pe.transpose(accf[:, b * P:(b + 1) * P],
                                      source[:, b, :] if len(source.shape) == 3 else source[:, b * P:(b + 1) * P], ident[:, :])
                mm.then_inc(turned.sem, 1)

        def normalise(ch, dve, src, dst):
            mean, var = red[:, 0, :], red[:, 1, :]

            def over(v):
                return v.unsqueeze(2).to_broadcast([P, NB, H])
            ch(dve.tensor_reduce(mean, src, AX.X, ALU.add))
            ch(dve.tensor_scalar(mean, mean, 1.0 / H, None, ALU.mult))
            dve.tensor_tensor(dst, src, over(mean), ALU.subtract).then_inc(centred.sem, 1)
            dve.wait_ge(squared.sem, squared.at(1))
            ch(dve.tensor_reduce(var, arena[:, 0:NP].rearrange("p (b f) -> p b f", f=H), AX.X, ALU.add))
            dve.tensor_scalar(var, var, 1.0 / H, EPS, ALU.mult, ALU.add).then_inc(varied.sem, 1)
            dve.wait_ge(rooted.sem, rooted.at(1))
            ch(dve.reciprocal(var, var))
            return dve.tensor_tensor(dst, dst, over(var), ALU.mult)

        def normalise_act(act, dst):
            act.wait_ge(centred.sem, centred.at(1))
            act.activation(arena[:, 0:NP], dst.rearrange("p b f -> p (b f)"), ACT.Square).then_inc(squared.sem, 1)
            act.wait_ge(varied.sem, varied.at(1))
            act.activation(red[:, 1, :], red[:, 1, :], ACT.Sqrt).then_inc(rooted.sem, 1)

        def normalised():
            for s in (centred, squared, varied, rooted):
                s.base += 1

        def residual_norm_phase(prepare=None):
            with nc.Block() as block:
                @block.scalar
                def _(act):
                    normalise_act(act, Xn[:, :, :])

                @block.vector
                def _(dve):
                    ch = Chain(dve, vdone)
                    if prepare is not None:
                        prepare(ch, dve)
                    ch(normalise(ch, dve, Xn[:, :, :], Xn[:, :, :]))
                    ch.close()
            normalised()

        def load_phase_part(sp, loads):
            for dst_ap, src_ap in loads:
                sp.dma_start(dst_ap, src_ap).then_inc(loaded.sem, 16)

        def table_phase(src, scale=1.0, bias=0.0, loads=(), w=None, row=None, index=None):
            with nc.Block() as block:
                @block.sync
                def _(sp):
                    load_phase_part(sp, loads)
                    if w is not None:
                        sp.wait_ge(copied.sem, copied.at(BANKS))
                        sp.dma_start(table.rearrange("(b p) f -> p b f", p=P),
                                     HF[:, :].rearrange("p (b f) -> p b f", f=H)).then_inc(stored.sem, 16)
                        sp.wait_ge(stored.sem, stored.at(16))

                @block.tensor
                def _(pe):
                    turn_nodes(pe, src[:, :, :], lambda k: None)
                    if w is not None:
                        pe.wait_ge(loaded.sem, loaded.at(16 * len(loads)))
                        for k in range(BANKS):
                            a, b, blocks = span(k)
                            pe.wait_ge(evac.sem, evac.at(k + 1))
                            if row is not None:
                                pe.matmul(accf[:, a:b].rearrange("p (b f) -> p b f", f=H), ones[0:1, :],
                                          row.unsqueeze(1).to_broadcast([1, len(blocks), H]), start=True, stop=False, skip_group_check=True)
                            for b in blocks:
                                mm = pe.matmul(accf[:, b * P:(b + 1) * P], XT[:, b * P:(b + 1) * P], w,
                                               start=(row is None), stop=True, skip_group_check=True)
                            mm.then_inc(made.sem, 1)

                @block.scalar
                def _(act):
                    act.wait_ge(loaded.sem, loaded.at(16 * len(loads)))
                    for k in range(BANKS):
                        a, b, _ = span(k)
                        act.wait_ge(turned.sem, turned.at(k + 1))
                        act.activation(XT[:, a:b], accf[:, a:b], ACT.Identity, scale=scale, bias=bias).then_inc(evac.sem, 1)

                @block.vector
                def _(dve):
                    ch = Chain(dve, vdone)
                    if index is not None:
                        ch(dve.scalar_tensor_tensor(w1_f, src_s[:, :], float(index[1]), index[0][:, :], ALU.mult, ALU.add))
                        ch(dve.tensor_copy(idx_s[:, :], w1_f))
                    if w is not None:
                        for k in range(BANKS):
                            a, b, _ = span(k)
                            dve.wait_ge(made.sem, made.at(k + 1))
                            dve.tensor_copy(HF[:, a:b], accf[:, a:b]).then_inc(copied.sem, 1)
                    ch.close()
            loaded.base += 16 * len(loads)
            turned.base += BANKS
            evac.base += BANKS
            if w is not None:
                made.base += BANKS
                copied.base += BANKS
                stored.base += 16
        w1_f = arena[:, 24000:24000 + STEPS]

        def aggregate_phase(tab, weight, root=None, row=None, sums=None):
            with nc.Block() as block:
                @block.gpsimd
                def _(pool):
                    gathers(pool, tab, H)

                @block.vector
                def _(dve):
                    onehots(dve, weight)

                @block.tensor
                def _(pe):
                    fill_rows(pe, row)
                    if root is not None:
                        for b in range(NB):
                            pe.matmul(accf[:, b * P:(b + 1) * P], XT[:, b * P:(b + 1) * P], root, start=False, stop=False,
                                      skip_group_check=True)
                    if sums:
                        pe.matmul(misc[:, 0:NB], ident[:, :], zeros[:, 0:NB], start=True, stop=False, skip_group_check=True)

                    def body(i, first):
                        for u in range(U):
                            j = i * U + u
                            b = step_block(pe, j)
                            pe.wait_ge(onehot_ready.sem, onehot_ready.at(j + 1))
                            pe.wait_ge(gathered[u].sem, gathered[u].at(16 * (i + 1)))
                            o = onehot[:, u % HALF, :]
                            if sums:
                                pe.matmul(misc[:, ds(b, 1)], o, ones[:, 0:1], start=False, stop=False, skip_group_check=True)
                            pe.matmul(accf[:, ds(b * P, P)], o, G[:, u, 0:H],
                                      start=False, stop=False, skip_group_check=True).then_inc(step_done.sem, 1)
                    trips(pe, body)
            gather_pass_over()

        def col(ap):
            return ap.rearrange("(p a) -> p a", a=1)

        def one_row(ap):
            return ap.rearrange("(a f) -> a f", a=1)

        def over_nodes(ap):
            return ap.partition_broadcast(P)

        def full(v):
            return v.unsqueeze(2).to_broadcast([P, NB, H])

        loads = [(wts[:, 0:3, :], A["L0_neigh"].rearrange("l f o -> f l o")),
                 (wts[:, 3:6, :], A["L0_root"].rearrange("l f o -> f l o")),
                 (bc[:, 0, :], over_nodes(A["L0_gnn_ln_w"][L0 - 1])), (bc[:, 1, :], over_nodes(A["L0_gnn_ln_b"][L0 - 1]))]
        for l in range(L0):
            loads += [(vecs[:, l:l + 1], col(A["L0_gnn_ln_w"][l])), (vecs[:, 3 + l:4 + l], col(A["L0_gnn_ln_b"][l]))]

        for l in range(L0):
            if l == 0:
                table_phase(Xn, loads=loads, w=wts[:, 0, :])
            else:
                table_phase(Hn, scale=vecs[:, l - 1:l], bias=vecs[:, 2 + l:3 + l], w=wts[:, l, :])
            aggregate_phase(table, w_s, sums=(l == 0))
            with nc.Block() as block:
                @block.sync
                def _(sp):
                    sp.dma_start(brow[:, :], one_row(A["L0_gnn_lin_root_b"][l])).then_inc(loaded.sem, 16)

                @block.scalar
                def _(act):
                    act.wait_ge(mixed.sem, mixed.at(1))
                    act.activation(Hn[:, :, :].rearrange("p b f -> p (b f)"), HF[:, :], ACT.Relu).then_inc(evac.sem, 1)
                    normalise_act(act, Hn[:, :, :])

                @block.tensor
                def _(pe):
                    pe.wait_ge(loaded.sem, loaded.at(16))
                    pe.wait_ge(copied.sem, copied.at(1))
                    fill_rows(pe, brow[:, :])
                    for b in range(NB):
                        mm = pe.matmul(accf[:, b * P:(b + 1) * P], XT[:, b * P:(b + 1) * P], wts[:, 3 + l, :], start=False,
                                       stop=True, skip_group_check=True)
                    mm.then_inc(made.sem, 1)

                @block.vector
                def _(dve):
                    ch = Chain(dve, vdone)
                    if l == 0:
                        ch(dve.tensor_scalar(rsum[:, :], misc[:, 0:NB], 1.0, None, ALU.max))
                        ch(dve.reciprocal(rsum[:, :], rsum[:, :]))
                    hf = HF[:, :].rearrange("p (b f) -> p b f", f=H)
                    dve.tensor_tensor(hf, acc_nodes, full(rsum[:, :]), ALU.mult).then_inc(copied.sem, 1)
                    dve.wait_ge(copied.sem, copied.at(1))
                    dve.wait_ge(made.sem, made.at(1))
                    dve.tensor_tensor(hf, hf, acc_nodes, ALU.add).then_inc(mixed.sem, 1)
                    dve.wait_ge(evac.sem, evac.at(1))
                    ch(normalise(ch, dve, Hn[:, :, :], Hn[:, :, :]))
                    if l == L0 - 1:
                        ch(dve.tensor_tensor(Hn[:, :, :], Hn[:, :, :], bc[:, 0:1, :].to_broadcast([P, NB, H]), ALU.mult))
                        ch(dve.tensor_tensor(Hn[:, :, :], Hn[:, :, :], bc[:, 1:2, :].to_broadcast([P, NB, H]), ALU.add))
                        ch(dve.tensor_tensor(Xn[:, :, :], Xn[:, :, :], Hn[:, :, :], ALU.add))
                    ch.close()
            loaded.base += 16
            for s in (evac, made, mixed, copied):
                s.base += 1
            normalised()
        residual_norm_phase()

        if STAGE >= 2:
            GROUP = 4 * P
            GROUPS = TILES // 4
            attrT = arena[0:EDIM, 0:2 * GROUP].rearrange("p (r e) -> p r e", r=2)
            ts_bc = arena[:, 1024:1024 + 2 * GROUP].rearrange("p (r e) -> p r e", r=2)
            hid = arena[:, 2048:2048 + 2 * GROUP].rearrange("p (r e) -> p r e", r=2)
            tw = arena[:, 3072:3072 + 2 * GROUP].rearrange("p (r e) -> p r e", r=2)
            ef = arena[:, 4096:4096 + 2 * GROUP].rearrange("p (r e) -> p r e", r=2)
            zout = arena[:, 5120:5120 + 2 * GROUP].rearrange("p (r e) -> p r e", r=2)
            we1 = arena[0:EDIM, 6144:6144 + H]
            We2, Wn1a, Wn1b, Wn2 = (wts[:, r, :] for r in range(4))
            be1, be2, wt_c, bt_c = (vecs[:, r:r + 1] for r in range(4))
            loads = [(we1, A["L1_gnn_We1"]), (We2, A["L1_gnn_We2"]), (Wn1a, A["L1_gnn_Wn1"][0:H, :]),
                     (Wn1b, A["L1_gnn_Wn1"][H:2 * H, :]), (Wn2, A["L1_gnn_Wn2"]), (be1, col(A["L1_gnn_be1"])),
                     (be2, col(A["L1_gnn_be2"])), (wt_c, A["L1_gnn_Wt"].rearrange("a f -> f a")), (bt_c, col(A["L1_gnn_bt"])),
                     (brow[:, :], one_row(A["L1_gnn_bn1"])), (bc[:, 0, :], over_nodes(A["L1_gnn_bn2"]))]
            times = A["edge_w"].rearrange("t e -> (t e)")
            with nc.Block() as block:
                @block.sync
                def _(sp):
                    load_phase_part(sp, loads)

                    def body(i, first):
                        for r in range(2):
                            g = i * 2 + r
                            if not first:
                                sp.wait_ge(made.sem, made.at(g - 1))
                            sp.dma_start(attrT[:, r, :], A["edge_attr_T"][:, ds(g * GROUP, GROUP)]).then_inc(ring_in[r].sem, 16)
                            if not first:
                                sp.wait_ge(mixed.sem, mixed.at(g - 1))
                            sp.dma_start(ts_bc[:, r, :], times[ds(g * GROUP, GROUP)].partition_broadcast(P)).then_inc(ring_in[2 + r].sem, 16)
                    trips(sp, body, GROUPS // 2)

                @block.tensor
                def _(pe):
                    pe.wait_ge(loaded.sem, loaded.at(16 * len(loads)))

                    def body(i, first):
                        for r in range(2):
                            g = i * 2 + r
                            pe.wait_ge(ring_in[r].sem, ring_in[r].at(16 * (i + 1)))
                            if not first:
                                pe.wait_ge(evac.sem, evac.at(g - 1))
                            pe.matmul(ps[:, r, :], we1, attrT[:, r, :], start=True, stop=True).then_inc(made.sem, 1)
                        for r in range(2):
                            g = i * 2 + r
                            pe.wait_ge(evac.sem, evac.at(g + 1))
                            if not first:
                                pe.wait_ge(copied.sem, copied.at(g - 1))
                            pe.matmul(ps[:, 2 + r, :], We2, hid[:, r, :], start=True, stop=True).then_inc(turned.sem, 1)
                        for r in range(2):
                            g = i * 2 + r
                            pe.wait_ge(copied.sem, copied.at(g + 1))
                            if not first:
                                pe.wait_ge(centred.sem, centred.at(g - 1))
                            for c in range(4):
                                mm = pe.matmul(ps[:, 4 + r, c * P:(c + 1) * P], ef[:, r, c * P:(c + 1) * P], Wn1b, start=True, stop=True)
                            mm.then_inc(rooted.sem, 1)
                    trips(pe, body, GROUPS // 2)

                @block.scalar
                def _(act):
                    act.wait_ge(loaded.sem, loaded.at(16 * len(loads)))

                    def body(i, first):
                        for r in range(2):
                            g = i * 2 + r
                            act.wait_ge(made.sem, made.at(g + 1))
                            if not first:
                                act.wait_ge(turned.sem, turned.at(g - 1))
                            act.activation(hid[:, r, :], ps[:, r, :], ACT.Relu, bias=be1).then_inc(evac.sem, 1)
                        for r in range(2):
                            g = i * 2 + r
                            act.wait_ge(ring_in[2 + r].sem, ring_in[2 + r].at(16 * (i + 1)))
                            if not first:
                                act.wait_ge(copied.sem, copied.at(g - 1))
                            act.activation(tw[:, r, :], ts_bc[:, r, :], ACT.Sigmoid, scale=wt_c, bias=bt_c).then_inc(mixed.sem, 1)
                        for r in range(2):
                            g = i * 2 + r
                            act.wait_ge(rooted.sem, rooted.at(g + 1))
                            if not first:
                                act.wait_ge(edge_out[r].sem, edge_out[r].at(16 * i))
                            act.activation(zout[:, r, :], ps[:, 4 + r, :], ACT.Copy).then_inc(centred.sem, 1)
                    trips(act, body, GROUPS // 2)

                @block.vector
                def _(dve):
                    def body(i, first):
                        for r in range(2):
                            g = i * 2 + r
                            dve.wait_ge(turned.sem, turned.at(g + 1))
                            dve.wait_ge(mixed.sem, mixed.at(g + 1))
                            if not first:
                                dve.wait_ge(rooted.sem, rooted.at(g - 1))
                            dve.scalar_tensor_tensor(ef[:, r, :], ps[:, 2 + r, :], be2, tw[:, r, :], ALU.add, ALU.mult).then_inc(copied.sem, 1)
                    trips(dve, body, GROUPS // 2)

                @block.gpsimd
                def _(pool):
                    def body(i, first):
                        for r in range(2):
                            g = i * 2 + r
                            pool.wait_ge(centred.sem, centred.at(g + 1))
                            pool.dma_start(edge_part[ds(g * 4, 4), :, :].rearrange("t e f -> e t f"),
                                           zout[:, r, :].rearrange("p (t f) -> p t f", t=4)).then_inc(edge_out[r].sem, 16)
                    trips(pool, body, GROUPS // 2)
                    for r in range(2):
                        pool.wait_ge(edge_out[r].sem, edge_out[r].at(16 * (GROUPS // 2)))
            loaded.base += 16 * len(loads)
            for s in (made, evac, turned, copied, rooted, centred, mixed):
                s.base += GROUPS
            for s in ring_in[0:4] + edge_out:
                s.base += 16 * (GROUPS // 2)

            table_phase(Xn, w=Wn1a, row=brow[:, :])
            share = arena[:, 0:HALF * H].rearrange("p (r f) -> p r f", r=HALF)
            hidden = arena[:, 2048:2048 + HALF * H].rearrange("p (r f) -> p r f", r=HALF)
            relu_h = arena[:, 4096:4096 + HALF * H].rearrange("p (r f) -> p r f", r=HALF)
            with nc.Block() as block:
                @block.gpsimd
                def _(pool):
                    gathers(pool, table, H)

                @block.sync
                def _(sp):
                    def body(i, first):
                        for u in range(U):
                            j = i * U + u
                            t = sp.value_load(tile_i[0:1, ds(j, 1)], min_val=0, max_val=TILES - 1)
                            if not (first and u < HALF):
                                sp.wait_ge(mixed.sem, mixed.at(j - HALF + 1))
                            sp.dma_start(share[:, u % HALF, :], edge_part[ds(t, 1), :, :].rearrange("a e f -> (a e) f")).then_inc(ring_in[u % HALF].sem, 16)
                    trips(sp, body)

                @block.vector
                def _(dve):
                    def join(i, u, first):
                        j = i * U + u
                        dve.wait_ge(gathered[u].sem, gathered[u].at(16 * (i + 1)))
                        dve.wait_ge(ring_in[u % HALF].sem, ring_in[u % HALF].at(32 * i + 16 * (u // HALF) + 16))
                        if not (first and u < HALF):
                            dve.wait_ge(evac.sem, evac.at(j - HALF + 1))
                        dve.tensor_tensor(hidden[:, u % HALF, :], share[:, u % HALF, :], G[:, u, 0:H], ALU.add).then_inc(mixed.sem, 1)
                    onehots(dve, None, join)

                @block.scalar
                def _(act):
                    def body(i, first):
                        for u in range(U):
                            j = i * U + u
                            act.wait_ge(mixed.sem, mixed.at(j + 1))
                            if not (first and u < HALF):
                                act.wait_ge(step_done.sem, step_done.at(j - HALF + 1))
                            act.activation(relu_h[:, u % HALF, :], hidden[:, u % HALF, :], ACT.Relu).then_inc(evac.sem, 1)
                    trips(act, body)

                @block.tensor
                def _(pe):
                    fill_rows(pe, None)
                    pe.matmul(misc[:, 0:NB], ident[:, :], zeros[:, 0:NB], start=True, stop=False, skip_group_check=True)

                    def body(i, first):
                        for u in range(U):
                            j = i * U + u
                            b = step_block(pe, j)
                            pe.wait_ge(onehot_ready.sem, onehot_ready.at(j + 1))
                            o = onehot[:, u % HALF, :]
                            pe.matmul(misc[:, ds(b, 1)], o, ones[:, 0:1], start=False, stop=False, skip_group_check=True)
                            pe.wait_ge(evac.sem, evac.at(j + 1))
                            pe.matmul(accf[:, ds(b * P, P)], relu_h[:, u % HALF, :], o,
                                      start=False, stop=False, skip_group_check=True).then_inc(step_done.sem, 1)
                    trips(pe, body)
            gather_pass_over()
            mixed.base += STEPS
            evac.base += STEPS
            for s in ring_in:
                s.base += 32 * TRIPS

            with nc.Block() as block:
                @block.scalar
                def _(act):
                    for k in range(BANKS):
                        a, b, _ = span(k)
                        act.activation(HF[:, a:b], accf[:, a:b], ACT.Copy).then_inc(evac.sem, 1)

                @block.tensor
                def _(pe):
                    for k in range(BANKS):
                        pe.wait_ge(evac.sem, evac.at(k + 1))
                        for b in span(k)[2]:
                            mm = pe.matmul(accf[:, b * P:(b + 1) * P], HF[:, b * P:(b + 1) * P], Wn2, start=True, stop=True)
                        mm.then_inc(made.sem, 1)

                @block.vector
                def _(dve):
                    ch = Chain(dve, vdone)
                    ch(dve.tensor_copy(deg[:, :], misc[:, 0:NB]))
                    ch(dve.tensor_tensor(Hn[:, :, :], full(deg[:, :]), bc[:, 0:1, :].to_broadcast([P, NB, H]), ALU.mult))
                    ch(dve.scalar_tensor_tensor(Hn[:, :, :].rearrange("p b f -> p (b f)"), Xn[:, :, :].rearrange("p b f -> p (b f)"), 2.0,
                                                Hn[:, :, :].rearrange("p b f -> p (b f)"), ALU.mult, ALU.add))
                    dve.wait_ge(made.sem, made.at(BANKS))
                    ch(dve.tensor_tensor(Xn[:, :, :], Hn[:, :, :], acc_nodes, ALU.add))
                    ch.close()
            evac.base += BANKS
            made.base += BANKS
            residual_norm_phase()

        if STAGE >= 3:
            relw = arena[:, 0:R8 * H]
            RING = 4
            rows8 = arena[:, 2048:2048 + RING * R8 * H].rearrange("p (r c) -> p r c", r=RING)
            Wl = wts[:, 0, :]

            def relation_table_phase(src, W, Wl_dram, b_dram):
                table_phase(src, loads=[(relw, W.rearrange("i r o -> i (r o)")), (Wl, Wl_dram), (brow[:, :], one_row(b_dram))],
                            index=(t8_s, R8))
                with nc.Block() as block:
                    @block.tensor
                    def _(pe):
                        for b in range(NB):
                            for c in range(2):
                                n = 2 * b + c
                                if n >= 8:
                                    pe.wait_ge((evac if c == 0 else copied).sem, (evac if c == 0 else copied).at(b - 3))
                                pe.matmul(ps[:, n % 8, :], XT[:, b * P:(b + 1) * P], relw[:, c * 512:(c + 1) * 512],
                                          start=True, stop=True).then_inc(made.sem, 1)

                    @block.scalar
                    def _(act):
                        for b in range(NB):
                            act.wait_ge(made.sem, made.at(2 * b + 1))
                            if b >= RING:
                                act.wait_ge(ring_out[b % RING].sem, ring_out[b % RING].at(16 * (b // RING)))
                            act.activation(rows8[:, b % RING, 0:512], ps[:, 2 * b % 8, :], ACT.Copy).then_inc(evac.sem, 1)

                    @block.vector
                    def _(dve):
                        for b in range(NB):
                            dve.wait_ge(made.sem, made.at(2 * b + 2))
                            if b >= RING:
                                dve.wait_ge(ring_out[b % RING].sem, ring_out[b % RING].at(16 * (b // RING)))
                            dve.tensor_copy(rows8[:, b % RING, 512:1024], ps[:, (2 * b + 1) % 8, :]).then_inc(copied.sem, 1)

                    @block.sync
                    def _(sp):
                        for b in range(NB):
                            sp.wait_ge(evac.sem, evac.at(b + 1))
                            sp.wait_ge(copied.sem, copied.at(b + 1))
                            sp.dma_start(table8[b * P * R8:(b + 1) * P * R8, :].rearrange("(n r) f -> n (r f)", r=R8),
                                         rows8[:, b % RING, :]).then_inc(ring_out[b % RING].sem, 16)
                        for r in range(RING):
                            sp.wait_ge(ring_out[r].sem, ring_out[r].at(16 * len(range(r, NB, RING))))
                made.base += 2 * NB
                evac.base += NB
                copied.base += NB
                for r in range(RING):
                    ring_out[r].base += 16 * len(range(r, NB, RING))

            relation_table_phase(Xn, A["L2_W1"], A["L2_gnn_Wl1"], A["L2_gnn_b1"])
            aggregate_phase(table8, None, root=Wl, row=brow[:, :])
            with nc.Block() as block:
                @block.scalar
                def _(act):
                    act.activation(Hn[:, :, :].rearrange("p b f -> p (b f)"), accf[:, 0:NP], ACT.Relu)
            relation_table_phase(Hn, A["L2_W2"], A["L2_gnn_Wl2"], A["L2_gnn_b2"])
            aggregate_phase(table8, None, root=Wl, row=brow[:, :])
            residual_norm_phase(lambda ch, dve: ch(dve.tensor_tensor(Xn[:, :, :], Xn[:, :, :], acc_nodes, ALU.add)))

        if STAGE >= 4:
            LINKS = GSTEPS * P
            Qn = arena[:, 0:NP].rearrange("p (b f) -> p b f", f=H)
            masked = arena[:, NP:3 * NP].rearrange("p (r n) -> p r n", r=2)
            types_bc = arena[:, 3 * NP:4 * NP].bitcast(I32)
            type_w = arena[:, 4 * NP:4 * NP + 2 * H].rearrange("p (r o) -> p r o", r=2)
            block_k = arena[:, 3200:7296].rearrange("p (t c) -> p t c", t=T32)
            block_v = arena[:, 7296:11392].rearrange("p (t c) -> p t c", t=T32)
            raw = arena[:, 11392:12416].rearrange("p (a t o) -> p a t o", a=2, t=T32)
            pri = arena[:, 12416:12448]
            rows32 = arena[:, 12480:12480 + 4 * 2048].rearrange("p (q t c) -> p q t c", q=4, t=8)
            node_cols = G[:, 0, :].rearrange("p (a n) -> p a n", a=2)
            score = arena[:, 3200:3200 + STEPS * HEADS].rearrange("p (s h) -> p s h", h=HEADS)
            onehotT = arena[:, 6528:6528 + 4 * P].rearrange("p (r e) -> p r e", r=4)
            prod = arena[:, 7040:7040 + 4 * P].rearrange("p (r e) -> p r e", r=4)
            scan_in = arena[:, 7600:7600 + LINKS]
            ahead = arena[:, 10928:10928 + LINKS]
            behind = arena[:, 14256:14256 + LINKS]
            rows = arena[0:1, 17600:17600 + 8 * P].rearrange("p (r x) -> p r x", r=8)
            carry = arena[:, 18700:18702]
            gsum = arena[:, 18704:18706]
            rs8 = arena[:, 18720:18720 + NB * HEADS]
            alpha = arena[:, 18940:18940 + NB]
            types_n = arena[:, 18980:18980 + NB].bitcast(I32)
            skip_bc = arena[:, 19010:19010 + NT]
            eq_types = arena[:, 19040:19040 + NB * NT].rearrange("p (b t) -> p b t", t=NT)
            grow = arena[0:1, 20700:20700 + 2 * P].rearrange("p (r x) -> p r x", r=2)
            link = arena[:, 24500 - LINKS - 1:24500]
            vals = arena[:, 7600:7600 + HALF * H].rearrange("p (r f) -> p r f", r=HALF)
            msgs = arena[:, 8624:8624 + HALF * H].rearrange("p (r f) -> p r f", r=HALF)
            keep = w_s
            g_bc, b_bc = bc[:, 0, :], bc[:, 1, :]
            ff_w = wts[:, 4, :]

            def typed_phase(W, src, dst, node_major):
                with nc.Block() as block:
                    @block.sync
                    def _(sp):
                        sp.dma_start(types_bc, A["node_type"].partition_broadcast(P)).then_inc(loaded.sem, 16)

                        def body(i, first):
                            for r in range(2):
                                t = 2 * i + r
                                if not first:
                                    sp.wait_ge(made.sem, made.at(t - 1))
                                sp.dma_start(type_w[:, r, :], W[ds(t, 1), :, :].rearrange("a f o -> (a f) o")).then_inc(ring_in[r].sem, 16)
                        trips(sp, body, NT // 2)

                    @block.vector
                    def _(dve):
                        dve.wait_ge(loaded.sem, loaded.at(16))

                        def body(i, first):
                            for r in range(2):
                                t = 2 * i + r
                                if not first:
                                    dve.wait_ge(made.sem, made.at(t - 1))
                                dve.scalar_tensor_tensor(masked[:, r, :], types_bc, iota_row[:, ds(t, 1)], src,
                                                         ALU.is_equal, ALU.mult).then_inc(mixed.sem, 1)
                        trips(dve, body, NT // 2)

                    @block.tensor
                    def _(pe):
                        fill_rows(pe, None)

                        def body(i, first):
                            for r in range(2):
                                t = 2 * i + r
                                pe.wait_ge(ring_in[r].sem, ring_in[r].at(16 * (i + 1)))
                                pe.wait_ge(mixed.sem, mixed.at(t + 1))
                                if node_major:
                                    for b in range(NB):
                                        mm = pe.matmul(accf[:, b * P:(b + 1) * P], masked[:, r, b * P:(b + 1) * P], type_w[:, r, :],
                                                       start=False, stop=False, skip_group_check=True)
                                else:
                                    for k in range(BANKS):
                                        a, b, _ = span(k)
                                        mm = pe.matmul(accf[:, a:b], type_w[:, r, :], masked[:, r, a:b],
                                                       start=False, stop=False, skip_group_check=True)
                                mm.then_inc(made.sem, 1)
                        trips(pe, body, NT // 2)

                    if dst is not None:
                        @block.scalar
                        def _(act):
                            act.wait_ge(made.sem, made.at(NT))
                            act.activation(dst, accf[:, 0:NP], ACT.Copy)
                loaded.base += 16
                made.base += NT
                mixed.base += NT
                for r in range(2):
                    ring_in[r].base += 16 * (NT // 2)

            def key_value_table_phase(l):
                kT, vT = HF[:, :], Hn[:, :, :].rearrange("p b f -> p (b f)")
                with nc.Block() as block:
                    @block.sync
                    def _(sp):
                        sp.dma_start(raw[:, 0, :, :].rearrange("p t o -> p (t o)"), A["L3_Watt"][l]).then_inc(loaded.sem, 16)
                        sp.dma_start(raw[:, 1, :, :].rearrange("p t o -> p (t o)"), A["L3_Wmsg"][l]).then_inc(loaded.sem, 16)
                        for h in range(HEADS):
                            sp.dma_start(pri[h * HS:(h + 1) * HS, :], A["L3_gnn_pri"][l, h].partition_broadcast(HS)).then_inc(loaded.sem, 16)

                        def body(i, first):
                            for q in range(4):
                                sp.wait_ge(copied.sem, copied.at(4 * i + q + 1))
                                sp.dma_start(table32.rearrange("(n t) f -> n t f", t=T32)[ds(i * P, P), q * 8:(q + 1) * 8, :],
                                             rows32[:, q, :, :]).then_inc(ring_out[q].sem, 16)
                        trips(sp, body, NB)
                        for q in range(4):
                            sp.wait_ge(ring_out[q].sem, ring_out[q].at(16 * NB))

                    @block.gpsimd
                    def _(pool):
                        def body(i, first):
                            if not first:
                                pool.wait_ge(made.sem, made.at(4 * i))
                            pool.tensor_copy(node_cols[:, 0, :], kT[:, ds(i * P, P)]).then_inc(idx_ready.sem, 1)
                            if not first:
                                pool.wait_ge(turned.sem, turned.at(4 * i))
                            pool.tensor_copy(node_cols[:, 1, :], vT[:, ds(i * P, P)]).then_inc(go.sem, 1)
                        trips(pool, body, NB)

                    @block.tensor
                    def _(pe):
                        pe.wait_ge(centred.sem, centred.at(2))

                        def body(i, first):
                            for q in range(4):
                                n = 4 * i + q
                                s = 4 * (q % 2)
                                if q == 0:
                                    pe.wait_ge(idx_ready.sem, idx_ready.at(i + 1))
                                if not (first and q < 2):
                                    pe.wait_ge(evac.sem, evac.at(n - 1))
                                for c in range(2):
                                    mm = pe.matmul(ps[:, s + c, :], node_cols[:, 0, :],
                                                   block_k[:, 8 * q + 4 * c:8 * q + 4 * c + 4, :].rearrange("p t c -> p (t c)"), start=True, stop=True)
                                mm.then_inc(made.sem, 1)
                                if q == 0:
                                    pe.wait_ge(go.sem, go.at(i + 1))
                                if not (first and q < 2):
                                    pe.wait_ge(copied.sem, copied.at(n - 1))
                                for c in range(2):
                                    mm = pe.matmul(ps[:, s + 2 + c, :], node_cols[:, 1, :],
                                                   block_v[:, 8 * q + 4 * c:8 * q + 4 * c + 4, :].rearrange("p t c -> p (t c)"), start=True, stop=True)
                                mm.then_inc(turned.sem, 1)
                        trips(pe, body, NB)

                    @block.scalar
                    def _(act):
                        def body(i, first):
                            for q in range(4):
                                act.wait_ge(made.sem, made.at(4 * i + q + 1))
                                if not first:
                                    act.wait_ge(ring_out[q].sem, ring_out[q].at(16 * i))
                                act.activation(rows32[:, q, :, 0:H], ps[:, 4 * (q % 2):4 * (q % 2) + 2, :].rearrange("p a (t f) -> p (a t) f", f=H),
                                               ACT.Copy).then_inc(evac.sem, 1)
                        trips(act, body, NB)

                    @block.vector
                    def _(dve):
                        ch = Chain(dve, vdone)
                        dve.wait_ge(loaded.sem, loaded.at(16 * (2 + HEADS)))
                        ch(dve.tensor_tensor(raw[:, 0, :, :], raw[:, 0, :, :], pri.unsqueeze(2).to_broadcast([P, T32, HS]), ALU.mult))
                        ch(dve.tensor_scalar(raw[:, 0, :, :], raw[:, 0, :, :], 1.0 / HS ** 0.5, None, ALU.mult))
                        for n, blk in enumerate((block_k, block_v)):
                            dve.tensor_tensor(blk.rearrange("p t (h o) -> p t h o", o=HS),
                                              raw[:, n, :, :].unsqueeze(2).to_broadcast([P, T32, HEADS, HS]),
                                              head_mask[:, :].unsqueeze(1).unsqueeze(3).to_broadcast([P, T32, HEADS, HS]),
                                              ALU.mult).then_inc(centred.sem, 1)

                        def body(i, first):
                            for q in range(4):
                                dve.wait_ge(turned.sem, turned.at(4 * i + q + 1))
                                dve.wait_ge(evac.sem, evac.at(4 * i + q + 1))
                                if not first:
                                    dve.wait_ge(ring_out[q].sem, ring_out[q].at(16 * i))
                                dve.tensor_copy(rows32[:, q, :, H:2 * H],
                                                ps[:, 4 * (q % 2) + 2:4 * (q % 2) + 4, :].rearrange("p a (t f) -> p (a t) f", f=H)).then_inc(copied.sem, 1)
                        trips(dve, body, NB)
                        ch.close()
                loaded.base += 16 * (2 + HEADS)
                idx_ready.base += NB
                go.base += NB
                centred.base += 2
                for s in (made, turned, evac, copied):
                    s.base += 4 * NB
                for q in range(4):
                    ring_out[q].base += 16 * NB

            def score_phase():
                LAG = 3
                with nc.Block() as block:
                    @block.gpsimd
                    def _(pool):
                        def free(pool, i, h):
                            pool.wait_ge(mixed.sem, mixed.at(i * U - U + (h + 1) * HALF))
                            for u in range(h * HALF, (h + 1) * HALF):
                                pool.wait_ge(ring_out[u].sem, ring_out[u].at(16 * i))
                        gathers(pool, table32, 2 * H, free)

                    @block.sync
                    def _(sp):
                        def body(i, first):
                            for u in range(U):
                                sp.wait_ge(gathered[u].sem, gathered[u].at(16 * (i + 1)))
                                sp.dma_start(values[ds(i * U + u, 1), :, :].rearrange("a e f -> (a e) f"), G[:, u, H:2 * H]).then_inc(ring_out[u].sem, 16)
                        trips(sp, body)
                        for u in range(U):
                            sp.wait_ge(ring_out[u].sem, ring_out[u].at(16 * TRIPS))

                    @block.vector
                    def _(dve):
                        def multiply(i, u, first):
                            j = i * U + u
                            g = gathered[u]
                            dve.wait_ge(g.sem, g.at(16 * (i + 1)))
                            dve.wait_ge(made.sem, made.at(j + 1))
                            if not (first and u < 4):
                                dve.wait_ge(copied.sem, copied.at(j - 3))
                            dve.tensor_tensor(prod[:, u % 4, :], G[:, u, 0:H], ps[:, 4 + u % 4, 0:P], ALU.mult).then_inc(mixed.sem, 1)

                        def reduce(i, u):
                            j = i * U + u
                            dve.wait_ge(mixed.sem, mixed.at(j + 1))
                            dve.tensor_reduce(score[:, ds(j, 1), :].rearrange("p a h -> p (a h)"),
                                              prod[:, u % 4, :].rearrange("p (h o) -> p h o", o=HS), AX.X, ALU.add).then_inc(copied.sem, 1)

                        def lagged(i, u, first):
                            if not (first and u < LAG):
                                multiply(i if u >= LAG else i - 1, (u - LAG) % U, first)
                            if not (first and u < LAG + 1):
                                reduce(i if u >= LAG + 1 else i - 1, (u - LAG - 1) % U)
                        onehots(dve, None, lagged)
                        for u in range(U - LAG, U):
                            multiply(TRIPS - 1, u, False)
                            reduce(TRIPS - 1, u - 1)
                        reduce(TRIPS - 1, U - 1)

                    @block.scalar
                    def _(act):
                        def body(i, first):
                            for u in range(U):
                                j = i * U + u
                                act.wait_ge(step_done.sem, step_done.at(j + 1))
                                if not (first and u < 4):
                                    act.wait_ge(made.sem, made.at(j - 3))
                                act.activation(onehotT[:, u % 4, :], ps[:, u % 4, 0:P], ACT.Copy).then_inc(evac.sem, 1)
                        trips(act, body)

                    @block.tensor
                    def _(pe):
                        def turn(i, u, fresh):
                            j = i * U + u
                            pe.wait_ge(onehot_ready.sem, onehot_ready.at(j + 1))
                            if not fresh:
                                pe.wait_ge(evac.sem, evac.at(j - 3))
                            pe.transpose(ps[:, u % 4, 0:P], onehot[:, u % HALF, :], ident[:, :]).then_inc(step_done.sem, 1)

                        def query(i, u, fresh):
                            j = i * U + u
                            b = step_block(pe, j)
                            pe.wait_ge(evac.sem, evac.at(j + 1))
                            if not fresh:
                                pe.wait_ge(mixed.sem, mixed.at(j - 3))
                            pe.matmul(ps[:, 4 + u % 4, 0:P], onehotT[:, u % 4, :], Qn_flat[:, ds(b * P, P)], start=True, stop=True).then_inc(made.sem, 1)

                        def body(i, first):
                            for u in range(U):
                                turn(i, u, first and u < 4)
                                if not (first and u < 2):
                                    query(i if u >= 2 else i - 1, (u - 2) % U, first and u < 6)
                        Qn_flat = Qn.rearrange("p b f -> p (b f)")
                        trips(pe, body)
                        query(TRIPS - 1, U - 2, False)
                        query(TRIPS - 1, U - 1, False)
                gather_pass_over()
                for s in (mixed, made, copied, evac):
                    s.base += STEPS
                for s in ring_out:
                    s.base += 16 * TRIPS

            def turn_steps(pe, t):
                for k in range(7):
                    for g in range(4 * k, min(GSTEPS, 4 * k + 4)):
                        mm = pe.transpose(accf[:, g * P:(g + 1) * P], t[:, g, :], ident[:, :])
                    mm.then_inc(turned.sem, 1)

            def link_phase():
                D = arena[:, 0:LINKS + 1]
                wide = arena[:, 3400:3400 + STEPS * HEADS].rearrange("p (g x) -> p g x", g=GSTEPS)
                with nc.Block() as block:
                    @block.vector
                    def _(dve):
                        ch = Chain(dve, vdone)
                        dve.tensor_copy(wide.rearrange("p g (c h) -> p g c h", h=HEADS),
                                        dv_s[:, :].rearrange("p (c g) -> p g c", g=GSTEPS).unsqueeze(3).to_broadcast([P, GSTEPS, CHUNKS, HEADS])).then_inc(mixed.sem, 1)
                        ch(dve.tensor_scalar(keep[:, :], dv_s[:, :], 0.0, 2 * BIG, ALU.is_gt, ALU.mult))
                        ch(dve.tensor_scalar(keep[:, :], keep[:, :], BIG, None, ALU.subtract))
                        dve.wait_ge(turned.sem, turned.at(7))
                        dve.tensor_copy(D[:, 1:LINKS + 1], accf[:, 0:LINKS]).then_inc(copied.sem, 1)
                        dve.wait_ge(made.sem, made.at(1))
                        ch(dve.tensor_copy(D[:, 0:1], misc[:, 0:1]))
                        dve.wait_ge(copied.sem, copied.at(1))
                        ch(dve.tensor_tensor(link[:, 0:LINKS], D[:, 1:LINKS + 1], D[:, 0:LINKS], ALU.is_equal))
                        dve.scalar_tensor_tensor(link[:, 0:LINKS], D[:, 1:LINKS + 1], 0.0, link[:, 0:LINKS], ALU.is_equal, ALU.max).then_inc(copied.sem, 1)
                        dve.wait_ge(made.sem, made.at(2))
                        ch(dve.tensor_copy(link[:, LINKS:LINKS + 1], misc[:, 1:2]))
                        ch(dve.tensor_scalar(link, link, 2 * BIG, -BIG, ALU.mult, ALU.add))
                        ch(dve.tensor_reduce(gsum[:, 0:1], link[:, 0:LINKS], AX.X, ALU.min))
                        dve.tensor_reduce(gsum[:, 1:2], link[:, 1:LINKS + 1], AX.X, ALU.min).then_inc(copied.sem, 1)
                        dve.wait_ge(turned.sem, turned.at(8))
                        ch(dve.tensor_copy(grow[:, 0, :].rearrange("p (h c) -> p h c", h=HEADS), ps[0:1, 0, 0:P].rearrange("p (c h) -> p h c", h=HEADS)))
                        ch(dve.tensor_copy(grow[:, 1, :].rearrange("p (h c) -> p h c", h=HEADS),
                                           ps[0:1, 1, 0:P].rearrange("p (c h) -> p h c", h=HEADS)[:, :, ::-1]))
                        ch.close()

                    @block.tensor
                    def _(pe):
                        pe.wait_ge(mixed.sem, mixed.at(1))
                        turn_steps(pe, wide)
                        pe.wait_ge(copied.sem, copied.at(1))
                        pe.matmul(misc[:, 0:1], shift[:, 0, :], D[:, LINKS:LINKS + 1], start=True, stop=True).then_inc(made.sem, 1)
                        pe.wait_ge(copied.sem, copied.at(2))
                        pe.matmul(misc[:, 1:2], shift[:, 1, :], link[:, 0:1], start=True, stop=True).then_inc(made.sem, 1)
                        pe.wait_ge(copied.sem, copied.at(3))
                        pe.transpose(ps[0:1, 0, 0:P], gsum[:, 0:1], ident[:, :])
                        pe.transpose(ps[0:1, 1, 0:P], gsum[:, 1:2], ident[:, :]).then_inc(turned.sem, 1)
                mixed.base += 1
                turned.base += 8
                copied.base += 3
                made.base += 2

            def softmax_phase():
                wide = arena[:, 14256:14256 + STEPS * HEADS].rearrange("p (g x) -> p g x", g=GSTEPS)
                with nc.Block() as block:
                    @block.vector
                    def _(dve):
                        ch = Chain(dve, vdone)
                        dve.tensor_tensor(wide.rearrange("p g (c h) -> p g c h", h=HEADS),
                                          score.rearrange("p (c g) h -> p g c h", g=GSTEPS),
                                          keep[:, :].rearrange("p (c g) -> p g c", g=GSTEPS).unsqueeze(3).to_broadcast([P, GSTEPS, CHUNKS, HEADS]),
                                          ALU.min).then_inc(mixed.sem, 1)
                        dve.wait_ge(turned.sem, turned.at(7))
                        ch(dve.tensor_copy(scan_in, accf[:, 0:LINKS]))
                        rev = slice(None, None, -1)

                        def scans(first_f, first_b):
                            ch(dve.tensor_tensor_scan(ahead, link[:, 0:LINKS], scan_in, first_f, ALU.min, ALU.max))
                            return dve.tensor_tensor_scan(behind[:, rev], link[:, 1:LINKS + 1][:, rev], scan_in[:, rev], first_b, ALU.min, ALU.max)
                        scans(-BIG, -BIG).then_inc(copied.sem, 1)
                        dve.wait_ge(turned.sem, turned.at(8))
                        ch(dve.tensor_copy(rows[:, 0, :].rearrange("p (h c) -> p h c", h=HEADS), ps[0:1, 0, 0:P].rearrange("p (c h) -> p h c", h=HEADS)))
                        ch(dve.tensor_copy(rows[:, 1, :].rearrange("p (h c) -> p h c", h=HEADS),
                                           ps[0:1, 1, 0:P].rearrange("p (c h) -> p h c", h=HEADS)[:, :, rev]))
                        for r in range(2):
                            ch(dve.tensor_tensor_scan(rows[:, 2 + r, :], grow[:, r, :], rows[:, r, :], -BIG, ALU.min, ALU.max))
                            ch(dve.memset(rows[:, 4 + r, :], -BIG))
                        out_f = rows[:, 4, :].rearrange("p (c h) -> p h c", h=HEADS)
                        out_b = rows[:, 5, :].rearrange("p (c h) -> p h c", h=HEADS)
                        in_f = rows[:, 2, :].rearrange("p (h c) -> p h c", h=HEADS)
                        in_b = rows[:, 3, :].rearrange("p (h c) -> p h c", h=HEADS)
                        ch(dve.tensor_copy(out_f[:, :, 1:CHUNKS], in_f[:, :, 0:CHUNKS - 1]))
                        dve.tensor_copy(out_b[:, :, rev][:, :, 1:CHUNKS], in_b[:, :, 0:CHUNKS - 1]).then_inc(copied.sem, 1)
                        dve.wait_ge(turned.sem, turned.at(9))
                        ch(dve.tensor_copy(carry, misc[:, 0:2]))
                        ch(scans(carry[:, 0:1], carry[:, 1:2]))
                        ch(dve.tensor_tensor(ahead, ahead, behind, ALU.max))
                        dve.tensor_tensor(scan_in, scan_in, ahead, ALU.subtract).then_inc(copied.sem, 1)
                        for k in range(7):
                            g0, g1 = 4 * k, min(GSTEPS, 4 * k + 4)
                            dve.wait_ge(turned.sem, turned.at(10 + k))
                            dve.tensor_copy(score.rearrange("p (c g) h -> p g c h", g=GSTEPS)[:, g0:g1, :, :],
                                            accf[:, g0 * P:g1 * P].rearrange("p (g c h) -> p g c h", c=CHUNKS, h=HEADS))
                        ch.close()

                    @block.scalar
                    def _(act):
                        act.wait_ge(copied.sem, copied.at(3))
                        act.activation(scan_in, scan_in, ACT.Exp).then_inc(evac.sem, 1)

                    @block.tensor
                    def _(pe):
                        pe.wait_ge(mixed.sem, mixed.at(1))
                        turn_steps(pe, wide)
                        pe.wait_ge(copied.sem, copied.at(1))
                        pe.transpose(ps[0:1, 0, 0:P], ahead[:, LINKS - 1:LINKS], ident[:, :])
                        pe.transpose(ps[0:1, 1, 0:P], behind[:, 0:1], ident[:, :]).then_inc(turned.sem, 1)
                        pe.wait_ge(copied.sem, copied.at(2))
                        pe.transpose(misc[:, 0:1], rows[:, 4, :], ident[0:1, 0:1])
                        pe.transpose(misc[:, 1:2], rows[:, 5, :], ident[0:1, 0:1]).then_inc(turned.sem, 1)
                        pe.wait_ge(evac.sem, evac.at(1))
                        turn_steps(pe, scan_in.rearrange("p (g e) -> p g e", e=P))
                mixed.base += 1
                turned.base += 16
                copied.base += 3
                evac.base += 1

            def message_phase():
                with nc.Block() as block:
                    @block.sync
                    def _(sp):
                        def body(i, first):
                            for u in range(U):
                                j = i * U + u
                                if not (first and u < HALF):
                                    sp.wait_ge(mixed.sem, mixed.at(j - HALF + 1))
                                sp.dma_start(vals[:, u % HALF, :], values[ds(j, 1), :, :].rearrange("a e f -> (a e) f")).then_inc(ring_in[u % HALF].sem, 16)
                        trips(sp, body)

                    @block.vector
                    def _(dve):
                        def weigh(i, u, first):
                            j = i * U + u
                            dve.wait_ge(ring_in[u % HALF].sem, ring_in[u % HALF].at(32 * i + 16 * (u // HALF) + 16))
                            dve.tensor_tensor(msgs[:, u % HALF, :].rearrange("p (h o) -> p h o", o=HS),
                                              vals[:, u % HALF, :].rearrange("p (h o) -> p h o", o=HS),
                                              score[:, ds(j, 1), :].rearrange("p a h -> p (a h)").unsqueeze(2).to_broadcast([P, HEADS, HS]),
                                              ALU.mult).then_inc(mixed.sem, 1)
                        onehots(dve, None, weigh)

                    @block.tensor
                    def _(pe):
                        fill_rows(pe, None)
                        pe.matmul(misc[:, 0:NB * HEADS], ident[:, :], zeros[:, 0:NB * HEADS], start=True, stop=False, skip_group_check=True)

                        def body(i, first):
                            for u in range(U):
                                j = i * U + u
                                b = step_block(pe, j)
                                pe.wait_ge(onehot_ready.sem, onehot_ready.at(j + 1))
                                o = onehot[:, u % HALF, :]
                                pe.matmul(misc[:, ds(b * HEADS, HEADS)], o, score[:, ds(j, 1), :].rearrange("p a h -> p (a h)"),
                                          start=False, stop=False, skip_group_check=True)
                                pe.wait_ge(mixed.sem, mixed.at(j + 1))
                                pe.matmul(accf[:, ds(b * P, P)], o, msgs[:, u % HALF, :],
                                          start=False, stop=False, skip_group_check=True).then_inc(step_done.sem, 1)
                        trips(pe, body)
                step_pass_over()
                mixed.base += STEPS
                for s in ring_in:
                    s.base += 32 * TRIPS

            for l in range(2):
                if l == 0:
                    table_phase(Xn, index=(t32_s, T32))
                    with nc.Block() as block:
                        @block.gpsimd
                        def _(pool):
                            pool.tensor_copy(Lx[:, :, :], Xn[:, :, :])
                    link_phase()
                else:
                    table_phase(Lx)
                typed_phase(A["L3_gnn_Wk"][l], XT[:, :], HF[:, :], False)
                typed_phase(A["L3_gnn_Wv"][l], XT[:, :], Hn[:, :, :].rearrange("p b f -> p (b f)"), False)
                typed_phase(A["L3_gnn_Wq"][l], XT[:, :], arena[:, 0:NP], True)
                key_value_table_phase(l)
                score_phase()
                softmax_phase()
                message_phase()
                with nc.Block() as block:
                    @block.vector
                    def _(dve):
                        ch = Chain(dve, vdone)
                        ch(dve.tensor_scalar(rs8, misc[:, 0:NB * HEADS], 1e-20, None, ALU.max))
                        ch(dve.reciprocal(rs8, rs8))
                        ch(dve.tensor_tensor(Hn[:, :, :].rearrange("p b (h o) -> p (b h) o", o=HS),
                                             accf[:, 0:NP].rearrange("p (x o) -> p x o", o=HS),
                                             rs8.unsqueeze(2).to_broadcast([P, NB * HEADS, HS]), ALU.mult))
                        ch.close()
                table_phase(Hn)
                typed_phase(A["L3_gnn_Wa"][l], XT[:, :], None, True)
                with nc.Block() as block:
                    @block.sync
                    def _(sp):
                        sp.dma_start(skip_bc, over_nodes(A["L3_gnn_skip"][l])).then_inc(loaded.sem, 16)
                        sp.dma_start(types_n, A["node_type_rows"]).then_inc(loaded.sem, 16)
                        sp.dma_start(g_bc, over_nodes(A["L3_gnn_ln_g"][l])).then_inc(loaded.sem, 16)
                        sp.dma_start(b_bc, over_nodes(A["L3_gnn_ln_b"][l])).then_inc(loaded.sem, 16)

                    @block.scalar
                    def _(act):
                        act.activation(Hn[:, :, :].rearrange("p b f -> p (b f)"), accf[:, 0:NP], ACT.Sigmoid).then_inc(evac.sem, 1)
                        act.wait_ge(loaded.sem, loaded.at(64))
                        act.activation(skip_bc, skip_bc, ACT.Sigmoid).then_inc(evac.sem, 1)
                        normalise_act(act, Hn[:, :, :])

                    @block.vector
                    def _(dve):
                        ch = Chain(dve, vdone)
                        dve.wait_ge(loaded.sem, loaded.at(64))
                        dve.wait_ge(evac.sem, evac.at(2))
                        ch(dve.tensor_tensor(eq_types, types_n.unsqueeze(2).to_broadcast([P, NB, NT]),
                                             iota_row[:, 0:NT].unsqueeze(1).to_broadcast([P, NB, NT]), ALU.is_equal))
                        ch(dve.tensor_tensor(eq_types, eq_types, skip_bc.unsqueeze(1).to_broadcast([P, NB, NT]), ALU.mult))
                        ch(dve.tensor_reduce(alpha, eq_types, AX.X, ALU.add))
                        ch(dve.tensor_tensor(Hn[:, :, :], Hn[:, :, :], acc_nodes, ALU.mult))
                        ch(dve.tensor_tensor(Hn[:, :, :], Hn[:, :, :], Lx[:, :, :], ALU.subtract))
                        ch(dve.tensor_tensor(Hn[:, :, :], Hn[:, :, :], full(alpha), ALU.mult))
                        ch(dve.tensor_tensor(Hn[:, :, :], Hn[:, :, :], Lx[:, :, :], ALU.add))
                        ch(normalise(ch, dve, Hn[:, :, :], Hn[:, :, :]))
                        ch(dve.tensor_tensor(Hn[:, :, :], Hn[:, :, :], bc[:, 0:1, :].to_broadcast([P, NB, H]), ALU.mult))
                        ch(dve.tensor_tensor(Lx[:, :, :], Hn[:, :, :], bc[:, 1:2, :].to_broadcast([P, NB, H]), ALU.add))
                        ch.close()
                loaded.base += 64
                evac.base += 2
                normalised()

            table_phase(Lx, loads=[(ff_w, A["L3_gnn_ff_w"]), (brow[:, :], one_row(A["L3_gnn_ff_b"]))])
            with nc.Block() as block:
                @block.tensor
                def _(pe):
                    fill_rows(pe, brow[:, :])
                    for b in range(NB):
                        pe.matmul(accf[:, b * P:(b + 1) * P], XT[:, b * P:(b + 1) * P], ff_w, start=False, stop=False, skip_group_check=True)
            residual_norm_phase(lambda ch, dve: ch(dve.tensor_tensor(Xn[:, :, :], Xn[:, :, :], acc_nodes, ALU.add)))

        with nc.Block() as block:
            @block.sync
            def _(sp):
                sp.dma_start(out[0:(NB - 1) * P, :].rearrange("(b p) f -> p b f", p=P), Xn[:, 0:NB - 1, :]).then_inc(stored.sem, 16)
                sp.dma_start(out[(NB - 1) * P:N, :], Xn[0:LAST, NB - 1, :]).then_inc(stored.sem, 16)
                sp.wait_ge(stored.sem, stored.at(32))


def kernel(**inputs):
    import numpy as np
    import concourse.bacc as bacc
    from concourse.bass_utils import run_bass_kernel_spmd

    a = {k: np.asarray(v) for k, v in inputs.items()}
    ints = np.stack([a["src"], a["dst"], a["edge_type_32"], a["edge_type_8"]], axis=1)
    pad = np.full((EP - E, 4), 0, ints.dtype)
    pad[:, 1] = -1
    attr = a["edge_attr_64"]
    types = np.concatenate([a["node_type_16"], np.zeros(NP - N, a["node_type_16"].dtype)])
    arrays = {
        "x": a["x"], "dst": a["dst"],
        "edge_ints": np.ascontiguousarray(np.concatenate([ints, pad])).reshape(TILES, P * 4),
        "edge_w": np.concatenate([a["edge_weight"], np.zeros(EP - E, a["edge_weight"].dtype)]).reshape(TILES, P),
        "edge_attr_T": np.ascontiguousarray(np.concatenate([attr, np.zeros((EP - E, EDIM), attr.dtype)]).T),
        "node_type": types, "node_type_rows": np.ascontiguousarray(types.reshape(NB, P).T),
        "L0_neigh": np.ascontiguousarray(a["L0_gnn_lin_neigh_w"].transpose(0, 2, 1)),
        "L0_root": np.ascontiguousarray(a["L0_gnn_lin_root_w"].transpose(0, 2, 1)),
        "L2_W1": np.ascontiguousarray(a["L2_gnn_W1"].transpose(1, 0, 2)),
        "L2_W2": np.ascontiguousarray(a["L2_gnn_W2"].transpose(1, 0, 2)),
        "L3_Watt": np.ascontiguousarray(a["L3_gnn_Watt"].transpose(0, 1, 3, 2, 4)).reshape(2, H, T32 * HS),
        "L3_Wmsg": np.ascontiguousarray(a["L3_gnn_Wmsg"].transpose(0, 1, 3, 2, 4)).reshape(2, H, T32 * HS),
    }
    used = set(_PLAIN_STAGE1) | (set(_PLAIN_STAGE2) if STAGE >= 2 else set()) | (set(_PLAIN_STAGE3) if STAGE >= 3 else set()) \
        | (set(_PLAIN_STAGE4) if STAGE >= 4 else set())
    for name in sorted(used):
        arrays[name] = a[name]

    nc = bacc.Bacc("TRN2", target_bir_lowering=False, num_devices=1)
    aps = {k: nc.dram_tensor(k, v.shape, mybir.dt.from_np(v.dtype), kind="ExternalInput").ap() for k, v in arrays.items()}
    out = nc.dram_tensor("out", (N, H), F32, kind="ExternalOutput").ap()
    build(nc, aps, out)
    r = run_bass_kernel_spmd(nc, [arrays], core_ids=[0])
    return r.results[0]["out"]


_PLAIN_STAGE1 = ("L0_gnn_lin_root_b", "L0_gnn_ln_w", "L0_gnn_ln_b")
_PLAIN_STAGE2 = ("L1_gnn_We1", "L1_gnn_be1", "L1_gnn_We2", "L1_gnn_be2", "L1_gnn_Wt", "L1_gnn_bt", "L1_gnn_Wn1", "L1_gnn_bn1",
                 "L1_gnn_Wn2", "L1_gnn_bn2")
_PLAIN_STAGE3 = ("L2_gnn_Wl1", "L2_gnn_b1", "L2_gnn_Wl2", "L2_gnn_b2")
_PLAIN_STAGE4 = ("L3_gnn_Wk", "L3_gnn_Wq", "L3_gnn_Wv", "L3_gnn_Wa", "L3_gnn_pri", "L3_gnn_skip", "L3_gnn_ln_g", "L3_gnn_ln_b",
                 "L3_gnn_ff_w", "L3_gnn_ff_b")
```

```python
from contextlib import ExitStack

import concourse.bass as bass
from concourse import mybir

ALU = mybir.AluOpType
ACT = mybir.ActivationFunctionType
AX = mybir.AxisListType
F32 = mybir.dt.float32
I32 = mybir.dt.int32
ds = bass.ds

P = 128
N = 3125
E = 50000
H = 128
NB = -(-N // P)
NP = NB * P
LAST = N - (NB - 1) * P
BANKS = -(-NB // 4)
U = 16
HALF = U // 2
QUADS = U // 4
TILES = 4 * -(-E // (4 * P))
STEPS = -(-(-(-E // P) + NB - 1) // U) * U
TRIPS = STEPS // U
ALL_QUADS = STEPS // 4
SHARE_TILES = 2 * 2 * ALL_QUADS
EP = TILES * P
TCH = 4
TROWS = TILES // TCH
CROWS = 125
CCOLS = E // CROWS
L0 = 3
R8 = 8
T32 = 32
NT = 16
HEADS = 8
HS = H // HEADS
EDIM = 64
CHUNKS = P // HEADS
GSTEPS = STEPS // CHUNKS
BIG = 1e30
EPS = 1e-5
STAGE = 4


class Signal:

    def __init__(self, sem):
        self.sem, self.base = sem, 0

    def at(self, count):
        return count + self.base


class Chain:

    def __init__(self, eng, mark):
        self.eng, self.mark, self.n = eng, mark, 0

    def __call__(self, inst):
        self.n += 1
        inst.then_inc(self.mark.sem, 1)
        self.eng.wait_ge(self.mark.sem, self.mark.at(self.n))

    def close(self):
        self.mark.base += self.n


def trips(eng, body, n=TRIPS):
    body(0, True)
    with eng.Fori(1, n) as i:
        body(i, False)


def span(k):
    return 512 * k, min(NP, 512 * k + 512), range(4 * k, min(NB, 4 * k + 4))


def build(nc, A, out):
    ctx = ExitStack()
    with ctx:
        def sb(name, shape, dt=F32):
            return ctx.enter_context(nc.sbuf_tensor(name, shape, dt))

        def signal(name):
            return Signal(ctx.enter_context(nc.semaphore(name)))

        def dram(name, shape, dt=F32):
            return nc.dram_tensor(name, shape, dt, kind="Internal").ap()

        table = dram("table", [NP, H])
        table8 = dram("table8", [NP * R8, H])
        table32 = dram("table32", [NP * T32, 2 * H])
        edge_part = dram("edge_part", [SHARE_TILES, P, H])
        values = dram("values", [STEPS, P, H])

        ident = sb("ident", [P, P])
        iota_row = sb("iota_row", [P, P])
        zeros = sb("zeros", [P, 512])
        ones = sb("ones", [P, P])
        shift = sb("shift", [P, 2, P])
        head_mask = sb("head_mask", [P, HEADS])
        blk4_i = sb("blk4_i", [P, ALL_QUADS], I32)
        tile_i = sb("tile_i", [P, STEPS], I32)
        src_s = sb("src_s", [P, STEPS])
        dl_s = sb("dl_s", [P, STEPS])
        t32_s = sb("t32_s", [P, STEPS])
        t8_s = sb("t8_s", [P, STEPS])
        w_s = sb("w_s", [P, STEPS])
        dv_s = sb("dv_s", [P, STEPS])
        idx_s = sb("idx_s", [P, STEPS], I32)
        rsum = sb("rsum", [P, NB])
        deg = sb("deg", [P, NB])
        Xn = sb("Xn", [P, NB, H])
        Lx = sb("Lx", [P, NB, H])
        XT = sb("XT", [P, NP])
        Hn = sb("Hn", [P, NB, H])
        HF = sb("HF", [P, NP])
        G = sb("G", [P, U, 2 * H])
        gidx = sb("gidx", [P, U], I32)
        onehot = sb("onehot", [P, HALF, P])
        red = sb("red", [P, 4, NB])
        wts = sb("wts", [P, 6, H])
        vecs = sb("vecs", [P, 16])
        bc = sb("bc", [P, 2, H])
        brow = sb("brow", [1, H])
        arena = sb("arena", [P, 24500])

        ps = ctx.enter_context(nc.psum_tensor("ps", [P, 8, 512], F32))
        acc, misc = ps[:, 0:7, :], ps[:, 7, :]
        accf = acc.rearrange("p a b -> p (a b)")
        acc_nodes = accf[:, 0:NP].rearrange("p (b f) -> p b f", f=H)

        loaded = signal("loaded")
        stored = signal("stored")
        consts = signal("consts")
        vdone = signal("vdone")
        adone = signal("adone")
        pdone = signal("pdone")
        idx_ready = signal("idx_ready")
        go = signal("go")
        gathered = [signal(f"gathered{u}") for u in range(U)]
        onehot_ready = signal("onehot_ready")
        compared = signal("compared")
        quad_done = signal("quad_done")
        turned = signal("turned")
        evac = signal("evac")
        made = signal("made")
        copied = signal("copied")
        mixed = signal("mixed")
        centred = signal("centred")
        squared = signal("squared")
        varied = signal("varied")
        rooted = signal("rooted")
        ring_in = [signal(f"ring_in{u}") for u in range(HALF)]
        ring_out = [signal(f"ring_out{u}") for u in range(U)]

        edge_out = [signal(f"edge_out{u}") for u in range(2)]

        cube = arena[:, 0:STEPS * NB]
        dst_i = Hn[0:CROWS, 0:4, :].rearrange("p a b -> p (a b)").bitcast(I32)[:, 0:CCOLS]
        dst_f = Hn[0:CROWS, 4:8, :].rearrange("p a b -> p (a b)")[:, 0:CCOLS]
        cnt = red[:, 0, :]
        jrow_i = XT[:, 0:STEPS].bitcast(I32)
        jrow = XT[:, 512:512 + STEPS]
        blk_f = XT[:, 1024:1024 + STEPS]
        tile_f = XT[:, 1536:1536 + STEPS]
        blk128 = XT[:, 2048:2048 + STEPS]
        valid = XT[:, 2560:2560 + STEPS]
        pack_f = HF[:, 1024:1024 + STEPS]
        sm = HF[:, 0:12 * 32].rearrange("p (a b) -> p a b", b=32)
        smi = HF[:, 512:512 + 64].bitcast(I32)
        chunk_i = HF[:, 600:604].bitcast(I32)
        chunk_f = HF[:, 604:608]
        start_f, n_f, first_f, last_f, tiles_f, base_f, delta_f, dd_f, thr = (sm[:, r, 0:NB + 1] for r in range(9))
        fields_i = Hn[:, 8:24, :].rearrange("p a b -> p (a b)")[0:TROWS, :].bitcast(I32).rearrange("p (c e k) -> p c e k", c=TCH, k=4)
        fields_f = Lx[:, 0:16, :].rearrange("p a b -> p (a b)")[0:TROWS, :].rearrange("p (c e k) -> p c e k", c=TCH, k=4)
        fields_w = Lx[:, 16:20, :].rearrange("p a b -> p (a b)")[0:TROWS, :].rearrange("p (c e) -> p c e", c=TCH)
        select = arena[0:TROWS, 12000:12000 + TCH * STEPS].rearrange("p (c s) -> p c s", c=TCH)
        dests = [src_s, dl_s, t32_s, t8_s, w_s]

        with nc.Block() as block:
            @block.gpsimd
            def _(pool):
                ch = Chain(pool, pdone)
                pool.memset(zeros[:, :], 0.0).then_inc(consts.sem, 1)
                pool.memset(ones[:, :], 1.0).then_inc(consts.sem, 1)
                pool.memset(red[:, :, :], 0.0).then_inc(consts.sem, 1)
                ch(pool.memset(ident[:, :], 0.0))
                pool.affine_select(out=ident[:, :], in_=ident[:, :], compare_op=ALU.not_equal, fill=1.0,
                                   base=0, pattern=[[-1, P]], channel_multiplier=1).then_inc(consts.sem, 1)
                pool.iota(jrow_i, pattern=[[1, STEPS]], base=0, channel_multiplier=0).then_inc(consts.sem, 1)
                pool.iota(chunk_i, pattern=[[TROWS, TCH]], base=0, channel_multiplier=1).then_inc(consts.sem, 1)
                ch(pool.memset(shift[:, :, :], 0.0))
                pool.affine_select(out=shift[:, 0, :], in_=shift[:, 0, :], compare_op=ALU.not_equal, fill=1.0,
                                   base=HEADS, pattern=[[-1, P]], channel_multiplier=1).then_inc(consts.sem, 1)
                pool.affine_select(out=shift[:, 1, :], in_=shift[:, 1, :], compare_op=ALU.not_equal, fill=1.0,
                                   base=-HEADS, pattern=[[-1, P]], channel_multiplier=1).then_inc(consts.sem, 1)
                ch(pool.memset(head_mask[:, :], 1.0))
                ch(pool.affine_select(out=head_mask[:, :], in_=head_mask[:, :], compare_op=ALU.is_ge, fill=0.0,
                                      base=0, pattern=[[-HS, HEADS]], channel_multiplier=1))
                pool.affine_select(out=head_mask[:, :], in_=head_mask[:, :], compare_op=ALU.is_ge, fill=0.0,
                                   base=HS - 1, pattern=[[HS, HEADS]], channel_multiplier=-1).then_inc(consts.sem, 1)
                ch.close()

            @block.sync
            def _(sp):
                sp.dma_start(dst_i, A["dst"].rearrange("(p c) -> p c", p=CROWS)).then_inc(loaded.sem, 16)
                sp.dma_start(fields_i.rearrange("p c e k -> p c (e k)"),
                             A["edge_ints"].rearrange("(c p) k -> p c k", c=TCH)).then_inc(stored.sem, 16)
                sp.dma_start(fields_w, A["edge_w"].rearrange("(c p) k -> p c k", c=TCH)).then_inc(stored.sem, 16)
                sp.dma_start(Xn[:, 0:NB - 1, :], A["x"][0:(NB - 1) * P, :].rearrange("(b p) f -> p b f", p=P)).then_inc(stored.sem, 16)
                sp.wait_ge(copied.sem, 1)
                sp.dma_start(Xn[0:LAST, NB - 1, :], A["x"][(NB - 1) * P:N, :]).then_inc(stored.sem, 16)
                sp.wait_ge(stored.sem, 64)

            @block.tensor
            def _(pe):
                pe.wait_ge(consts.sem, 9)
                pe.wait_ge(made.sem, 1)
                pe.matmul(misc[:, 0:NB], ones[0:CROWS, :], cnt[0:CROWS, :], start=True, stop=True).then_inc(turned.sem, 1)
                pe.wait_ge(mixed.sem, 1)
                for f in range(5):
                    for c in range(TCH):
                        rows = fields_f[:, c, :, f] if f < 4 else fields_w[:, c, :]
                        mm = pe.matmul(acc[:, f, 0:STEPS], rows, select[:, c, :], start=(c == 0), stop=(c == TCH - 1))
                    mm.then_inc(turned.sem, 1)

            @block.vector
            def _(dve):
                ch = Chain(dve, vdone)
                dve.memset(Xn[:, NB - 1, :], 0.0).then_inc(copied.sem, 1)
                dve.wait_ge(consts.sem, 9)
                ch(dve.tensor_copy(jrow, jrow_i))
                ch(dve.tensor_copy(chunk_f, chunk_i))
                ch(dve.tensor_copy(iota_row[:, :], jrow[:, 0:P]))
                ch(dve.tensor_scalar(thr, jrow[:, 0:NB + 1], float(P), None, ALU.mult))
                dve.wait_ge(loaded.sem, 16)
                ch(dve.tensor_copy(dst_f, dst_i))
                below = cube[0:CROWS, 0:NB * CCOLS].rearrange("p (b c) -> p b c", b=NB)
                ch(dve.tensor_tensor(below, dst_f.unsqueeze(1).to_broadcast([CROWS, NB, CCOLS]),
                                     thr[0:CROWS, 0:NB].unsqueeze(2).to_broadcast([CROWS, NB, CCOLS]), ALU.is_lt))
                dve.tensor_reduce(cnt[0:CROWS, :], below, AX.X, ALU.add).then_inc(made.sem, 1)
                dve.wait_ge(turned.sem, 1)
                ch(dve.tensor_copy(start_f[:, 0:NB], misc[:, 0:NB]))
                ch(dve.memset(start_f[:, NB:NB + 1], float(E)))
                ch(dve.tensor_tensor(n_f[:, 0:NB], start_f[:, 1:NB + 1], start_f[:, 0:NB], ALU.subtract))
                ch(dve.tensor_copy(smi[:, 0:NB], start_f[:, 0:NB]))
                ch(dve.tensor_scalar(n_f[:, 0:NB], n_f[:, 0:NB], 0.0, None, ALU.is_gt))
                ch(dve.tensor_scalar(last_f[:, 0:NB], start_f[:, 1:NB + 1], float(P - 1), None, ALU.add))
                ch(dve.tensor_copy(smi[:, 32:32 + NB], last_f[:, 0:NB]))
                ch(dve.tensor_scalar(smi[:, 0:NB], smi[:, 0:NB], 7, None, ALU.arith_shift_right))
                ch(dve.tensor_scalar(smi[:, 32:32 + NB], smi[:, 32:32 + NB], 7, None, ALU.arith_shift_right))
                ch(dve.tensor_copy(first_f[:, 0:NB], smi[:, 0:NB]))
                ch(dve.tensor_copy(last_f[:, 0:NB], smi[:, 32:32 + NB]))
                ch(dve.tensor_tensor(tiles_f[:, 0:NB], last_f[:, 0:NB], first_f[:, 0:NB], ALU.subtract))
                ch(dve.tensor_tensor(tiles_f[:, 0:NB], tiles_f[:, 0:NB], n_f[:, 0:NB], ALU.mult))
                ch(dve.tensor_tensor_scan(base_f[:, 0:NB], tiles_f[:, 0:NB], zeros[:, 0:NB], 0.0, ALU.add, ALU.add))
                ch(dve.tensor_tensor(base_f[:, 0:NB], base_f[:, 0:NB], tiles_f[:, 0:NB], ALU.subtract))
                ch(dve.tensor_tensor(delta_f[:, 0:NB], first_f[:, 0:NB], base_f[:, 0:NB], ALU.subtract))
                ch(dve.tensor_copy(dd_f[:, 0:1], delta_f[:, 0:1]))
                ch(dve.tensor_tensor(dd_f[:, 1:NB], delta_f[:, 1:NB], delta_f[:, 0:NB - 1], ALU.subtract))
                reached = cube.rearrange("p (j b) -> p j b", b=NB)
                ch(dve.tensor_tensor(reached, jrow.unsqueeze(2).to_broadcast([P, STEPS, NB]),
                                     base_f[:, 0:NB].unsqueeze(1).to_broadcast([P, STEPS, NB]), ALU.is_ge))
                ch(dve.tensor_reduce(blk_f, reached, AX.X, ALU.add))
                ch(dve.tensor_scalar(blk_f, blk_f, 1.0, None, ALU.subtract))
                ch(dve.tensor_tensor(reached, reached, dd_f[:, 0:NB].unsqueeze(1).to_broadcast([P, STEPS, NB]), ALU.mult))
                ch(dve.tensor_reduce(tile_f, reached, AX.X, ALU.add))
                ch(dve.tensor_tensor(tile_f, jrow, tile_f, ALU.add))
                ch(dve.tensor_scalar(valid, tile_f, float(TILES) - 0.5, None, ALU.is_lt))
                ch(dve.tensor_scalar(tile_f, tile_f, float(TILES - 1), None, ALU.min))
                blk_q = blk_f.rearrange("p (n c) -> p n c", c=4)
                pack = pack_f[:, 0:ALL_QUADS]
                ch(dve.scalar_tensor_tensor(pack, blk_q[:, :, 3], 32.0, blk_q[:, :, 2], ALU.mult, ALU.add))
                ch(dve.scalar_tensor_tensor(pack, pack, 32.0, blk_q[:, :, 1], ALU.mult, ALU.add))
                ch(dve.scalar_tensor_tensor(pack, pack, 32.0, blk_q[:, :, 0], ALU.mult, ALU.add))
                ch(dve.tensor_copy(blk4_i[:, :], pack))
                ch(dve.tensor_copy(tile_i[:, :], tile_f))
                ch(dve.tensor_scalar(blk128, blk_f, float(P), None, ALU.mult))
                for c in range(TCH):
                    ch(dve.tensor_scalar(select[:, c, :], tile_f[0:TROWS, :], chunk_f[0:TROWS, c:c + 1], None, ALU.is_equal))
                dve.wait_ge(stored.sem, 64)
                dve.tensor_copy(fields_f.rearrange("p c e k -> p (c e k)"), fields_i.rearrange("p c e k -> p (c e k)")).then_inc(mixed.sem, 1)
                for f in range(5):
                    dve.wait_ge(turned.sem, f + 2)
                    ch(dve.tensor_copy(dests[f][:, :], acc[:, f, 0:STEPS]))
                ch(dve.tensor_scalar(dv_s[:, :], dl_s[:, :], 1.0, None, ALU.add))
                ch(dve.tensor_tensor(dl_s[:, :], dl_s[:, :], blk128, ALU.subtract))
                ch(dve.scalar_tensor_tensor(valid, dl_s[:, :], 0.0, valid, ALU.is_ge, ALU.mult))
                ch(dve.scalar_tensor_tensor(valid, dl_s[:, :], float(P), valid, ALU.is_lt, ALU.mult))
                ch(dve.tensor_tensor(dv_s[:, :], dv_s[:, :], valid, ALU.mult))
                ch(dve.scalar_tensor_tensor(dl_s[:, :], dl_s[:, :], 1.0, valid, ALU.add, ALU.mult))
                ch(dve.tensor_scalar(dl_s[:, :], dl_s[:, :], 1.0, None, ALU.subtract))
                ch(dve.tensor_copy(idx_s[:, :], src_s[:, :]))
                ch.close()
        loaded.base, stored.base, consts.base, made.base, turned.base, mixed.base, copied.base = 16, 64, 9, 1, 6, 1, 1

        def onehots(dve, weight, after=None):
            def body(i, first):
                for q in range(QUADS):
                    n = i * QUADS + q
                    j = i * U + 4 * q
                    if not (first and q < 2):
                        dve.wait_ge(quad_done.sem, quad_done.at(n - 1))
                    o = onehot[:, 4 * (q % 2):4 * (q % 2) + 4, :]
                    is_dst = dve.tensor_tensor(o, iota_row[:, :].unsqueeze(1).to_broadcast([P, 4, P]),
                                               dl_s[:, ds(j, 4)].unsqueeze(2).to_broadcast([P, 4, P]), ALU.is_equal)
                    if weight is not None:
                        is_dst.then_inc(compared.sem, 1)
                        dve.wait_ge(compared.sem, compared.at(n + 1))
                        is_dst = dve.tensor_tensor(o, o, weight[:, ds(j, 4)].unsqueeze(2).to_broadcast([P, 4, P]), ALU.mult)
                    is_dst.then_inc(onehot_ready.sem, 1)
                    if after is not None:
                        after(i, q, first)
            trips(dve, body)
            if weight is not None:
                compared.base += ALL_QUADS

        def gathers(pool, tab, width, free=None):
            def body(i, first):
                for h in range(2):
                    if not first:
                        if free is None:
                            pool.wait_ge(quad_done.sem, quad_done.at(i * QUADS - QUADS + 2 * h + 2))
                        else:
                            free(pool, i, h)
                    pool.tensor_copy(gidx[:, h * HALF:(h + 1) * HALF],
                                     idx_s[:, ds(i * U + h * HALF, HALF)]).then_inc(idx_ready.sem, 1)
                    pool.wait_ge(idx_ready.sem, idx_ready.at(2 * i + h + 1))
                    pool.sem_inc(go.sem, 1)
                    for u in range(h * HALF, (h + 1) * HALF):
                        pool.indirect_dma_start(G[:, u, 0:width], None, tab,
                                                bass.IndirectOffsetOnAxis(ap=gidx[:, u:u + 1], axis=0)).then_inc(gathered[u].sem, 16)
            trips(pool, body)

        def quad_blocks(pe, n):
            four = nc.values_load(blk4_i[0:1, ds(n, 1)], engines=(pe.engine,), min_val=0, max_val=32 ** 4 - 1,
                                  skip_runtime_bounds_check_because="block numbers by construction")
            return [nc.snap((four >> (5 * c)) & 31, engines=(pe.engine,), min_val=0, max_val=NB - 1) for c in range(4)]

        def quad_pass_over():
            onehot_ready.base += ALL_QUADS
            quad_done.base += ALL_QUADS

        def gather_pass_over():
            quad_pass_over()
            idx_ready.base += 2 * TRIPS
            go.base += 2 * TRIPS
            for s in gathered:
                s.base += 16 * TRIPS

        def fill_rows(pe, row):
            for k in range(BANKS):
                a, b, blocks = span(k)
                if row is None:
                    pe.matmul(accf[:, a:b], ident[:, :], zeros[:, 0:b - a], start=True, stop=False, skip_group_check=True)
                else:
                    pe.matmul(accf[:, a:b].rearrange("p (b f) -> p b f", f=H), ones[0:1, :],
                              row.unsqueeze(1).to_broadcast([1, len(blocks), H]), start=True, stop=False, skip_group_check=True)

        def turn_nodes(pe, source, need):
            for k in range(BANKS):
                need(k)
                for b in span(k)[2]:
                    mm = pe.transpose(accf[:, b * P:(b + 1) * P],
                                      source[:, b, :] if len(source.shape) == 3 else source[:, b * P:(b + 1) * P], ident[:, :])
                mm.then_inc(turned.sem, 1)

        def normalise(ch, dve, src, dst):
            mean, var = red[:, 0, :], red[:, 1, :]

            def over(v):
                return v.unsqueeze(2).to_broadcast([P, NB, H])
            ch(dve.tensor_reduce(mean, src, AX.X, ALU.add))
            ch(dve.tensor_scalar(mean, mean, 1.0 / H, None, ALU.mult))
            dve.tensor_tensor(dst, src, over(mean), ALU.subtract).then_inc(centred.sem, 1)
            dve.wait_ge(squared.sem, squared.at(1))
            ch(dve.tensor_reduce(var, arena[:, 0:NP].rearrange("p (b f) -> p b f", f=H), AX.X, ALU.add))
            dve.tensor_scalar(var, var, 1.0 / H, EPS, ALU.mult, ALU.add).then_inc(varied.sem, 1)
            dve.wait_ge(rooted.sem, rooted.at(1))
            ch(dve.reciprocal(var, var))
            return dve.tensor_tensor(dst, dst, over(var), ALU.mult)

        def normalise_act(act, dst):
            act.wait_ge(centred.sem, centred.at(1))
            act.activation(arena[:, 0:NP], dst.rearrange("p b f -> p (b f)"), ACT.Square).then_inc(squared.sem, 1)
            act.wait_ge(varied.sem, varied.at(1))
            act.activation(red[:, 1, :], red[:, 1, :], ACT.Sqrt).then_inc(rooted.sem, 1)

        def normalised():
            for s in (centred, squared, varied, rooted):
                s.base += 1

        def residual_norm_phase(prepare=None):
            with nc.Block() as block:
                @block.scalar
                def _(act):
                    normalise_act(act, Xn[:, :, :])

                @block.vector
                def _(dve):
                    ch = Chain(dve, vdone)
                    if prepare is not None:
                        prepare(ch, dve)
                    ch(normalise(ch, dve, Xn[:, :, :], Xn[:, :, :]))
                    ch.close()
            normalised()

        def load_phase_part(sp, loads):
            for dst_ap, src_ap in loads:
                sp.dma_start(dst_ap, src_ap).then_inc(loaded.sem, 16)

        def table_phase(src, scale=1.0, bias=0.0, loads=(), w=None, row=None, index=None):
            with nc.Block() as block:
                @block.sync
                def _(sp):
                    load_phase_part(sp, loads)
                    if w is not None:
                        sp.wait_ge(copied.sem, copied.at(BANKS))
                        sp.dma_start(table.rearrange("(b p) f -> p b f", p=P),
                                     HF[:, :].rearrange("p (b f) -> p b f", f=H)).then_inc(stored.sem, 16)
                        sp.wait_ge(stored.sem, stored.at(16))

                @block.tensor
                def _(pe):
                    turn_nodes(pe, src[:, :, :], lambda k: None)
                    if w is not None:
                        pe.wait_ge(loaded.sem, loaded.at(16 * len(loads)))
                        for k in range(BANKS):
                            a, b, blocks = span(k)
                            pe.wait_ge(evac.sem, evac.at(k + 1))
                            if row is not None:
                                pe.matmul(accf[:, a:b].rearrange("p (b f) -> p b f", f=H), ones[0:1, :],
                                          row.unsqueeze(1).to_broadcast([1, len(blocks), H]), start=True, stop=False, skip_group_check=True)
                            for b in blocks:
                                mm = pe.matmul(accf[:, b * P:(b + 1) * P], XT[:, b * P:(b + 1) * P], w,
                                               start=(row is None), stop=True, skip_group_check=True)
                            mm.then_inc(made.sem, 1)

                @block.scalar
                def _(act):
                    act.wait_ge(loaded.sem, loaded.at(16 * len(loads)))
                    for k in range(BANKS):
                        a, b, _ = span(k)
                        act.wait_ge(turned.sem, turned.at(k + 1))
                        act.activation(XT[:, a:b], accf[:, a:b], ACT.Identity, scale=scale, bias=bias).then_inc(evac.sem, 1)

                @block.vector
                def _(dve):
                    ch = Chain(dve, vdone)
                    if index is not None:
                        ch(dve.scalar_tensor_tensor(w1_f, src_s[:, :], float(index[1]), index[0][:, :], ALU.mult, ALU.add))
                        ch(dve.tensor_copy(idx_s[:, :], w1_f))
                    if w is not None:
                        for k in range(BANKS):
                            a, b, _ = span(k)
                            dve.wait_ge(made.sem, made.at(k + 1))
                            dve.tensor_copy(HF[:, a:b], accf[:, a:b]).then_inc(copied.sem, 1)
                    ch.close()
            loaded.base += 16 * len(loads)
            turned.base += BANKS
            evac.base += BANKS
            if w is not None:
                made.base += BANKS
                copied.base += BANKS
                stored.base += 16
        w1_f = arena[:, 24000:24000 + STEPS]

        def aggregate_phase(tab, weight, root=None, row=None, sums=None, edges=None):
            with nc.Block() as block:
                @block.gpsimd
                def _(pool):
                    gathers(pool, tab, H)

                @block.vector
                def _(dve):
                    onehots(dve, weight, edges.join if edges else None)
                    if edges:
                        edges.join_last(dve)

                @block.tensor
                def _(pe):
                    fill_rows(pe, row)
                    if root is not None:
                        for b in range(NB):
                            pe.matmul(accf[:, b * P:(b + 1) * P], XT[:, b * P:(b + 1) * P], root, start=False, stop=False,
                                      skip_group_check=True)
                    if sums:
                        pe.matmul(misc[:, 0:NB], ident[:, :], zeros[:, 0:NB], start=True, stop=False, skip_group_check=True)
                    if edges:
                        pe.wait_ge(loaded.sem, loaded.at(16 * edges.LOADS))

                    def body(i, first):
                        for u in range(U):
                            if u % 4 == 0:
                                blocks = quad_blocks(pe, i * QUADS + u // 4)
                                if edges:
                                    edges.hidden(pe, i, u // 4, first)
                                pe.wait_ge(onehot_ready.sem, onehot_ready.at(i * QUADS + u // 4 + 1))
                            if u % 4 == 2 and edges:
                                edges.output(pe, i, u // 4, first)
                            pe.wait_ge(gathered[u].sem, gathered[u].at(16 * (i + 1)))
                            o, b = onehot[:, u % HALF, :], blocks[u % 4]
                            if sums:
                                pe.matmul(misc[:, ds(b, 1)], o, ones[:, 0:1], start=False, stop=False, skip_group_check=True)
                            mm = pe.matmul(accf[:, ds(b * P, P)], o, G[:, u, 0:H],
                                           start=False, stop=False, skip_group_check=True)
                            if u % 4 == 3:
                                mm.then_inc(quad_done.sem, 1)
                    trips(pe, body)
                    if edges:
                        edges.products_last(pe)

                if edges:
                    @block.sync
                    def _(sp):
                        edges.transfers(sp)

                    @block.scalar
                    def _(act):
                        edges.activations(act)
            gather_pass_over()
            if edges:
                edges.over()

        def col(ap):
            return ap.rearrange("(p a) -> p a", a=1)

        def one_row(ap):
            return ap.rearrange("(a f) -> a f", a=1)

        def over_nodes(ap):
            return ap.partition_broadcast(P)

        def full(v):
            return v.unsqueeze(2).to_broadcast([P, NB, H])

        class EdgeShare:
            PAIR = 2 * P
            LOADS = 7
            half_a, half_b = misc[:, 0:PAIR], misc[:, PAIR:2 * PAIR]
            attrT = arena[0:EDIM, 0:4 * PAIR].rearrange("p (r e) -> p r e", r=4)
            ts_bc = arena[:, 1024:1024 + 4 * PAIR].rearrange("p (r e) -> p r e", r=4)
            hid = arena[:, 2048:2048 + 2 * PAIR].rearrange("p (r e) -> p r e", r=2)
            tw = arena[:, 2560:2560 + 2 * PAIR].rearrange("p (r e) -> p r e", r=2)
            ef = arena[:, 3072:3072 + 2 * PAIR].rearrange("p (r e) -> p r e", r=2)
            zout = arena[:, 3584:3584 + 2 * PAIR].rearrange("p (r e) -> p r e", r=2)
            We2, Wn1b = arena[:, 4096:4224], arena[:, 4224:4352]
            we1 = arena[0:EDIM, 4352:4480]
            be1, be2, wt_c, bt_c = (vecs[:, 8 + r:9 + r] for r in range(4))

            def __init__(self, part):
                self.pair0 = part * ALL_QUADS

            def load(self, sp, i, q, first):
                n = i * QUADS + q
                edge = (i * QUADS + (self.pair0 + q)) * self.PAIR
                if not first:
                    sp.wait_ge(made.sem, made.at(n - 3))
                sp.dma_start(self.attrT[:, q, :], A["edge_attr_T"][:, ds(edge, self.PAIR)]).then_inc(ring_in[q].sem, 16)
                if not first:
                    sp.wait_ge(mixed.sem, mixed.at(n - 3))
                sp.dma_start(self.ts_bc[:, q, :], A["edge_times"][ds(edge, self.PAIR)].partition_broadcast(P)).then_inc(ring_in[4 + q].sem, 16)

            def store(self, sp, i, q):
                sp.wait_ge(centred.sem, centred.at(i * QUADS + q + 1))
                sp.dma_start(edge_part[ds((i * QUADS + (self.pair0 + q)) * 2, 2), :, :].rearrange("t e f -> e t f"),
                             self.zout[:, q % 2, :].rearrange("p (t f) -> p t f", t=2)).then_inc(edge_out[q % 2].sem, 16)

            def transfers(self, sp):
                for dst_ap, src_ap in ((self.we1, A["L1_gnn_We1"]), (self.We2, A["L1_gnn_We2"]), (self.Wn1b, A["L1_gnn_Wn1"][H:2 * H, :]),
                                       (self.be1, col(A["L1_gnn_be1"])), (self.be2, col(A["L1_gnn_be2"])),
                                       (self.wt_c, A["L1_gnn_Wt"].rearrange("a f -> f a")), (self.bt_c, col(A["L1_gnn_bt"]))):
                    sp.dma_start(dst_ap, src_ap).then_inc(loaded.sem, 16)

                def body(i, first):
                    for q in range(QUADS):
                        self.load(sp, i, q, first)
                        if q == 3:
                            self.store(sp, i, 0)
                        elif not first:
                            self.store(sp, i - 1, q + 1)
                trips(sp, body)
                for q in range(1, QUADS):
                    self.store(sp, TRIPS - 1, q)
                for r in range(2):
                    sp.wait_ge(edge_out[r].sem, edge_out[r].at(16 * (ALL_QUADS // 2)))

            def second(self, pe, m, r):
                pe.wait_ge(evac.sem, evac.at(m + 1))
                pe.matmul(self.half_b, self.We2, self.hid[:, r, :], start=True, stop=True, skip_group_check=True).then_inc(turned.sem, 1)

            def third(self, pe, m, r):
                pe.wait_ge(copied.sem, copied.at(m + 1))
                for c in range(2):
                    mm = pe.matmul(self.half_a[:, c * P:(c + 1) * P], self.ef[:, r, c * P:(c + 1) * P], self.Wn1b, start=True, stop=True,
                                   skip_group_check=True)
                mm.then_inc(rooted.sem, 1)

            def hidden(self, pe, i, q, first):
                n = i * QUADS + q
                if not (first and q < 3):
                    pe.wait_ge(centred.sem, centred.at(n - 2))
                if not (first and q < 1):
                    if q == 2 and first:
                        pe.wait_ge(squared.sem, squared.at(n - 1))
                    elif q == 1 and first:
                        pe.wait_ge(evac.sem, evac.at(n))
                    self.second(pe, n - 1, (q + 1) % 2)
                pe.wait_ge(ring_in[q].sem, ring_in[q].at(16 * (i + 1)))
                pe.matmul(self.half_a, self.we1, self.attrT[:, q, :], start=True, stop=True, skip_group_check=True).then_inc(made.sem, 1)

            def output(self, pe, i, q, first):
                n = i * QUADS + q
                if not (first and q < 2):
                    pe.wait_ge(squared.sem, squared.at(n))
                    self.third(pe, n - 2, q % 2)

            def products_last(self, pe):
                m = ALL_QUADS - 1
                pe.wait_ge(centred.sem, centred.at(m - 1))
                self.second(pe, m, m % 2)
                pe.wait_ge(squared.sem, squared.at(m + 1))
                self.third(pe, m - 1, (m - 1) % 2)
                pe.wait_ge(centred.sem, centred.at(m))
                self.third(pe, m, m % 2)

            def take_b(self, act, m, r, used):
                if used:
                    act.wait_ge(rooted.sem, rooted.at(m - 1))
                act.activation(self.ef[:, r, :], self.half_b, ACT.Identity, bias=self.be2).then_inc(squared.sem, 1)

            def take_output(self, act, m, r, stores):
                act.wait_ge(rooted.sem, rooted.at(m + 1))
                if stores is not None:
                    act.wait_ge(edge_out[r].sem, edge_out[r].at(stores))
                act.activation(self.zout[:, r, :], self.half_a, ACT.Copy).then_inc(centred.sem, 1)

            def activations(self, act):
                act.wait_ge(loaded.sem, loaded.at(16 * self.LOADS))

                def body(i, first):
                    for q in range(QUADS):
                        n = i * QUADS + q
                        r = q % 2
                        act.wait_ge(made.sem, made.at(n + 1))
                        act.activation(self.hid[:, r, :], self.half_a, ACT.Relu, bias=self.be1).then_inc(evac.sem, 1)
                        if not (first and q < 1):
                            self.take_b(act, n - 1, (q + 1) % 2, not (first and q < 3))
                        act.wait_ge(ring_in[4 + q].sem, ring_in[4 + q].at(16 * (i + 1)))
                        if not (first and q < 2):
                            act.wait_ge(copied.sem, copied.at(n - 1))
                        act.activation(self.tw[:, r, :], self.ts_bc[:, q, :], ACT.Sigmoid, scale=self.wt_c, bias=self.bt_c).then_inc(mixed.sem, 1)
                        if not (first and q < 2):
                            self.take_output(act, n - 2, r, None if first and q < 4 else 32 * i + 16 * ((q - 2) // 2))
                trips(act, body)
                m = ALL_QUADS - 1
                act.wait_ge(turned.sem, turned.at(m + 1))
                self.take_b(act, m, m % 2, True)
                for m in range(ALL_QUADS - 2, ALL_QUADS):
                    self.take_output(act, m, m % 2, 16 * (m // 2))

            def mix(self, dve, m, r):
                dve.wait_ge(squared.sem, squared.at(m + 1))
                dve.wait_ge(mixed.sem, mixed.at(m + 1))
                dve.tensor_tensor(self.ef[:, r, :], self.ef[:, r, :], self.tw[:, r, :], ALU.mult).then_inc(copied.sem, 1)

            def join(self, i, q, first):
                if not (first and q < 1):
                    self.mix(nc.vector, i * QUADS + q - 1, (q + 1) % 2)

            def join_last(self, dve):
                self.mix(dve, ALL_QUADS - 1, (ALL_QUADS - 1) % 2)

            def over(self):
                loaded.base += 16 * self.LOADS
                for s in (made, evac, turned, copied, rooted, centred, squared, mixed):
                    s.base += ALL_QUADS
                for s in ring_in[0:8]:
                    s.base += 16 * TRIPS
                for s in edge_out:
                    s.base += 16 * (ALL_QUADS // 2)

        loads = [(wts[:, 0:3, :], A["L0_neigh"].rearrange("l f o -> f l o")),
                 (wts[:, 3:6, :], A["L0_root"].rearrange("l f o -> f l o")),
                 (bc[:, 0, :], over_nodes(A["L0_gnn_ln_w"][L0 - 1])), (bc[:, 1, :], over_nodes(A["L0_gnn_ln_b"][L0 - 1]))]
        for l in range(L0):
            loads += [(vecs[:, l:l + 1], col(A["L0_gnn_ln_w"][l])), (vecs[:, 3 + l:4 + l], col(A["L0_gnn_ln_b"][l]))]

        for l in range(L0):
            if l == 0:
                table_phase(Xn, loads=loads, w=wts[:, 0, :])
            else:
                table_phase(Hn, scale=vecs[:, l - 1:l], bias=vecs[:, 2 + l:3 + l], w=wts[:, l, :])
            aggregate_phase(table, w_s, sums=(l == 0), edges=EdgeShare(l - 1) if l else None)
            with nc.Block() as block:
                @block.sync
                def _(sp):
                    sp.dma_start(brow[:, :], one_row(A["L0_gnn_lin_root_b"][l])).then_inc(loaded.sem, 16)

                @block.scalar
                def _(act):
                    act.wait_ge(mixed.sem, mixed.at(1))
                    act.activation(Hn[:, :, :].rearrange("p b f -> p (b f)"), HF[:, :], ACT.Relu).then_inc(evac.sem, 1)
                    normalise_act(act, Hn[:, :, :])

                @block.tensor
                def _(pe):
                    pe.wait_ge(loaded.sem, loaded.at(16))
                    pe.wait_ge(copied.sem, copied.at(1))
                    fill_rows(pe, brow[:, :])
                    for b in range(NB):
                        mm = pe.matmul(accf[:, b * P:(b + 1) * P], XT[:, b * P:(b + 1) * P], wts[:, 3 + l, :], start=False,
                                       stop=True, skip_group_check=True)
                    mm.then_inc(made.sem, 1)

                @block.vector
                def _(dve):
                    ch = Chain(dve, vdone)
                    if l == 0:
                        ch(dve.tensor_scalar(rsum[:, :], misc[:, 0:NB], 1.0, None, ALU.max))
                        ch(dve.reciprocal(rsum[:, :], rsum[:, :]))
                    hf = HF[:, :].rearrange("p (b f) -> p b f", f=H)
                    dve.tensor_tensor(hf, acc_nodes, full(rsum[:, :]), ALU.mult).then_inc(copied.sem, 1)
                    dve.wait_ge(copied.sem, copied.at(1))
                    dve.wait_ge(made.sem, made.at(1))
                    dve.tensor_tensor(hf, hf, acc_nodes, ALU.add).then_inc(mixed.sem, 1)
                    dve.wait_ge(evac.sem, evac.at(1))
                    ch(normalise(ch, dve, Hn[:, :, :], Hn[:, :, :]))
                    if l == L0 - 1:
                        ch(dve.tensor_tensor(Hn[:, :, :], Hn[:, :, :], bc[:, 0:1, :].to_broadcast([P, NB, H]), ALU.mult))
                        ch(dve.tensor_tensor(Hn[:, :, :], Hn[:, :, :], bc[:, 1:2, :].to_broadcast([P, NB, H]), ALU.add))
                        ch(dve.tensor_tensor(Xn[:, :, :], Xn[:, :, :], Hn[:, :, :], ALU.add))
                    ch.close()
            loaded.base += 16
            for s in (evac, made, mixed, copied):
                s.base += 1
            normalised()
        residual_norm_phase()

        if STAGE >= 2:
            Wn1a, Wn2 = wts[:, 0, :], wts[:, 1, :]
            loads = [(Wn1a, A["L1_gnn_Wn1"][0:H, :]), (Wn2, A["L1_gnn_Wn2"]),
                     (brow[:, :], one_row(A["L1_gnn_bn1"])), (bc[:, 0, :], over_nodes(A["L1_gnn_bn2"]))]

            table_phase(Xn, loads=loads, w=Wn1a, row=brow[:, :])
            share = arena[:, 0:HALF * H].rearrange("p (r f) -> p r f", r=HALF)
            hidden = arena[:, 2048:2048 + HALF * H].rearrange("p (r f) -> p r f", r=HALF)
            relu_h = arena[:, 4096:4096 + HALF * H].rearrange("p (r f) -> p r f", r=HALF)
            with nc.Block() as block:
                @block.gpsimd
                def _(pool):
                    gathers(pool, table, H)

                @block.sync
                def _(sp):
                    def body(i, first):
                        for u in range(U):
                            j = i * U + u
                            t = nc.values_load(tile_i[0:1, ds(j, 1)], engines=(sp.engine,), min_val=0, max_val=TILES - 1,
                                               skip_runtime_bounds_check_because="a tile number by construction")
                            if u % 4 == 0 and not (first and u < HALF):
                                sp.wait_ge(mixed.sem, mixed.at(i * QUADS + u // 4 - 1))
                            sp.dma_start(share[:, u % HALF, :], edge_part[ds(t, 1), :, :].rearrange("a e f -> (a e) f")).then_inc(ring_in[u % HALF].sem, 16)
                    trips(sp, body)

                @block.vector
                def _(dve):
                    def join(i, q, first):
                        n = i * QUADS + q
                        r = 4 * (q % 2)
                        for u in range(4 * q, 4 * q + 4):
                            dve.wait_ge(gathered[u].sem, gathered[u].at(16 * (i + 1)))
                            dve.wait_ge(ring_in[u % HALF].sem, ring_in[u % HALF].at(32 * i + 16 * (u // HALF) + 16))
                        if not (first and q < 2):
                            dve.wait_ge(evac.sem, evac.at(n - 1))
                        dve.tensor_tensor(hidden[:, r:r + 4, :], share[:, r:r + 4, :], G[:, 4 * q:4 * q + 4, 0:H], ALU.add).then_inc(mixed.sem, 1)
                    onehots(dve, None, join)

                @block.scalar
                def _(act):
                    def body(i, first):
                        for q in range(QUADS):
                            n = i * QUADS + q
                            r = 4 * (q % 2)
                            act.wait_ge(mixed.sem, mixed.at(n + 1))
                            if not (first and q < 2):
                                act.wait_ge(quad_done.sem, quad_done.at(n - 1))
                            act.activation(relu_h[:, r:r + 4, :], hidden[:, r:r + 4, :], ACT.Relu).then_inc(evac.sem, 1)
                    trips(act, body)

                @block.tensor
                def _(pe):
                    fill_rows(pe, None)
                    pe.matmul(misc[:, 0:NB], ident[:, :], zeros[:, 0:NB], start=True, stop=False, skip_group_check=True)

                    def body(i, first):
                        for u in range(U):
                            if u % 4 == 0:
                                blocks = quad_blocks(pe, i * QUADS + u // 4)
                                pe.wait_ge(onehot_ready.sem, onehot_ready.at(i * QUADS + u // 4 + 1))
                                pe.wait_ge(evac.sem, evac.at(i * QUADS + u // 4 + 1))
                            o, b = onehot[:, u % HALF, :], blocks[u % 4]
                            pe.matmul(misc[:, ds(b, 1)], o, ones[:, 0:1], start=False, stop=False, skip_group_check=True)
                            mm = pe.matmul(accf[:, ds(b * P, P)], relu_h[:, u % HALF, :], o,
                                           start=False, stop=False, skip_group_check=True)
                            if u % 4 == 3:
                                mm.then_inc(quad_done.sem, 1)
                    trips(pe, body)
            gather_pass_over()
            mixed.base += ALL_QUADS
            evac.base += ALL_QUADS
            for s in ring_in:
                s.base += 32 * TRIPS

            with nc.Block() as block:
                @block.scalar
                def _(act):
                    for k in range(BANKS):
                        a, b, _ = span(k)
                        act.activation(HF[:, a:b], accf[:, a:b], ACT.Copy).then_inc(evac.sem, 1)

                @block.tensor
                def _(pe):
                    for k in range(BANKS):
                        pe.wait_ge(evac.sem, evac.at(k + 1))
                        for b in span(k)[2]:
                            mm = pe.matmul(accf[:, b * P:(b + 1) * P], HF[:, b * P:(b + 1) * P], Wn2, start=True, stop=True)
                        mm.then_inc(made.sem, 1)

                @block.vector
                def _(dve):
                    ch = Chain(dve, vdone)
                    ch(dve.tensor_copy(deg[:, :], misc[:, 0:NB]))
                    ch(dve.tensor_tensor(Hn[:, :, :], full(deg[:, :]), bc[:, 0:1, :].to_broadcast([P, NB, H]), ALU.mult))
                    ch(dve.scalar_tensor_tensor(Hn[:, :, :].rearrange("p b f -> p (b f)"), Xn[:, :, :].rearrange("p b f -> p (b f)"), 2.0,
                                                Hn[:, :, :].rearrange("p b f -> p (b f)"), ALU.mult, ALU.add))
                    dve.wait_ge(made.sem, made.at(BANKS))
                    ch(dve.tensor_tensor(Xn[:, :, :], Hn[:, :, :], acc_nodes, ALU.add))
                    ch.close()
            evac.base += BANKS
            made.base += BANKS
            residual_norm_phase()

        if STAGE >= 3:
            relw = arena[:, 0:R8 * H]
            RING = 4
            rows8 = arena[:, 2048:2048 + RING * R8 * H].rearrange("p (r c) -> p r c", r=RING)
            Wl = wts[:, 0, :]

            def relation_table_phase(src, W, Wl_dram, b_dram):
                table_phase(src, loads=[(relw, W.rearrange("i r o -> i (r o)")), (Wl, Wl_dram), (brow[:, :], one_row(b_dram))],
                            index=(t8_s, R8))
                with nc.Block() as block:
                    @block.tensor
                    def _(pe):
                        for b in range(NB):
                            for c in range(2):
                                n = 2 * b + c
                                if n >= 8:
                                    pe.wait_ge((evac if c == 0 else copied).sem, (evac if c == 0 else copied).at(b - 3))
                                pe.matmul(ps[:, n % 8, :], XT[:, b * P:(b + 1) * P], relw[:, c * 512:(c + 1) * 512],
                                          start=True, stop=True).then_inc(made.sem, 1)

                    @block.scalar
                    def _(act):
                        for b in range(NB):
                            act.wait_ge(made.sem, made.at(2 * b + 1))
                            if b >= RING:
                                act.wait_ge(ring_out[b % RING].sem, ring_out[b % RING].at(16 * (b // RING)))
                            act.activation(rows8[:, b % RING, 0:512], ps[:, 2 * b % 8, :], ACT.Copy).then_inc(evac.sem, 1)

                    @block.vector
                    def _(dve):
                        for b in range(NB):
                            dve.wait_ge(made.sem, made.at(2 * b + 2))
                            if b >= RING:
                                dve.wait_ge(ring_out[b % RING].sem, ring_out[b % RING].at(16 * (b // RING)))
                            dve.tensor_copy(rows8[:, b % RING, 512:1024], ps[:, (2 * b + 1) % 8, :]).then_inc(copied.sem, 1)

                    @block.sync
                    def _(sp):
                        for b in range(NB):
                            sp.wait_ge(evac.sem, evac.at(b + 1))
                            sp.wait_ge(copied.sem, copied.at(b + 1))
                            sp.dma_start(table8[b * P * R8:(b + 1) * P * R8, :].rearrange("(n r) f -> n (r f)", r=R8),
                                         rows8[:, b % RING, :]).then_inc(ring_out[b % RING].sem, 16)
                        for r in range(RING):
                            sp.wait_ge(ring_out[r].sem, ring_out[r].at(16 * len(range(r, NB, RING))))
                made.base += 2 * NB
                evac.base += NB
                copied.base += NB
                for r in range(RING):
                    ring_out[r].base += 16 * len(range(r, NB, RING))

            relation_table_phase(Xn, A["L2_W1"], A["L2_gnn_Wl1"], A["L2_gnn_b1"])
            aggregate_phase(table8, None, root=Wl, row=brow[:, :])
            with nc.Block() as block:
                @block.scalar
                def _(act):
                    act.activation(Hn[:, :, :].rearrange("p b f -> p (b f)"), accf[:, 0:NP], ACT.Relu)
            relation_table_phase(Hn, A["L2_W2"], A["L2_gnn_Wl2"], A["L2_gnn_b2"])
            aggregate_phase(table8, None, root=Wl, row=brow[:, :])
            residual_norm_phase(lambda ch, dve: ch(dve.tensor_tensor(Xn[:, :, :], Xn[:, :, :], acc_nodes, ALU.add)))

        if STAGE >= 4:
            LINKS = GSTEPS * P
            Qn = arena[:, 0:NP].rearrange("p (b f) -> p b f", f=H)
            masked = arena[:, NP:3 * NP].rearrange("p (r n) -> p r n", r=2)
            types_bc = arena[:, 3 * NP:4 * NP].bitcast(I32)
            type_w = arena[:, 4 * NP:4 * NP + 2 * H].rearrange("p (r o) -> p r o", r=2)
            block_k = arena[:, 3200:7296].rearrange("p (t c) -> p t c", t=T32)
            block_v = arena[:, 7296:11392].rearrange("p (t c) -> p t c", t=T32)
            raw = arena[:, 11392:12416].rearrange("p (a t o) -> p a t o", a=2, t=T32)
            pri = arena[:, 12416:12448]
            rows32 = arena[:, 12480:12480 + 4 * 2048].rearrange("p (q t c) -> p q t c", q=4, t=8)
            node_cols = G[:, 0, :].rearrange("p (a n) -> p a n", a=2)
            score = arena[:, 3200:3200 + STEPS * HEADS].rearrange("p (s h) -> p s h", h=HEADS)
            onehotT = arena[:, 6528:6528 + 8 * P].rearrange("p (r e) -> p r e", r=2)
            prod = arena[:, 7552:7552 + 8 * H].rearrange("p (r s f) -> p r s f", r=2, s=4)
            scan_in = arena[:, 7600:7600 + LINKS]
            ahead = arena[:, 10928:10928 + LINKS]
            behind = arena[:, 14256:14256 + LINKS]
            rows = arena[0:1, 17600:17600 + 8 * P].rearrange("p (r x) -> p r x", r=8)
            carry = arena[:, 18700:18702]
            gsum = arena[:, 18704:18706]
            rs8 = arena[:, 18720:18720 + NB * HEADS]
            alpha = arena[:, 18940:18940 + NB]
            types_n = arena[:, 18980:18980 + NB].bitcast(I32)
            skip_bc = arena[:, 19010:19010 + NT]
            eq_types = arena[:, 19040:19040 + NB * NT].rearrange("p (b t) -> p b t", t=NT)
            grow = arena[0:1, 20700:20700 + 2 * P].rearrange("p (r x) -> p r x", r=2)
            link = arena[:, 24500 - LINKS - 1:24500]
            vals = arena[:, 7600:7600 + U * H].rearrange("p (r f) -> p r f", r=U)
            msgs = arena[:, 9648:9648 + HALF * H].rearrange("p (r f) -> p r f", r=HALF)
            keep = w_s
            g_bc, b_bc = bc[:, 0, :], bc[:, 1, :]
            ff_w = wts[:, 4, :]

            def typed_phase(W, src, dst, node_major):
                with nc.Block() as block:
                    @block.sync
                    def _(sp):
                        sp.dma_start(types_bc, A["node_type"].partition_broadcast(P)).then_inc(loaded.sem, 16)

                        def body(i, first):
                            for r in range(2):
                                t = 2 * i + r
                                if not first:
                                    sp.wait_ge(made.sem, made.at(t - 1))
                                sp.dma_start(type_w[:, r, :], W[ds(t, 1), :, :].rearrange("a f o -> (a f) o")).then_inc(ring_in[r].sem, 16)
                        trips(sp, body, NT // 2)

                    @block.vector
                    def _(dve):
                        dve.wait_ge(loaded.sem, loaded.at(16))

                        def body(i, first):
                            for r in range(2):
                                t = 2 * i + r
                                if not first:
                                    dve.wait_ge(made.sem, made.at(t - 1))
                                dve.scalar_tensor_tensor(masked[:, r, :], types_bc, iota_row[:, ds(t, 1)], src,
                                                         ALU.is_equal, ALU.mult).then_inc(mixed.sem, 1)
                        trips(dve, body, NT // 2)

                    @block.tensor
                    def _(pe):
                        fill_rows(pe, None)

                        def body(i, first):
                            for r in range(2):
                                t = 2 * i + r
                                pe.wait_ge(ring_in[r].sem, ring_in[r].at(16 * (i + 1)))
                                pe.wait_ge(mixed.sem, mixed.at(t + 1))
                                if node_major:
                                    for b in range(NB):
                                        mm = pe.matmul(accf[:, b * P:(b + 1) * P], masked[:, r, b * P:(b + 1) * P], type_w[:, r, :],
                                                       start=False, stop=False, skip_group_check=True)
                                else:
                                    for k in range(BANKS):
                                        a, b, _ = span(k)
                                        mm = pe.matmul(accf[:, a:b], type_w[:, r, :], masked[:, r, a:b],
                                                       start=False, stop=False, skip_group_check=True)
                                mm.then_inc(made.sem, 1)
                        trips(pe, body, NT // 2)

                    if dst is not None:
                        @block.scalar
                        def _(act):
                            act.wait_ge(made.sem, made.at(NT))
                            act.activation(dst, accf[:, 0:NP], ACT.Copy)
                loaded.base += 16
                made.base += NT
                mixed.base += NT
                for r in range(2):
                    ring_in[r].base += 16 * (NT // 2)

            def key_value_table_phase(l):
                kT, vT = HF[:, :], Hn[:, :, :].rearrange("p b f -> p (b f)")
                with nc.Block() as block:
                    @block.sync
                    def _(sp):
                        sp.dma_start(raw[:, 0, :, :].rearrange("p t o -> p (t o)"), A["L3_Watt"][l]).then_inc(loaded.sem, 16)
                        sp.dma_start(raw[:, 1, :, :].rearrange("p t o -> p (t o)"), A["L3_Wmsg"][l]).then_inc(loaded.sem, 16)
                        for h in range(HEADS):
                            sp.dma_start(pri[h * HS:(h + 1) * HS, :], A["L3_gnn_pri"][l, h].partition_broadcast(HS)).then_inc(loaded.sem, 16)

                        def body(i, first):
                            for q in range(4):
                                sp.wait_ge(copied.sem, copied.at(4 * i + q + 1))
                                sp.dma_start(table32.rearrange("(n t) f -> n t f", t=T32)[ds(i * P, P), q * 8:(q + 1) * 8, :],
                                             rows32[:, q, :, :]).then_inc(ring_out[q].sem, 16)
                        trips(sp, body, NB)
                        for q in range(4):
                            sp.wait_ge(ring_out[q].sem, ring_out[q].at(16 * NB))

                    @block.gpsimd
                    def _(pool):
                        def body(i, first):
                            if not first:
                                pool.wait_ge(made.sem, made.at(4 * i))
                            pool.tensor_copy(node_cols[:, 0, :], kT[:, ds(i * P, P)]).then_inc(idx_ready.sem, 1)
                            if not first:
                                pool.wait_ge(turned.sem, turned.at(4 * i))
                            pool.tensor_copy(node_cols[:, 1, :], vT[:, ds(i * P, P)]).then_inc(go.sem, 1)
                        trips(pool, body, NB)

                    @block.tensor
                    def _(pe):
                        pe.wait_ge(centred.sem, centred.at(2))

                        def body(i, first):
                            for q in range(4):
                                n = 4 * i + q
                                s = 4 * (q % 2)
                                if q == 0:
                                    pe.wait_ge(idx_ready.sem, idx_ready.at(i + 1))
                                if not (first and q < 2):
                                    pe.wait_ge(evac.sem, evac.at(n - 1))
                                for c in range(2):
                                    mm = pe.matmul(ps[:, s + c, :], node_cols[:, 0, :],
                                                   block_k[:, 8 * q + 4 * c:8 * q + 4 * c + 4, :].rearrange("p t c -> p (t c)"), start=True, stop=True)
                                mm.then_inc(made.sem, 1)
                                if q == 0:
                                    pe.wait_ge(go.sem, go.at(i + 1))
                                if not (first and q < 2):
                                    pe.wait_ge(copied.sem, copied.at(n - 1))
                                for c in range(2):
                                    mm = pe.matmul(ps[:, s + 2 + c, :], node_cols[:, 1, :],
                                                   block_v[:, 8 * q + 4 * c:8 * q + 4 * c + 4, :].rearrange("p t c -> p (t c)"), start=True, stop=True)
                                mm.then_inc(turned.sem, 1)
                        trips(pe, body, NB)

                    @block.scalar
                    def _(act):
                        def body(i, first):
                            for q in range(4):
                                act.wait_ge(made.sem, made.at(4 * i + q + 1))
                                if not first:
                                    act.wait_ge(ring_out[q].sem, ring_out[q].at(16 * i))
                                act.activation(rows32[:, q, :, 0:H], ps[:, 4 * (q % 2):4 * (q % 2) + 2, :].rearrange("p a (t f) -> p (a t) f", f=H),
                                               ACT.Copy).then_inc(evac.sem, 1)
                        trips(act, body, NB)

                    @block.vector
                    def _(dve):
                        ch = Chain(dve, vdone)
                        dve.wait_ge(loaded.sem, loaded.at(16 * (2 + HEADS)))
                        ch(dve.tensor_tensor(raw[:, 0, :, :], raw[:, 0, :, :], pri.unsqueeze(2).to_broadcast([P, T32, HS]), ALU.mult))
                        ch(dve.tensor_scalar(raw[:, 0, :, :], raw[:, 0, :, :], 1.0 / HS ** 0.5, None, ALU.mult))
                        for n, blk in enumerate((block_k, block_v)):
                            dve.tensor_tensor(blk.rearrange("p t (h o) -> p t h o", o=HS),
                                              raw[:, n, :, :].unsqueeze(2).to_broadcast([P, T32, HEADS, HS]),
                                              head_mask[:, :].unsqueeze(1).unsqueeze(3).to_broadcast([P, T32, HEADS, HS]),
                                              ALU.mult).then_inc(centred.sem, 1)

                        def body(i, first):
                            for q in range(4):
                                dve.wait_ge(turned.sem, turned.at(4 * i + q + 1))
                                dve.wait_ge(evac.sem, evac.at(4 * i + q + 1))
                                if not first:
                                    dve.wait_ge(ring_out[q].sem, ring_out[q].at(16 * i))
                                dve.tensor_copy(rows32[:, q, :, H:2 * H],
                                                ps[:, 4 * (q % 2) + 2:4 * (q % 2) + 4, :].rearrange("p a (t f) -> p (a t) f", f=H)).then_inc(copied.sem, 1)
                        trips(dve, body, NB)
                        ch.close()
                loaded.base += 16 * (2 + HEADS)
                idx_ready.base += NB
                go.base += NB
                centred.base += 2
                for s in (made, turned, evac, copied):
                    s.base += 4 * NB
                for q in range(4):
                    ring_out[q].base += 16 * NB

            def score_phase():
                with nc.Block() as block:
                    @block.gpsimd
                    def _(pool):
                        def free(pool, i, h):
                            pool.wait_ge(mixed.sem, mixed.at(i * QUADS - QUADS + 2 * h + 2))
                            for q in range(2 * h, 2 * h + 2):
                                pool.wait_ge(ring_out[q].sem, ring_out[q].at(16 * i))
                        gathers(pool, table32, 2 * H, free)

                    @block.sync
                    def _(sp):
                        def body(i, first):
                            for q in range(QUADS):
                                for u in range(4 * q, 4 * q + 4):
                                    sp.wait_ge(gathered[u].sem, gathered[u].at(16 * (i + 1)))
                                sp.dma_start(values[ds(i * U + 4 * q, 4), :, :].rearrange("a e f -> e a f"),
                                             G[:, 4 * q:4 * q + 4, H:2 * H]).then_inc(ring_out[q].sem, 16)
                        trips(sp, body)
                        for q in range(QUADS):
                            sp.wait_ge(ring_out[q].sem, ring_out[q].at(16 * TRIPS))

                    @block.vector
                    def _(dve):
                        def multiply(i, q, first):
                            n = i * QUADS + q
                            for u in range(4 * q, 4 * q + 4):
                                dve.wait_ge(gathered[u].sem, gathered[u].at(16 * (i + 1)))
                            dve.wait_ge(made.sem, made.at(n + 1))
                            if not (first and q < 2):
                                dve.wait_ge(copied.sem, copied.at(n - 1))
                            dve.tensor_tensor(prod[:, q % 2, :, :], G[:, 4 * q:4 * q + 4, 0:H],
                                              ps[:, 4 + q, :].rearrange("p (s f) -> p s f", f=H), ALU.mult).then_inc(mixed.sem, 1)

                        def reduce(i, q):
                            n = i * QUADS + q
                            dve.wait_ge(mixed.sem, mixed.at(n + 1))
                            dve.tensor_reduce(score[:, ds(i * U + 4 * q, 4), :].rearrange("p s h -> p (s h)"),
                                              prod[:, q % 2, :, :].rearrange("p s (h o) -> p (s h) o", o=HS), AX.X, ALU.add).then_inc(copied.sem, 1)

                        def lagged(i, q, first):
                            if not (first and q < 2):
                                multiply(i if q >= 2 else i - 1, (q - 2) % QUADS, first)
                            if not (first and q < 3):
                                reduce(i if q >= 3 else i - 1, (q - 3) % QUADS)
                        onehots(dve, None, lagged)
                        for q in range(QUADS - 2, QUADS):
                            multiply(TRIPS - 1, q, False)
                            reduce(TRIPS - 1, q - 1)
                        reduce(TRIPS - 1, QUADS - 1)

                    @block.scalar
                    def _(act):
                        def body(i, first):
                            for q in range(QUADS):
                                n = i * QUADS + q
                                act.wait_ge(quad_done.sem, quad_done.at(n + 1))
                                if not (first and q < 2):
                                    act.wait_ge(made.sem, made.at(n - 1))
                                act.activation(onehotT[:, q % 2, :], ps[:, q, :], ACT.Copy).then_inc(evac.sem, 1)
                        trips(act, body)

                    @block.tensor
                    def _(pe):
                        def turn(i, q, fresh):
                            n = i * QUADS + q
                            pe.wait_ge(onehot_ready.sem, onehot_ready.at(n + 1))
                            if not fresh:
                                pe.wait_ge(evac.sem, evac.at(n - 3))
                            for c in range(4):
                                mm = pe.transpose(ps[:, q, c * P:(c + 1) * P], onehot[:, 4 * (q % 2) + c, :], ident[:, :])
                            mm.then_inc(quad_done.sem, 1)

                        def query(i, q, fresh):
                            n = i * QUADS + q
                            blocks = quad_blocks(pe, i * QUADS + q)
                            pe.wait_ge(evac.sem, evac.at(n + 1))
                            if not fresh:
                                pe.wait_ge(mixed.sem, mixed.at(n - 3))
                            for c, b in enumerate(blocks):
                                mm = pe.matmul(ps[:, 4 + q, c * P:(c + 1) * P], onehotT[:, q % 2, c * P:(c + 1) * P],
                                               Qn_flat[:, ds(b * P, P)], start=True, stop=True)
                            mm.then_inc(made.sem, 1)

                        def body(i, first):
                            for q in range(QUADS):
                                turn(i, q, first)
                                if not (first and q < 1):
                                    query(i if q >= 1 else i - 1, (q - 1) % QUADS, first)
                        Qn_flat = Qn.rearrange("p b f -> p (b f)")
                        body(0, True)
                        with pe.Fori(1, TRIPS) as i:
                            body(i, False)
                        query(TRIPS - 1, QUADS - 1, False)
                gather_pass_over()
                for s in (mixed, made, copied, evac):
                    s.base += ALL_QUADS
                for s in ring_out[0:QUADS]:
                    s.base += 16 * TRIPS

            def turn_steps(pe, t):
                for k in range(7):
                    for g in range(4 * k, min(GSTEPS, 4 * k + 4)):
                        mm = pe.transpose(accf[:, g * P:(g + 1) * P], t[:, g, :], ident[:, :])
                    mm.then_inc(turned.sem, 1)

            def link_phase():
                D = arena[:, 0:LINKS + 1]
                wide = arena[:, 3400:3400 + STEPS * HEADS].rearrange("p (g x) -> p g x", g=GSTEPS)
                with nc.Block() as block:
                    @block.vector
                    def _(dve):
                        ch = Chain(dve, vdone)
                        dve.tensor_copy(wide.rearrange("p g (c h) -> p g c h", h=HEADS),
                                        dv_s[:, :].rearrange("p (c g) -> p g c", g=GSTEPS).unsqueeze(3).to_broadcast([P, GSTEPS, CHUNKS, HEADS])).then_inc(mixed.sem, 1)
                        ch(dve.tensor_scalar(keep[:, :], dv_s[:, :], 0.0, 2 * BIG, ALU.is_gt, ALU.mult))
                        ch(dve.tensor_scalar(keep[:, :], keep[:, :], BIG, None, ALU.subtract))
                        dve.wait_ge(turned.sem, turned.at(7))
                        dve.tensor_copy(D[:, 1:LINKS + 1], accf[:, 0:LINKS]).then_inc(copied.sem, 1)
                        dve.wait_ge(made.sem, made.at(1))
                        ch(dve.tensor_copy(D[:, 0:1], misc[:, 0:1]))
                        dve.wait_ge(copied.sem, copied.at(1))
                        ch(dve.tensor_tensor(link[:, 0:LINKS], D[:, 1:LINKS + 1], D[:, 0:LINKS], ALU.is_equal))
                        dve.scalar_tensor_tensor(link[:, 0:LINKS], D[:, 1:LINKS + 1], 0.0, link[:, 0:LINKS], ALU.is_equal, ALU.max).then_inc(copied.sem, 1)
                        dve.wait_ge(made.sem, made.at(2))
                        ch(dve.tensor_copy(link[:, LINKS:LINKS + 1], misc[:, 1:2]))
                        ch(dve.tensor_scalar(link, link, 2 * BIG, -BIG, ALU.mult, ALU.add))
                        ch(dve.tensor_reduce(gsum[:, 0:1], link[:, 0:LINKS], AX.X, ALU.min))
                        dve.tensor_reduce(gsum[:, 1:2], link[:, 1:LINKS + 1], AX.X, ALU.min).then_inc(copied.sem, 1)
                        dve.wait_ge(turned.sem, turned.at(8))
                        ch(dve.tensor_copy(grow[:, 0, :].rearrange("p (h c) -> p h c", h=HEADS), ps[0:1, 0, 0:P].rearrange("p (c h) -> p h c", h=HEADS)))
                        ch(dve.tensor_copy(grow[:, 1, :].rearrange("p (h c) -> p h c", h=HEADS),
                                           ps[0:1, 1, 0:P].rearrange("p (c h) -> p h c", h=HEADS)[:, :, ::-1]))
                        ch.close()

                    @block.tensor
                    def _(pe):
                        pe.wait_ge(mixed.sem, mixed.at(1))
                        turn_steps(pe, wide)
                        pe.wait_ge(copied.sem, copied.at(1))
                        pe.matmul(misc[:, 0:1], shift[:, 0, :], D[:, LINKS:LINKS + 1], start=True, stop=True).then_inc(made.sem, 1)
                        pe.wait_ge(copied.sem, copied.at(2))
                        pe.matmul(misc[:, 1:2], shift[:, 1, :], link[:, 0:1], start=True, stop=True).then_inc(made.sem, 1)
                        pe.wait_ge(copied.sem, copied.at(3))
                        pe.transpose(ps[0:1, 0, 0:P], gsum[:, 0:1], ident[:, :])
                        pe.transpose(ps[0:1, 1, 0:P], gsum[:, 1:2], ident[:, :]).then_inc(turned.sem, 1)
                mixed.base += 1
                turned.base += 8
                copied.base += 3
                made.base += 2

            def softmax_phase():
                wide = arena[:, 14256:14256 + STEPS * HEADS].rearrange("p (g x) -> p g x", g=GSTEPS)
                with nc.Block() as block:
                    @block.vector
                    def _(dve):
                        ch = Chain(dve, vdone)
                        dve.tensor_tensor(wide.rearrange("p g (c h) -> p g c h", h=HEADS),
                                          score.rearrange("p (c g) h -> p g c h", g=GSTEPS),
                                          keep[:, :].rearrange("p (c g) -> p g c", g=GSTEPS).unsqueeze(3).to_broadcast([P, GSTEPS, CHUNKS, HEADS]),
                                          ALU.min).then_inc(mixed.sem, 1)
                        dve.wait_ge(turned.sem, turned.at(7))
                        ch(dve.tensor_copy(scan_in, accf[:, 0:LINKS]))
                        rev = slice(None, None, -1)

                        def scans(first_f, first_b):
                            ch(dve.tensor_tensor_scan(ahead, link[:, 0:LINKS], scan_in, first_f, ALU.min, ALU.max))
                            return dve.tensor_tensor_scan(behind[:, rev], link[:, 1:LINKS + 1][:, rev], scan_in[:, rev], first_b, ALU.min, ALU.max)
                        scans(-BIG, -BIG).then_inc(copied.sem, 1)
                        dve.wait_ge(turned.sem, turned.at(8))
                        ch(dve.tensor_copy(rows[:, 0, :].rearrange("p (h c) -> p h c", h=HEADS), ps[0:1, 0, 0:P].rearrange("p (c h) -> p h c", h=HEADS)))
                        ch(dve.tensor_copy(rows[:, 1, :].rearrange("p (h c) -> p h c", h=HEADS),
                                           ps[0:1, 1, 0:P].rearrange("p (c h) -> p h c", h=HEADS)[:, :, rev]))
                        for r in range(2):
                            ch(dve.tensor_tensor_scan(rows[:, 2 + r, :], grow[:, r, :], rows[:, r, :], -BIG, ALU.min, ALU.max))
                            ch(dve.memset(rows[:, 4 + r, :], -BIG))
                        out_f = rows[:, 4, :].rearrange("p (c h) -> p h c", h=HEADS)
                        out_b = rows[:, 5, :].rearrange("p (c h) -> p h c", h=HEADS)
                        in_f = rows[:, 2, :].rearrange("p (h c) -> p h c", h=HEADS)
                        in_b = rows[:, 3, :].rearrange("p (h c) -> p h c", h=HEADS)
                        ch(dve.tensor_copy(out_f[:, :, 1:CHUNKS], in_f[:, :, 0:CHUNKS - 1]))
                        dve.tensor_copy(out_b[:, :, rev][:, :, 1:CHUNKS], in_b[:, :, 0:CHUNKS - 1]).then_inc(copied.sem, 1)
                        dve.wait_ge(turned.sem, turned.at(9))
                        ch(dve.tensor_copy(carry, misc[:, 0:2]))
                        ch(scans(carry[:, 0:1], carry[:, 1:2]))
                        ch(dve.tensor_tensor(ahead, ahead, behind, ALU.max))
                        dve.tensor_tensor(scan_in, scan_in, ahead, ALU.subtract).then_inc(copied.sem, 1)
                        for k in range(7):
                            g0, g1 = 4 * k, min(GSTEPS, 4 * k + 4)
                            dve.wait_ge(turned.sem, turned.at(10 + k))
                            dve.tensor_copy(score.rearrange("p (c g) h -> p g c h", g=GSTEPS)[:, g0:g1, :, :],
                                            accf[:, g0 * P:g1 * P].rearrange("p (g c h) -> p g c h", c=CHUNKS, h=HEADS))
                        ch.close()

                    @block.scalar
                    def _(act):
                        act.wait_ge(copied.sem, copied.at(3))
                        act.activation(scan_in, scan_in, ACT.Exp).then_inc(evac.sem, 1)

                    @block.tensor
                    def _(pe):
                        pe.wait_ge(mixed.sem, mixed.at(1))
                        turn_steps(pe, wide)
                        pe.wait_ge(copied.sem, copied.at(1))
                        pe.transpose(ps[0:1, 0, 0:P], ahead[:, LINKS - 1:LINKS], ident[:, :])
                        pe.transpose(ps[0:1, 1, 0:P], behind[:, 0:1], ident[:, :]).then_inc(turned.sem, 1)
                        pe.wait_ge(copied.sem, copied.at(2))
                        pe.transpose(misc[:, 0:1], rows[:, 4, :], ident[0:1, 0:1])
                        pe.transpose(misc[:, 1:2], rows[:, 5, :], ident[0:1, 0:1]).then_inc(turned.sem, 1)
                        pe.wait_ge(evac.sem, evac.at(1))
                        turn_steps(pe, scan_in.rearrange("p (g e) -> p g e", e=P))
                mixed.base += 1
                turned.base += 16
                copied.base += 3
                evac.base += 1

            def message_phase():
                with nc.Block() as block:
                    @block.sync
                    def _(sp):
                        def body(i, first):
                            for q in range(QUADS):
                                if not first:
                                    sp.wait_ge(mixed.sem, mixed.at(i * QUADS + q - 3))
                                sp.dma_start(vals[:, 4 * q:4 * q + 4, :],
                                             values[ds(i * U + 4 * q, 4), :, :].rearrange("a e f -> e a f")).then_inc(ring_in[q].sem, 16)
                        trips(sp, body)

                    @block.vector
                    def _(dve):
                        def weigh(i, q, first):
                            dve.wait_ge(ring_in[q].sem, ring_in[q].at(16 * (i + 1)))
                            r = 4 * (q % 2)
                            dve.tensor_tensor(msgs[:, r:r + 4, :].rearrange("p s (h o) -> p (s h) o", o=HS),
                                              vals[:, 4 * q:4 * q + 4, :].rearrange("p s (h o) -> p (s h) o", o=HS),
                                              score[:, ds(i * U + 4 * q, 4), :].rearrange("p s h -> p (s h)").unsqueeze(2).to_broadcast([P, 4 * HEADS, HS]),
                                              ALU.mult).then_inc(mixed.sem, 1)
                        onehots(dve, None, weigh)

                    @block.tensor
                    def _(pe):
                        fill_rows(pe, None)
                        pe.matmul(misc[:, 0:NB * HEADS], ident[:, :], zeros[:, 0:NB * HEADS], start=True, stop=False, skip_group_check=True)

                        def body(i, first):
                            for q in range(QUADS):
                                blocks = quad_blocks(pe, i * QUADS + q)
                                pe.wait_ge(mixed.sem, mixed.at(i * QUADS + q + 1))
                                for c, b in enumerate(blocks):
                                    o = onehot[:, 4 * (q % 2) + c, :]
                                    pe.matmul(misc[:, ds(b * HEADS, HEADS)], o, score[:, ds(i * U + 4 * q + c, 1), :].rearrange("p a h -> p (a h)"),
                                              start=False, stop=False, skip_group_check=True)
                                    mm = pe.matmul(accf[:, ds(b * P, P)], o, msgs[:, 4 * (q % 2) + c, :],
                                                   start=False, stop=False, skip_group_check=True)
                                mm.then_inc(quad_done.sem, 1)
                        trips(pe, body)
                quad_pass_over()
                mixed.base += ALL_QUADS
                for s in ring_in[0:QUADS]:
                    s.base += 16 * TRIPS

            for l in range(2):
                if l == 0:
                    table_phase(Xn, index=(t32_s, T32))
                    with nc.Block() as block:
                        @block.gpsimd
                        def _(pool):
                            pool.tensor_copy(Lx[:, :, :], Xn[:, :, :])
                    link_phase()
                else:
                    table_phase(Lx)
                typed_phase(A["L3_gnn_Wk"][l], XT[:, :], HF[:, :], False)
                typed_phase(A["L3_gnn_Wv"][l], XT[:, :], Hn[:, :, :].rearrange("p b f -> p (b f)"), False)
                typed_phase(A["L3_gnn_Wq"][l], XT[:, :], arena[:, 0:NP], True)
                key_value_table_phase(l)
                score_phase()
                softmax_phase()
                message_phase()
                with nc.Block() as block:
                    @block.vector
                    def _(dve):
                        ch = Chain(dve, vdone)
                        ch(dve.tensor_scalar(rs8, misc[:, 0:NB * HEADS], 1e-20, None, ALU.max))
                        ch(dve.reciprocal(rs8, rs8))
                        ch(dve.tensor_tensor(Hn[:, :, :].rearrange("p b (h o) -> p (b h) o", o=HS),
                                             accf[:, 0:NP].rearrange("p (x o) -> p x o", o=HS),
                                             rs8.unsqueeze(2).to_broadcast([P, NB * HEADS, HS]), ALU.mult))
                        ch.close()
                table_phase(Hn)
                typed_phase(A["L3_gnn_Wa"][l], XT[:, :], None, True)
                with nc.Block() as block:
                    @block.sync
                    def _(sp):
                        sp.dma_start(skip_bc, over_nodes(A["L3_gnn_skip"][l])).then_inc(loaded.sem, 16)
                        sp.dma_start(types_n, A["node_type_rows"]).then_inc(loaded.sem, 16)
                        sp.dma_start(g_bc, over_nodes(A["L3_gnn_ln_g"][l])).then_inc(loaded.sem, 16)
                        sp.dma_start(b_bc, over_nodes(A["L3_gnn_ln_b"][l])).then_inc(loaded.sem, 16)

                    @block.scalar
                    def _(act):
                        act.activation(Hn[:, :, :].rearrange("p b f -> p (b f)"), accf[:, 0:NP], ACT.Sigmoid).then_inc(evac.sem, 1)
                        act.wait_ge(loaded.sem, loaded.at(64))
                        act.activation(skip_bc, skip_bc, ACT.Sigmoid).then_inc(evac.sem, 1)
                        normalise_act(act, Hn[:, :, :])

                    @block.vector
                    def _(dve):
                        ch = Chain(dve, vdone)
                        dve.wait_ge(loaded.sem, loaded.at(64))
                        dve.wait_ge(evac.sem, evac.at(2))
                        ch(dve.tensor_tensor(eq_types, types_n.unsqueeze(2).to_broadcast([P, NB, NT]),
                                             iota_row[:, 0:NT].unsqueeze(1).to_broadcast([P, NB, NT]), ALU.is_equal))
                        ch(dve.tensor_tensor(eq_types, eq_types, skip_bc.unsqueeze(1).to_broadcast([P, NB, NT]), ALU.mult))
                        ch(dve.tensor_reduce(alpha, eq_types, AX.X, ALU.add))
                        ch(dve.tensor_tensor(Hn[:, :, :], Hn[:, :, :], acc_nodes, ALU.mult))
                        ch(dve.tensor_tensor(Hn[:, :, :], Hn[:, :, :], Lx[:, :, :], ALU.subtract))
                        ch(dve.tensor_tensor(Hn[:, :, :], Hn[:, :, :], full(alpha), ALU.mult))
                        ch(dve.tensor_tensor(Hn[:, :, :], Hn[:, :, :], Lx[:, :, :], ALU.add))
                        ch(normalise(ch, dve, Hn[:, :, :], Hn[:, :, :]))
                        ch(dve.tensor_tensor(Hn[:, :, :], Hn[:, :, :], bc[:, 0:1, :].to_broadcast([P, NB, H]), ALU.mult))
                        ch(dve.tensor_tensor(Lx[:, :, :], Hn[:, :, :], bc[:, 1:2, :].to_broadcast([P, NB, H]), ALU.add))
                        ch.close()
                loaded.base += 64
                evac.base += 2
                normalised()

            table_phase(Lx, loads=[(ff_w, A["L3_gnn_ff_w"]), (brow[:, :], one_row(A["L3_gnn_ff_b"]))])
            with nc.Block() as block:
                @block.tensor
                def _(pe):
                    fill_rows(pe, brow[:, :])
                    for b in range(NB):
                        pe.matmul(accf[:, b * P:(b + 1) * P], XT[:, b * P:(b + 1) * P], ff_w, start=False, stop=False, skip_group_check=True)
            residual_norm_phase(lambda ch, dve: ch(dve.tensor_tensor(Xn[:, :, :], Xn[:, :, :], acc_nodes, ALU.add)))

        with nc.Block() as block:
            @block.sync
            def _(sp):
                sp.dma_start(out[0:(NB - 1) * P, :].rearrange("(b p) f -> p b f", p=P), Xn[:, 0:NB - 1, :]).then_inc(stored.sem, 16)
                sp.dma_start(out[(NB - 1) * P:N, :], Xn[0:LAST, NB - 1, :]).then_inc(stored.sem, 16)
                sp.wait_ge(stored.sem, stored.at(32))


def kernel(**inputs):
    import numpy as np
    import concourse.bacc as bacc
    from concourse.bass_utils import run_bass_kernel_spmd

    a = {k: np.asarray(v) for k, v in inputs.items()}
    ints = np.stack([a["src"], a["dst"], a["edge_type_32"], a["edge_type_8"]], axis=1)
    pad = np.full((EP - E, 4), 0, ints.dtype)
    pad[:, 1] = -1
    attr = a["edge_attr_64"]
    types = np.concatenate([a["node_type_16"], np.zeros(NP - N, a["node_type_16"].dtype)])
    arrays = {
        "x": a["x"], "dst": a["dst"],
        "edge_ints": np.ascontiguousarray(np.concatenate([ints, pad])).reshape(TILES, P * 4),
        "edge_w": np.concatenate([a["edge_weight"], np.zeros(EP - E, a["edge_weight"].dtype)]).reshape(TILES, P),
        "edge_attr_T": np.ascontiguousarray(np.concatenate([attr, np.zeros((SHARE_TILES * P - E, EDIM), attr.dtype)]).T),
        "edge_times": np.concatenate([a["edge_weight"], np.zeros(SHARE_TILES * P - E, a["edge_weight"].dtype)]),
        "node_type": types, "node_type_rows": np.ascontiguousarray(types.reshape(NB, P).T),
        "L0_neigh": np.ascontiguousarray(a["L0_gnn_lin_neigh_w"].transpose(0, 2, 1)),
        "L0_root": np.ascontiguousarray(a["L0_gnn_lin_root_w"].transpose(0, 2, 1)),
        "L2_W1": np.ascontiguousarray(a["L2_gnn_W1"].transpose(1, 0, 2)),
        "L2_W2": np.ascontiguousarray(a["L2_gnn_W2"].transpose(1, 0, 2)),
        "L3_Watt": np.ascontiguousarray(a["L3_gnn_Watt"].transpose(0, 1, 3, 2, 4)).reshape(2, H, T32 * HS),
        "L3_Wmsg": np.ascontiguousarray(a["L3_gnn_Wmsg"].transpose(0, 1, 3, 2, 4)).reshape(2, H, T32 * HS),
    }
    used = set(_PLAIN_STAGE1) | (set(_PLAIN_STAGE2) if STAGE >= 2 else set()) | (set(_PLAIN_STAGE3) if STAGE >= 3 else set()) \
        | (set(_PLAIN_STAGE4) if STAGE >= 4 else set())
    for name in sorted(used):
        arrays[name] = a[name]

    nc = bacc.Bacc("TRN2", target_bir_lowering=False, num_devices=1)
    aps = {k: nc.dram_tensor(k, v.shape, mybir.dt.from_np(v.dtype), kind="ExternalInput").ap() for k, v in arrays.items()}
    out = nc.dram_tensor("out", (N, H), F32, kind="ExternalOutput").ap()
    build(nc, aps, out)
    r = run_bass_kernel_spmd(nc, [arrays], core_ids=[0])
    return r.results[0]["out"]


_PLAIN_STAGE1 = ("L0_gnn_lin_root_b", "L0_gnn_ln_w", "L0_gnn_ln_b")
_PLAIN_STAGE2 = ("L1_gnn_We1", "L1_gnn_be1", "L1_gnn_We2", "L1_gnn_be2", "L1_gnn_Wt", "L1_gnn_bt", "L1_gnn_Wn1", "L1_gnn_bn1",
                 "L1_gnn_Wn2", "L1_gnn_bn2")
_PLAIN_STAGE3 = ("L2_gnn_Wl1", "L2_gnn_b1", "L2_gnn_Wl2", "L2_gnn_b2")
_PLAIN_STAGE4 = ("L3_gnn_Wk", "L3_gnn_Wq", "L3_gnn_Wv", "L3_gnn_Wa", "L3_gnn_pri", "L3_gnn_skip", "L3_gnn_ln_g", "L3_gnn_ln_b",
                 "L3_gnn_ff_w", "L3_gnn_ff_b")
```

```python
from contextlib import ExitStack

import concourse.bass as bass
from concourse import mybir

ALU = mybir.AluOpType
ACT = mybir.ActivationFunctionType
AX = mybir.AxisListType
F32 = mybir.dt.float32
I32 = mybir.dt.int32
ds = bass.ds

P = 128
N = 3125
E = 50000
H = 128
NB = -(-N // P)
NP = NB * P
LAST = N - (NB - 1) * P
BANKS = -(-NB // 4)
U = 16
HALF = U // 2
QUADS = U // 4
TILES = 4 * -(-E // (4 * P))
STEPS = -(-(-(-E // P) + NB - 1) // U) * U
TRIPS = STEPS // U
ALL_QUADS = STEPS // 4
SHARE_TILES = 2 * 2 * ALL_QUADS
EP = TILES * P
TCH = 4
TROWS = TILES // TCH
CROWS = 125
CCOLS = E // CROWS
L0 = 3
R8 = 8
T32 = 32
NT = 16
SORT_TILES = 8 * -(-(NB + NT - 1) // 8)
HEADS = 8
HS = H // HEADS
EDIM = 64
CHUNKS = P // HEADS
GSTEPS = STEPS // CHUNKS
BIG = 1e30
EPS = 1e-5


class Signal:

    def __init__(self, sem):
        self.sem, self.base = sem, 0

    def at(self, count):
        return count + self.base


class Chain:

    def __init__(self, eng, mark):
        self.eng, self.mark, self.n = eng, mark, 0

    def __call__(self, inst):
        self.n += 1
        inst.then_inc(self.mark.sem, 1)
        self.eng.wait_ge(self.mark.sem, self.mark.at(self.n))

    def close(self):
        self.mark.base += self.n


def trips(eng, body, n=TRIPS):
    body(0, True)
    with eng.Fori(1, n) as i:
        body(i, False)


def span(k):
    return 512 * k, min(NP, 512 * k + 512), range(4 * k, min(NB, 4 * k + 4))


def build(nc, A, out):
    ctx = ExitStack()
    with ctx:
        def sb(name, shape, dt=F32):
            return ctx.enter_context(nc.sbuf_tensor(name, shape, dt))

        def signal(name):
            return Signal(ctx.enter_context(nc.semaphore(name)))

        def dram(name, shape, dt=F32):
            return nc.dram_tensor(name, shape, dt, kind="Internal").ap()

        table = dram("table", [NP, H])
        table8 = dram("table8", [NP * R8, H])
        table32 = dram("table32", [NP * T32, 2 * H])
        edge_part = dram("edge_part", [SHARE_TILES, P, H])
        values = dram("values", [STEPS, P, H])

        sorted_x = dram("sorted_x", [SORT_TILES * P, H])
        sorted_kvq = dram("sorted_kvq", [SORT_TILES * P, 3 * H])
        sorted_a = dram("sorted_a", [SORT_TILES * P, H])

        ident = sb("ident", [P, P])
        iota_row = sb("iota_row", [P, P])
        zeros = sb("zeros", [P, 512])
        ones = sb("ones", [P, P])
        shift = sb("shift", [P, 2, P])
        head_mask = sb("head_mask", [P, HEADS])
        blk4_i = sb("blk4_i", [P, ALL_QUADS], I32)
        tile_i = sb("tile_i", [P, STEPS], I32)
        src_s = sb("src_s", [P, STEPS])
        dl_s = sb("dl_s", [P, STEPS])
        t32_s = sb("t32_s", [P, STEPS])
        t8_s = sb("t8_s", [P, STEPS])
        w_s = sb("w_s", [P, STEPS])
        dv_s = sb("dv_s", [P, STEPS])
        idx_s = sb("idx_s", [P, STEPS], I32)
        rsum = sb("rsum", [P, NB])
        deg = sb("deg", [P, NB])
        Xn = sb("Xn", [P, NB, H])
        Lx = sb("Lx", [P, NB, H])
        XT = sb("XT", [P, NP])
        Hn = sb("Hn", [P, NB, H])
        HF = sb("HF", [P, NP])
        G = sb("G", [P, U, 2 * H])
        gidx = sb("gidx", [P, U], I32)
        pos_i = sb("pos_i", [P, NB], I32)
        tile_type = sb("tile_type", [P, SORT_TILES], I32)
        onehot = sb("onehot", [P, HALF, P])
        red = sb("red", [P, 4, NB])
        wts = sb("wts", [P, 6, H])
        vecs = sb("vecs", [P, 16])
        bc = sb("bc", [P, 2, H])
        brow = sb("brow", [1, H])
        arena = sb("arena", [P, 24500])

        ps = ctx.enter_context(nc.psum_tensor("ps", [P, 8, 512], F32))
        acc, misc = ps[:, 0:7, :], ps[:, 7, :]
        accf = acc.rearrange("p a b -> p (a b)")
        acc_nodes = accf[:, 0:NP].rearrange("p (b f) -> p b f", f=H)

        loaded = signal("loaded")
        stored = signal("stored")
        consts = signal("consts")
        vdone = signal("vdone")
        pdone = signal("pdone")
        idx_ready = signal("idx_ready")
        placed = signal("placed")
        fetched = signal("fetched")
        go = signal("go")
        gathered = [signal(f"gathered{u}") for u in range(U)]
        onehot_ready = signal("onehot_ready")
        compared = signal("compared")
        quad_done = signal("quad_done")
        turned = signal("turned")
        evac = signal("evac")
        made = signal("made")
        copied = signal("copied")
        mixed = signal("mixed")
        centred = signal("centred")
        squared = signal("squared")
        varied = signal("varied")
        rooted = signal("rooted")
        ring_in = [signal(f"ring_in{u}") for u in range(HALF)]
        ring_out = [signal(f"ring_out{u}") for u in range(U)]

        edge_out = [signal(f"edge_out{u}") for u in range(2)]

        cube = arena[:, 0:STEPS * NB]
        dst_i = Hn[0:CROWS, 0:4, :].rearrange("p a b -> p (a b)").bitcast(I32)[:, 0:CCOLS]
        dst_f = Hn[0:CROWS, 4:8, :].rearrange("p a b -> p (a b)")[:, 0:CCOLS]
        cnt = red[:, 0, :]
        jrow_i = XT[:, 0:STEPS].bitcast(I32)
        jrow = XT[:, 512:512 + STEPS]
        blk_f = XT[:, 1024:1024 + STEPS]
        tile_f = XT[:, 1536:1536 + STEPS]
        blk128 = XT[:, 2048:2048 + STEPS]
        valid = XT[:, 2560:2560 + STEPS]
        pack_f = HF[:, 1024:1024 + STEPS]
        sm = HF[:, 0:12 * 32].rearrange("p (a b) -> p a b", b=32)
        smi = HF[:, 512:512 + 64].bitcast(I32)
        chunk_i = HF[:, 600:604].bitcast(I32)
        chunk_f = HF[:, 604:608]
        start_f, n_f, first_f, last_f, tiles_f, base_f, delta_f, dd_f, thr = (sm[:, r, 0:NB + 1] for r in range(9))
        fields_i = Hn[:, 8:24, :].rearrange("p a b -> p (a b)")[0:TROWS, :].bitcast(I32).rearrange("p (c e k) -> p c e k", c=TCH, k=4)
        fields_f = Lx[:, 0:16, :].rearrange("p a b -> p (a b)")[0:TROWS, :].rearrange("p (c e k) -> p c e k", c=TCH, k=4)
        fields_w = Lx[:, 16:20, :].rearrange("p a b -> p (a b)")[0:TROWS, :].rearrange("p (c e) -> p c e", c=TCH)
        select = arena[0:TROWS, 12000:12000 + TCH * STEPS].rearrange("p (c s) -> p c s", c=TCH)
        dests = [src_s, dl_s, t32_s, t8_s, w_s]

        with nc.Block() as block:
            @block.gpsimd
            def _(pool):
                ch = Chain(pool, pdone)
                pool.memset(zeros[:, :], 0.0).then_inc(consts.sem, 1)
                pool.memset(ones[:, :], 1.0).then_inc(consts.sem, 1)
                pool.memset(red[:, :, :], 0.0).then_inc(consts.sem, 1)
                ch(pool.memset(ident[:, :], 0.0))
                pool.affine_select(out=ident[:, :], in_=ident[:, :], compare_op=ALU.not_equal, fill=1.0,
                                   base=0, pattern=[[-1, P]], channel_multiplier=1).then_inc(consts.sem, 1)
                pool.iota(jrow_i, pattern=[[1, STEPS]], base=0, channel_multiplier=0).then_inc(consts.sem, 1)
                pool.iota(chunk_i, pattern=[[TROWS, TCH]], base=0, channel_multiplier=1).then_inc(consts.sem, 1)
                ch(pool.memset(shift[:, :, :], 0.0))
                pool.affine_select(out=shift[:, 0, :], in_=shift[:, 0, :], compare_op=ALU.not_equal, fill=1.0,
                                   base=HEADS, pattern=[[-1, P]], channel_multiplier=1).then_inc(consts.sem, 1)
                pool.affine_select(out=shift[:, 1, :], in_=shift[:, 1, :], compare_op=ALU.not_equal, fill=1.0,
                                   base=-HEADS, pattern=[[-1, P]], channel_multiplier=1).then_inc(consts.sem, 1)
                ch(pool.memset(head_mask[:, :], 1.0))
                ch(pool.affine_select(out=head_mask[:, :], in_=head_mask[:, :], compare_op=ALU.is_ge, fill=0.0,
                                      base=0, pattern=[[-HS, HEADS]], channel_multiplier=1))
                pool.affine_select(out=head_mask[:, :], in_=head_mask[:, :], compare_op=ALU.is_ge, fill=0.0,
                                   base=HS - 1, pattern=[[HS, HEADS]], channel_multiplier=-1).then_inc(consts.sem, 1)
                ch.close()

            @block.sync
            def _(sp):
                sp.dma_start(dst_i, A["dst"].rearrange("(p c) -> p c", p=CROWS)).then_inc(loaded.sem, 16)
                sp.dma_start(fields_i.rearrange("p c e k -> p c (e k)"),
                             A["edge_ints"].rearrange("(c p) k -> p c k", c=TCH)).then_inc(stored.sem, 16)
                sp.dma_start(fields_w, A["edge_w"].rearrange("(c p) k -> p c k", c=TCH)).then_inc(stored.sem, 16)
                sp.dma_start(Xn[:, 0:NB - 1, :], A["x"][0:(NB - 1) * P, :].rearrange("(b p) f -> p b f", p=P)).then_inc(stored.sem, 16)
                sp.wait_ge(copied.sem, 1)
                sp.dma_start(Xn[0:LAST, NB - 1, :], A["x"][(NB - 1) * P:N, :]).then_inc(stored.sem, 16)
                sp.wait_ge(stored.sem, 64)

            @block.tensor
            def _(pe):
                pe.wait_ge(consts.sem, 9)
                pe.wait_ge(made.sem, 1)
                pe.matmul(misc[:, 0:NB], ones[0:CROWS, :], cnt[0:CROWS, :], start=True, stop=True).then_inc(turned.sem, 1)
                pe.wait_ge(mixed.sem, 1)
                for f in range(5):
                    for c in range(TCH):
                        rows = fields_f[:, c, :, f] if f < 4 else fields_w[:, c, :]
                        mm = pe.matmul(acc[:, f, 0:STEPS], rows, select[:, c, :], start=(c == 0), stop=(c == TCH - 1))
                    mm.then_inc(turned.sem, 1)

            @block.vector
            def _(dve):
                ch = Chain(dve, vdone)
                dve.memset(Xn[:, NB - 1, :], 0.0).then_inc(copied.sem, 1)
                dve.wait_ge(consts.sem, 9)
                ch(dve.tensor_copy(jrow, jrow_i))
                ch(dve.tensor_copy(chunk_f, chunk_i))
                ch(dve.tensor_copy(iota_row[:, :], jrow[:, 0:P]))
                ch(dve.tensor_scalar(thr, jrow[:, 0:NB + 1], float(P), None, ALU.mult))
                dve.wait_ge(loaded.sem, 16)
                ch(dve.tensor_copy(dst_f, dst_i))
                below = cube[0:CROWS, 0:NB * CCOLS].rearrange("p (b c) -> p b c", b=NB)
                ch(dve.tensor_tensor(below, dst_f.unsqueeze(1).to_broadcast([CROWS, NB, CCOLS]),
                                     thr[0:CROWS, 0:NB].unsqueeze(2).to_broadcast([CROWS, NB, CCOLS]), ALU.is_lt))
                dve.tensor_reduce(cnt[0:CROWS, :], below, AX.X, ALU.add).then_inc(made.sem, 1)
                dve.wait_ge(turned.sem, 1)
                ch(dve.tensor_copy(start_f[:, 0:NB], misc[:, 0:NB]))
                ch(dve.memset(start_f[:, NB:NB + 1], float(E)))
                ch(dve.tensor_tensor(n_f[:, 0:NB], start_f[:, 1:NB + 1], start_f[:, 0:NB], ALU.subtract))
                ch(dve.tensor_copy(smi[:, 0:NB], start_f[:, 0:NB]))
                ch(dve.tensor_scalar(n_f[:, 0:NB], n_f[:, 0:NB], 0.0, None, ALU.is_gt))
                ch(dve.tensor_scalar(last_f[:, 0:NB], start_f[:, 1:NB + 1], float(P - 1), None, ALU.add))
                ch(dve.tensor_copy(smi[:, 32:32 + NB], last_f[:, 0:NB]))
                ch(dve.tensor_scalar(smi[:, 0:NB], smi[:, 0:NB], 7, None, ALU.arith_shift_right))
                ch(dve.tensor_scalar(smi[:, 32:32 + NB], smi[:, 32:32 + NB], 7, None, ALU.arith_shift_right))
                ch(dve.tensor_copy(first_f[:, 0:NB], smi[:, 0:NB]))
                ch(dve.tensor_copy(last_f[:, 0:NB], smi[:, 32:32 + NB]))
                ch(dve.tensor_tensor(tiles_f[:, 0:NB], last_f[:, 0:NB], first_f[:, 0:NB], ALU.subtract))
                ch(dve.tensor_tensor(tiles_f[:, 0:NB], tiles_f[:, 0:NB], n_f[:, 0:NB], ALU.mult))
                ch(dve.tensor_tensor_scan(base_f[:, 0:NB], tiles_f[:, 0:NB], zeros[:, 0:NB], 0.0, ALU.add, ALU.add))
                ch(dve.tensor_tensor(base_f[:, 0:NB], base_f[:, 0:NB], tiles_f[:, 0:NB], ALU.subtract))
                ch(dve.tensor_tensor(delta_f[:, 0:NB], first_f[:, 0:NB], base_f[:, 0:NB], ALU.subtract))
                ch(dve.tensor_copy(dd_f[:, 0:1], delta_f[:, 0:1]))
                ch(dve.tensor_tensor(dd_f[:, 1:NB], delta_f[:, 1:NB], delta_f[:, 0:NB - 1], ALU.subtract))
                reached = cube.rearrange("p (j b) -> p j b", b=NB)
                ch(dve.tensor_tensor(reached, jrow.unsqueeze(2).to_broadcast([P, STEPS, NB]),
                                     base_f[:, 0:NB].unsqueeze(1).to_broadcast([P, STEPS, NB]), ALU.is_ge))
                ch(dve.tensor_reduce(blk_f, reached, AX.X, ALU.add))
                ch(dve.tensor_scalar(blk_f, blk_f, 1.0, None, ALU.subtract))
                ch(dve.tensor_tensor(reached, reached, dd_f[:, 0:NB].unsqueeze(1).to_broadcast([P, STEPS, NB]), ALU.mult))
                ch(dve.tensor_reduce(tile_f, reached, AX.X, ALU.add))
                ch(dve.tensor_tensor(tile_f, jrow, tile_f, ALU.add))
                ch(dve.tensor_scalar(valid, tile_f, float(TILES) - 0.5, None, ALU.is_lt))
                ch(dve.tensor_scalar(tile_f, tile_f, float(TILES - 1), None, ALU.min))
                blk_q = blk_f.rearrange("p (n c) -> p n c", c=4)
                pack = pack_f[:, 0:ALL_QUADS]
                ch(dve.scalar_tensor_tensor(pack, blk_q[:, :, 3], 32.0, blk_q[:, :, 2], ALU.mult, ALU.add))
                ch(dve.scalar_tensor_tensor(pack, pack, 32.0, blk_q[:, :, 1], ALU.mult, ALU.add))
                ch(dve.scalar_tensor_tensor(pack, pack, 32.0, blk_q[:, :, 0], ALU.mult, ALU.add))
                ch(dve.tensor_copy(blk4_i[:, :], pack))
                ch(dve.tensor_copy(tile_i[:, :], tile_f))
                ch(dve.tensor_scalar(blk128, blk_f, float(P), None, ALU.mult))
                for c in range(TCH):
                    ch(dve.tensor_scalar(select[:, c, :], tile_f[0:TROWS, :], chunk_f[0:TROWS, c:c + 1], None, ALU.is_equal))
                dve.wait_ge(stored.sem, 64)
                dve.tensor_copy(fields_f.rearrange("p c e k -> p (c e k)"), fields_i.rearrange("p c e k -> p (c e k)")).then_inc(mixed.sem, 1)
                for f in range(5):
                    dve.wait_ge(turned.sem, f + 2)
                    ch(dve.tensor_copy(dests[f][:, :], acc[:, f, 0:STEPS]))
                ch(dve.tensor_scalar(dv_s[:, :], dl_s[:, :], 1.0, None, ALU.add))
                ch(dve.tensor_tensor(dl_s[:, :], dl_s[:, :], blk128, ALU.subtract))
                ch(dve.scalar_tensor_tensor(valid, dl_s[:, :], 0.0, valid, ALU.is_ge, ALU.mult))
                ch(dve.scalar_tensor_tensor(valid, dl_s[:, :], float(P), valid, ALU.is_lt, ALU.mult))
                ch(dve.tensor_tensor(dv_s[:, :], dv_s[:, :], valid, ALU.mult))
                ch(dve.scalar_tensor_tensor(dl_s[:, :], dl_s[:, :], 1.0, valid, ALU.add, ALU.mult))
                ch(dve.tensor_scalar(dl_s[:, :], dl_s[:, :], 1.0, None, ALU.subtract))
                ch(dve.tensor_copy(idx_s[:, :], src_s[:, :]))
                ch.close()
        loaded.base, stored.base, consts.base, made.base, turned.base, mixed.base, copied.base = 16, 64, 9, 1, 6, 1, 1

        def onehots(dve, weight, after=None):
            def body(i, first):
                for q in range(QUADS):
                    n = i * QUADS + q
                    j = i * U + 4 * q
                    if not (first and q < 2):
                        dve.wait_ge(quad_done.sem, quad_done.at(n - 1))
                    o = onehot[:, 4 * (q % 2):4 * (q % 2) + 4, :]
                    is_dst = dve.tensor_tensor(o, iota_row[:, :].unsqueeze(1).to_broadcast([P, 4, P]),
                                               dl_s[:, ds(j, 4)].unsqueeze(2).to_broadcast([P, 4, P]), ALU.is_equal)
                    if weight is not None:
                        is_dst.then_inc(compared.sem, 1)
                        dve.wait_ge(compared.sem, compared.at(n + 1))
                        is_dst = dve.tensor_tensor(o, o, weight[:, ds(j, 4)].unsqueeze(2).to_broadcast([P, 4, P]), ALU.mult)
                    is_dst.then_inc(onehot_ready.sem, 1)
                    if after is not None:
                        after(i, q, first)
            trips(dve, body)
            if weight is not None:
                compared.base += ALL_QUADS

        def gathers(pool, tab, width, free=None):
            def body(i, first):
                for h in range(2):
                    if not first:
                        if free is None:
                            pool.wait_ge(quad_done.sem, quad_done.at(i * QUADS - QUADS + 2 * h + 2))
                        else:
                            free(pool, i, h)
                    pool.tensor_copy(gidx[:, h * HALF:(h + 1) * HALF],
                                     idx_s[:, ds(i * U + h * HALF, HALF)]).then_inc(idx_ready.sem, 1)
                    pool.wait_ge(idx_ready.sem, idx_ready.at(2 * i + h + 1))
                    pool.sem_inc(go.sem, 1)
                    for u in range(h * HALF, (h + 1) * HALF):
                        pool.indirect_dma_start(G[:, u, 0:width], None, tab,
                                                bass.IndirectOffsetOnAxis(ap=gidx[:, u:u + 1], axis=0)).then_inc(gathered[u].sem, 16)
            trips(pool, body)

        def quad_blocks(pe, n):
            four = nc.values_load(blk4_i[0:1, ds(n, 1)], engines=(pe.engine,), min_val=0, max_val=32 ** 4 - 1,
                                  skip_runtime_bounds_check_because="block numbers by construction")
            return [nc.snap((four >> (5 * c)) & 31, engines=(pe.engine,), min_val=0, max_val=NB - 1) for c in range(4)]

        def quad_pass_over():
            onehot_ready.base += ALL_QUADS
            quad_done.base += ALL_QUADS

        def gather_pass_over():
            quad_pass_over()
            idx_ready.base += 2 * TRIPS
            go.base += 2 * TRIPS
            for s in gathered:
                s.base += 16 * TRIPS

        def fill_rows(pe, row):
            for k in range(BANKS):
                a, b, blocks = span(k)
                if row is None:
                    pe.matmul(accf[:, a:b], ident[:, :], zeros[:, 0:b - a], start=True, stop=False, skip_group_check=True)
                else:
                    pe.matmul(accf[:, a:b].rearrange("p (b f) -> p b f", f=H), ones[0:1, :],
                              row.unsqueeze(1).to_broadcast([1, len(blocks), H]), start=True, stop=False, skip_group_check=True)

        def turn_nodes(pe, source, need):
            for k in range(BANKS):
                need(k)
                for b in span(k)[2]:
                    mm = pe.transpose(accf[:, b * P:(b + 1) * P],
                                      source[:, b, :] if len(source.shape) == 3 else source[:, b * P:(b + 1) * P], ident[:, :])
                mm.then_inc(turned.sem, 1)

        def normalise(ch, dve, src, dst):
            mean, var = red[:, 0, :], red[:, 1, :]

            def over(v):
                return v.unsqueeze(2).to_broadcast([P, NB, H])
            ch(dve.tensor_reduce(mean, src, AX.X, ALU.add))
            ch(dve.tensor_scalar(mean, mean, 1.0 / H, None, ALU.mult))
            dve.tensor_tensor(dst, src, over(mean), ALU.subtract).then_inc(centred.sem, 1)
            dve.wait_ge(squared.sem, squared.at(1))
            ch(dve.tensor_reduce(var, arena[:, 0:NP].rearrange("p (b f) -> p b f", f=H), AX.X, ALU.add))
            dve.tensor_scalar(var, var, 1.0 / H, EPS, ALU.mult, ALU.add).then_inc(varied.sem, 1)
            dve.wait_ge(rooted.sem, rooted.at(1))
            ch(dve.reciprocal(var, var))
            return dve.tensor_tensor(dst, dst, over(var), ALU.mult)

        def normalise_act(act, dst):
            act.wait_ge(centred.sem, centred.at(1))
            act.activation(arena[:, 0:NP], dst.rearrange("p b f -> p (b f)"), ACT.Square).then_inc(squared.sem, 1)
            act.wait_ge(varied.sem, varied.at(1))
            act.activation(red[:, 1, :], red[:, 1, :], ACT.Sqrt).then_inc(rooted.sem, 1)

        def normalised():
            for s in (centred, squared, varied, rooted):
                s.base += 1

        def residual_norm_phase(prepare=None):
            with nc.Block() as block:
                @block.scalar
                def _(act):
                    normalise_act(act, Xn[:, :, :])

                @block.vector
                def _(dve):
                    ch = Chain(dve, vdone)
                    if prepare is not None:
                        prepare(ch, dve)
                    ch(normalise(ch, dve, Xn[:, :, :], Xn[:, :, :]))
                    ch.close()
            normalised()

        def load_phase_part(sp, loads):
            for dst_ap, src_ap in loads:
                sp.dma_start(dst_ap, src_ap).then_inc(loaded.sem, 16)

        def table_phase(src, scale=1.0, bias=0.0, loads=(), w=None, row=None, index=None):
            with nc.Block() as block:
                @block.sync
                def _(sp):
                    load_phase_part(sp, loads)
                    if w is not None:
                        sp.wait_ge(copied.sem, copied.at(BANKS))
                        sp.dma_start(table.rearrange("(b p) f -> p b f", p=P),
                                     HF[:, :].rearrange("p (b f) -> p b f", f=H)).then_inc(stored.sem, 16)
                        sp.wait_ge(stored.sem, stored.at(16))

                @block.tensor
                def _(pe):
                    turn_nodes(pe, src[:, :, :], lambda k: None)
                    if w is not None:
                        pe.wait_ge(loaded.sem, loaded.at(16 * len(loads)))
                        for k in range(BANKS):
                            a, b, blocks = span(k)
                            pe.wait_ge(evac.sem, evac.at(k + 1))
                            if row is not None:
                                pe.matmul(accf[:, a:b].rearrange("p (b f) -> p b f", f=H), ones[0:1, :],
                                          row.unsqueeze(1).to_broadcast([1, len(blocks), H]), start=True, stop=False, skip_group_check=True)
                            for b in blocks:
                                mm = pe.matmul(accf[:, b * P:(b + 1) * P], XT[:, b * P:(b + 1) * P], w,
                                               start=(row is None), stop=True, skip_group_check=True)
                            mm.then_inc(made.sem, 1)

                @block.scalar
                def _(act):
                    act.wait_ge(loaded.sem, loaded.at(16 * len(loads)))
                    for k in range(BANKS):
                        a, b, _ = span(k)
                        act.wait_ge(turned.sem, turned.at(k + 1))
                        act.activation(XT[:, a:b], accf[:, a:b], ACT.Identity, scale=scale, bias=bias).then_inc(evac.sem, 1)

                @block.vector
                def _(dve):
                    ch = Chain(dve, vdone)
                    if index is not None:
                        ch(dve.scalar_tensor_tensor(w1_f, src_s[:, :], float(index[1]), index[0][:, :], ALU.mult, ALU.add))
                        ch(dve.tensor_copy(idx_s[:, :], w1_f))
                    if w is not None:
                        for k in range(BANKS):
                            a, b, _ = span(k)
                            dve.wait_ge(made.sem, made.at(k + 1))
                            dve.tensor_copy(HF[:, a:b], accf[:, a:b]).then_inc(copied.sem, 1)
                    ch.close()
            loaded.base += 16 * len(loads)
            turned.base += BANKS
            evac.base += BANKS
            if w is not None:
                made.base += BANKS
                copied.base += BANKS
                stored.base += 16
        w1_f = arena[:, 24000:24000 + STEPS]

        def aggregate_phase(tab, weight, root=None, row=None, sums=None, edges=None):
            with nc.Block() as block:
                @block.gpsimd
                def _(pool):
                    gathers(pool, tab, H)

                @block.vector
                def _(dve):
                    onehots(dve, weight, edges.join if edges else None)
                    if edges:
                        edges.join_last(dve)

                @block.tensor
                def _(pe):
                    fill_rows(pe, row)
                    if root is not None:
                        for b in range(NB):
                            pe.matmul(accf[:, b * P:(b + 1) * P], XT[:, b * P:(b + 1) * P], root, start=False, stop=False,
                                      skip_group_check=True)
                    if sums:
                        pe.matmul(misc[:, 0:NB], ident[:, :], zeros[:, 0:NB], start=True, stop=False, skip_group_check=True)
                    if edges:
                        pe.wait_ge(loaded.sem, loaded.at(16 * edges.LOADS))

                    def body(i, first):
                        for u in range(U):
                            if u % 4 == 0:
                                blocks = quad_blocks(pe, i * QUADS + u // 4)
                                if edges:
                                    edges.hidden(pe, i, u // 4, first)
                                pe.wait_ge(onehot_ready.sem, onehot_ready.at(i * QUADS + u // 4 + 1))
                            if u % 4 == 2 and edges:
                                edges.output(pe, i, u // 4, first)
                            pe.wait_ge(gathered[u].sem, gathered[u].at(16 * (i + 1)))
                            o, b = onehot[:, u % HALF, :], blocks[u % 4]
                            if sums:
                                pe.matmul(misc[:, ds(b, 1)], o, ones[:, 0:1], start=False, stop=False, skip_group_check=True)
                            mm = pe.matmul(accf[:, ds(b * P, P)], o, G[:, u, 0:H],
                                           start=False, stop=False, skip_group_check=True)
                            if u % 4 == 3:
                                mm.then_inc(quad_done.sem, 1)
                    trips(pe, body)
                    if edges:
                        edges.products_last(pe)

                if edges:
                    @block.sync
                    def _(sp):
                        edges.transfers(sp)

                    @block.scalar
                    def _(act):
                        edges.activations(act)
            gather_pass_over()
            if edges:
                edges.over()

        def col(ap):
            return ap.rearrange("(p a) -> p a", a=1)

        def one_row(ap):
            return ap.rearrange("(a f) -> a f", a=1)

        def over_nodes(ap):
            return ap.partition_broadcast(P)

        def full(v):
            return v.unsqueeze(2).to_broadcast([P, NB, H])

        class EdgeShare:
            PAIR = 2 * P
            LOADS = 7
            half_a, half_b = misc[:, 0:PAIR], misc[:, PAIR:2 * PAIR]
            attrT = arena[0:EDIM, 0:4 * PAIR].rearrange("p (r e) -> p r e", r=4)
            ts_bc = arena[:, 1024:1024 + 4 * PAIR].rearrange("p (r e) -> p r e", r=4)
            hid = arena[:, 2048:2048 + 2 * PAIR].rearrange("p (r e) -> p r e", r=2)
            tw = arena[:, 2560:2560 + 2 * PAIR].rearrange("p (r e) -> p r e", r=2)
            ef = arena[:, 3072:3072 + 2 * PAIR].rearrange("p (r e) -> p r e", r=2)
            zout = arena[:, 3584:3584 + 2 * PAIR].rearrange("p (r e) -> p r e", r=2)
            We2, Wn1b = arena[:, 4096:4224], arena[:, 4224:4352]
            we1 = arena[0:EDIM, 4352:4480]
            be1, be2, wt_c, bt_c = (vecs[:, 8 + r:9 + r] for r in range(4))

            def __init__(self, part):
                self.pair0 = part * ALL_QUADS

            def load(self, sp, i, q, first):
                n = i * QUADS + q
                edge = (i * QUADS + (self.pair0 + q)) * self.PAIR
                if not first:
                    sp.wait_ge(made.sem, made.at(n - 3))
                sp.dma_start(self.attrT[:, q, :], A["edge_attr_T"][:, ds(edge, self.PAIR)]).then_inc(ring_in[q].sem, 16)
                if not first:
                    sp.wait_ge(mixed.sem, mixed.at(n - 3))
                sp.dma_start(self.ts_bc[:, q, :], A["edge_times"][ds(edge, self.PAIR)].partition_broadcast(P)).then_inc(ring_in[4 + q].sem, 16)

            def store(self, sp, i, q):
                sp.wait_ge(centred.sem, centred.at(i * QUADS + q + 1))
                sp.dma_start(edge_part[ds((i * QUADS + (self.pair0 + q)) * 2, 2), :, :].rearrange("t e f -> e t f"),
                             self.zout[:, q % 2, :].rearrange("p (t f) -> p t f", t=2)).then_inc(edge_out[q % 2].sem, 16)

            def transfers(self, sp):
                for dst_ap, src_ap in ((self.we1, A["L1_gnn_We1"]), (self.We2, A["L1_gnn_We2"]), (self.Wn1b, A["L1_gnn_Wn1"][H:2 * H, :]),
                                       (self.be1, col(A["L1_gnn_be1"])), (self.be2, col(A["L1_gnn_be2"])),
                                       (self.wt_c, A["L1_gnn_Wt"].rearrange("a f -> f a")), (self.bt_c, col(A["L1_gnn_bt"]))):
                    sp.dma_start(dst_ap, src_ap).then_inc(loaded.sem, 16)

                def body(i, first):
                    for q in range(QUADS):
                        self.load(sp, i, q, first)
                        if q == 3:
                            self.store(sp, i, 0)
                        elif not first:
                            self.store(sp, i - 1, q + 1)
                trips(sp, body)
                for q in range(1, QUADS):
                    self.store(sp, TRIPS - 1, q)
                for r in range(2):
                    sp.wait_ge(edge_out[r].sem, edge_out[r].at(16 * (ALL_QUADS // 2)))

            def second(self, pe, m, r):
                pe.wait_ge(evac.sem, evac.at(m + 1))
                pe.matmul(self.half_b, self.We2, self.hid[:, r, :], start=True, stop=True, skip_group_check=True).then_inc(turned.sem, 1)

            def third(self, pe, m, r):
                pe.wait_ge(copied.sem, copied.at(m + 1))
                for c in range(2):
                    mm = pe.matmul(self.half_a[:, c * P:(c + 1) * P], self.ef[:, r, c * P:(c + 1) * P], self.Wn1b, start=True, stop=True,
                                   skip_group_check=True)
                mm.then_inc(rooted.sem, 1)

            def hidden(self, pe, i, q, first):
                n = i * QUADS + q
                if not (first and q < 3):
                    pe.wait_ge(centred.sem, centred.at(n - 2))
                if not (first and q < 1):
                    if q == 2 and first:
                        pe.wait_ge(squared.sem, squared.at(n - 1))
                    elif q == 1 and first:
                        pe.wait_ge(evac.sem, evac.at(n))
                    self.second(pe, n - 1, (q + 1) % 2)
                pe.wait_ge(ring_in[q].sem, ring_in[q].at(16 * (i + 1)))
                pe.matmul(self.half_a, self.we1, self.attrT[:, q, :], start=True, stop=True, skip_group_check=True).then_inc(made.sem, 1)

            def output(self, pe, i, q, first):
                n = i * QUADS + q
                if not (first and q < 2):
                    pe.wait_ge(squared.sem, squared.at(n))
                    self.third(pe, n - 2, q % 2)

            def products_last(self, pe):
                m = ALL_QUADS - 1
                pe.wait_ge(centred.sem, centred.at(m - 1))
                self.second(pe, m, m % 2)
                pe.wait_ge(squared.sem, squared.at(m + 1))
                self.third(pe, m - 1, (m - 1) % 2)
                pe.wait_ge(centred.sem, centred.at(m))
                self.third(pe, m, m % 2)

            def take_b(self, act, m, r, used):
                if used:
                    act.wait_ge(rooted.sem, rooted.at(m - 1))
                act.activation(self.ef[:, r, :], self.half_b, ACT.Identity, bias=self.be2).then_inc(squared.sem, 1)

            def take_output(self, act, m, r, stores):
                act.wait_ge(rooted.sem, rooted.at(m + 1))
                if stores is not None:
                    act.wait_ge(edge_out[r].sem, edge_out[r].at(stores))
                act.activation(self.zout[:, r, :], self.half_a, ACT.Copy).then_inc(centred.sem, 1)

            def activations(self, act):
                act.wait_ge(loaded.sem, loaded.at(16 * self.LOADS))

                def body(i, first):
                    for q in range(QUADS):
                        n = i * QUADS + q
                        r = q % 2
                        act.wait_ge(made.sem, made.at(n + 1))
                        act.activation(self.hid[:, r, :], self.half_a, ACT.Relu, bias=self.be1).then_inc(evac.sem, 1)
                        if not (first and q < 1):
                            self.take_b(act, n - 1, (q + 1) % 2, not (first and q < 3))
                        act.wait_ge(ring_in[4 + q].sem, ring_in[4 + q].at(16 * (i + 1)))
                        if not (first and q < 2):
                            act.wait_ge(copied.sem, copied.at(n - 1))
                        act.activation(self.tw[:, r, :], self.ts_bc[:, q, :], ACT.Sigmoid, scale=self.wt_c, bias=self.bt_c).then_inc(mixed.sem, 1)
                        if not (first and q < 2):
                            self.take_output(act, n - 2, r, None if first and q < 4 else 32 * i + 16 * ((q - 2) // 2))
                trips(act, body)
                m = ALL_QUADS - 1
                act.wait_ge(turned.sem, turned.at(m + 1))
                self.take_b(act, m, m % 2, True)
                for m in range(ALL_QUADS - 2, ALL_QUADS):
                    self.take_output(act, m, m % 2, 16 * (m // 2))

            def mix(self, dve, m, r):
                dve.wait_ge(squared.sem, squared.at(m + 1))
                dve.wait_ge(mixed.sem, mixed.at(m + 1))
                dve.tensor_tensor(self.ef[:, r, :], self.ef[:, r, :], self.tw[:, r, :], ALU.mult).then_inc(copied.sem, 1)

            def join(self, i, q, first):
                if not (first and q < 1):
                    self.mix(nc.vector, i * QUADS + q - 1, (q + 1) % 2)

            def join_last(self, dve):
                self.mix(dve, ALL_QUADS - 1, (ALL_QUADS - 1) % 2)

            def over(self):
                loaded.base += 16 * self.LOADS
                for s in (made, evac, turned, copied, rooted, centred, squared, mixed):
                    s.base += ALL_QUADS
                for s in ring_in[0:8]:
                    s.base += 16 * TRIPS
                for s in edge_out:
                    s.base += 16 * (ALL_QUADS // 2)

        loads = [(wts[:, 0:3, :], A["L0_neigh"].rearrange("l f o -> f l o")),
                 (wts[:, 3:6, :], A["L0_root"].rearrange("l f o -> f l o")),
                 (bc[:, 0, :], over_nodes(A["L0_gnn_ln_w"][L0 - 1])), (bc[:, 1, :], over_nodes(A["L0_gnn_ln_b"][L0 - 1]))]
        for l in range(L0):
            loads += [(vecs[:, l:l + 1], col(A["L0_gnn_ln_w"][l])), (vecs[:, 3 + l:4 + l], col(A["L0_gnn_ln_b"][l]))]

        for l in range(L0):
            if l == 0:
                table_phase(Xn, loads=loads, w=wts[:, 0, :])
            else:
                table_phase(Hn, scale=vecs[:, l - 1:l], bias=vecs[:, 2 + l:3 + l], w=wts[:, l, :])
            aggregate_phase(table, w_s, sums=(l == 0), edges=EdgeShare(l - 1) if l else None)
            with nc.Block() as block:
                @block.sync
                def _(sp):
                    sp.dma_start(brow[:, :], one_row(A["L0_gnn_lin_root_b"][l])).then_inc(loaded.sem, 16)

                @block.scalar
                def _(act):
                    act.wait_ge(mixed.sem, mixed.at(1))
                    act.activation(Hn[:, :, :].rearrange("p b f -> p (b f)"), HF[:, :], ACT.Relu).then_inc(evac.sem, 1)
                    normalise_act(act, Hn[:, :, :])

                @block.tensor
                def _(pe):
                    pe.wait_ge(loaded.sem, loaded.at(16))
                    pe.wait_ge(copied.sem, copied.at(1))
                    fill_rows(pe, brow[:, :])
                    for b in range(NB):
                        mm = pe.matmul(accf[:, b * P:(b + 1) * P], XT[:, b * P:(b + 1) * P], wts[:, 3 + l, :], start=False,
                                       stop=True, skip_group_check=True)
                    mm.then_inc(made.sem, 1)

                @block.vector
                def _(dve):
                    ch = Chain(dve, vdone)
                    if l == 0:
                        ch(dve.tensor_scalar(rsum[:, :], misc[:, 0:NB], 1.0, None, ALU.max))
                        ch(dve.reciprocal(rsum[:, :], rsum[:, :]))
                    hf = HF[:, :].rearrange("p (b f) -> p b f", f=H)
                    dve.tensor_tensor(hf, acc_nodes, full(rsum[:, :]), ALU.mult).then_inc(copied.sem, 1)
                    dve.wait_ge(copied.sem, copied.at(1))
                    dve.wait_ge(made.sem, made.at(1))
                    dve.tensor_tensor(hf, hf, acc_nodes, ALU.add).then_inc(mixed.sem, 1)
                    dve.wait_ge(evac.sem, evac.at(1))
                    ch(normalise(ch, dve, Hn[:, :, :], Hn[:, :, :]))
                    if l == L0 - 1:
                        ch(dve.tensor_tensor(Hn[:, :, :], Hn[:, :, :], bc[:, 0:1, :].to_broadcast([P, NB, H]), ALU.mult))
                        ch(dve.tensor_tensor(Hn[:, :, :], Hn[:, :, :], bc[:, 1:2, :].to_broadcast([P, NB, H]), ALU.add))
                        ch(dve.tensor_tensor(Xn[:, :, :], Xn[:, :, :], Hn[:, :, :], ALU.add))
                    ch.close()
            loaded.base += 16
            for s in (evac, made, mixed, copied):
                s.base += 1
            normalised()
        residual_norm_phase()

        Wn1a, Wn2 = wts[:, 0, :], wts[:, 1, :]
        loads = [(Wn1a, A["L1_gnn_Wn1"][0:H, :]), (Wn2, A["L1_gnn_Wn2"]),
                 (brow[:, :], one_row(A["L1_gnn_bn1"])), (bc[:, 0, :], over_nodes(A["L1_gnn_bn2"]))]

        table_phase(Xn, loads=loads, w=Wn1a, row=brow[:, :])
        share = arena[:, 0:HALF * H].rearrange("p (r f) -> p r f", r=HALF)
        hidden = arena[:, 2048:2048 + HALF * H].rearrange("p (r f) -> p r f", r=HALF)
        relu_h = arena[:, 4096:4096 + HALF * H].rearrange("p (r f) -> p r f", r=HALF)
        with nc.Block() as block:
            @block.gpsimd
            def _(pool):
                gathers(pool, table, H)

            @block.sync
            def _(sp):
                def body(i, first):
                    for u in range(U):
                        j = i * U + u
                        t = nc.values_load(tile_i[0:1, ds(j, 1)], engines=(sp.engine,), min_val=0, max_val=TILES - 1,
                                           skip_runtime_bounds_check_because="a tile number by construction")
                        if u % 4 == 0 and not (first and u < HALF):
                            sp.wait_ge(mixed.sem, mixed.at(i * QUADS + u // 4 - 1))
                        sp.dma_start(share[:, u % HALF, :], edge_part[ds(t, 1), :, :].rearrange("a e f -> (a e) f")).then_inc(ring_in[u % HALF].sem, 16)
                trips(sp, body)

            @block.vector
            def _(dve):
                def join(i, q, first):
                    n = i * QUADS + q
                    r = 4 * (q % 2)
                    for u in range(4 * q, 4 * q + 4):
                        dve.wait_ge(gathered[u].sem, gathered[u].at(16 * (i + 1)))
                        dve.wait_ge(ring_in[u % HALF].sem, ring_in[u % HALF].at(32 * i + 16 * (u // HALF) + 16))
                    if not (first and q < 2):
                        dve.wait_ge(evac.sem, evac.at(n - 1))
                    dve.tensor_tensor(hidden[:, r:r + 4, :], share[:, r:r + 4, :], G[:, 4 * q:4 * q + 4, 0:H], ALU.add).then_inc(mixed.sem, 1)
                onehots(dve, None, join)

            @block.scalar
            def _(act):
                def body(i, first):
                    for q in range(QUADS):
                        n = i * QUADS + q
                        r = 4 * (q % 2)
                        act.wait_ge(mixed.sem, mixed.at(n + 1))
                        if not (first and q < 2):
                            act.wait_ge(quad_done.sem, quad_done.at(n - 1))
                        act.activation(relu_h[:, r:r + 4, :], hidden[:, r:r + 4, :], ACT.Relu).then_inc(evac.sem, 1)
                trips(act, body)

            @block.tensor
            def _(pe):
                fill_rows(pe, None)
                pe.matmul(misc[:, 0:NB], ident[:, :], zeros[:, 0:NB], start=True, stop=False, skip_group_check=True)

                def body(i, first):
                    for u in range(U):
                        if u % 4 == 0:
                            blocks = quad_blocks(pe, i * QUADS + u // 4)
                            pe.wait_ge(onehot_ready.sem, onehot_ready.at(i * QUADS + u // 4 + 1))
                            pe.wait_ge(evac.sem, evac.at(i * QUADS + u // 4 + 1))
                        o, b = onehot[:, u % HALF, :], blocks[u % 4]
                        pe.matmul(misc[:, ds(b, 1)], o, ones[:, 0:1], start=False, stop=False, skip_group_check=True)
                        mm = pe.matmul(accf[:, ds(b * P, P)], relu_h[:, u % HALF, :], o,
                                       start=False, stop=False, skip_group_check=True)
                        if u % 4 == 3:
                            mm.then_inc(quad_done.sem, 1)
                trips(pe, body)
        gather_pass_over()
        mixed.base += ALL_QUADS
        evac.base += ALL_QUADS
        for s in ring_in:
            s.base += 32 * TRIPS

        with nc.Block() as block:
            @block.scalar
            def _(act):
                for k in range(BANKS):
                    a, b, _ = span(k)
                    act.activation(HF[:, a:b], accf[:, a:b], ACT.Copy).then_inc(evac.sem, 1)

            @block.tensor
            def _(pe):
                for k in range(BANKS):
                    pe.wait_ge(evac.sem, evac.at(k + 1))
                    for b in span(k)[2]:
                        mm = pe.matmul(accf[:, b * P:(b + 1) * P], HF[:, b * P:(b + 1) * P], Wn2, start=True, stop=True)
                    mm.then_inc(made.sem, 1)

            @block.vector
            def _(dve):
                ch = Chain(dve, vdone)
                ch(dve.tensor_copy(deg[:, :], misc[:, 0:NB]))
                ch(dve.tensor_tensor(Hn[:, :, :], full(deg[:, :]), bc[:, 0:1, :].to_broadcast([P, NB, H]), ALU.mult))
                ch(dve.scalar_tensor_tensor(Hn[:, :, :].rearrange("p b f -> p (b f)"), Xn[:, :, :].rearrange("p b f -> p (b f)"), 2.0,
                                            Hn[:, :, :].rearrange("p b f -> p (b f)"), ALU.mult, ALU.add))
                dve.wait_ge(made.sem, made.at(BANKS))
                ch(dve.tensor_tensor(Xn[:, :, :], Hn[:, :, :], acc_nodes, ALU.add))
                ch.close()
        evac.base += BANKS
        made.base += BANKS
        residual_norm_phase()


        relw = arena[:, 0:R8 * H]
        RING = 4
        rows8 = arena[:, 2048:2048 + RING * R8 * H].rearrange("p (r c) -> p r c", r=RING)
        Wl = wts[:, 0, :]

        def relation_table_phase(src, W, Wl_dram, b_dram):
            table_phase(src, loads=[(relw, W.rearrange("i r o -> i (r o)")), (Wl, Wl_dram), (brow[:, :], one_row(b_dram))],
                        index=(t8_s, R8))
            with nc.Block() as block:
                @block.tensor
                def _(pe):
                    for b in range(NB):
                        for c in range(2):
                            n = 2 * b + c
                            if n >= 8:
                                pe.wait_ge((evac if c == 0 else copied).sem, (evac if c == 0 else copied).at(b - 3))
                            pe.matmul(ps[:, n % 8, :], XT[:, b * P:(b + 1) * P], relw[:, c * 512:(c + 1) * 512],
                                      start=True, stop=True).then_inc(made.sem, 1)

                @block.scalar
                def _(act):
                    for b in range(NB):
                        act.wait_ge(made.sem, made.at(2 * b + 1))
                        if b >= RING:
                            act.wait_ge(ring_out[b % RING].sem, ring_out[b % RING].at(16 * (b // RING)))
                        act.activation(rows8[:, b % RING, 0:512], ps[:, 2 * b % 8, :], ACT.Copy).then_inc(evac.sem, 1)

                @block.vector
                def _(dve):
                    for b in range(NB):
                        dve.wait_ge(made.sem, made.at(2 * b + 2))
                        if b >= RING:
                            dve.wait_ge(ring_out[b % RING].sem, ring_out[b % RING].at(16 * (b // RING)))
                        dve.tensor_copy(rows8[:, b % RING, 512:1024], ps[:, (2 * b + 1) % 8, :]).then_inc(copied.sem, 1)

                @block.sync
                def _(sp):
                    for b in range(NB):
                        sp.wait_ge(evac.sem, evac.at(b + 1))
                        sp.wait_ge(copied.sem, copied.at(b + 1))
                        sp.dma_start(table8[b * P * R8:(b + 1) * P * R8, :].rearrange("(n r) f -> n (r f)", r=R8),
                                     rows8[:, b % RING, :]).then_inc(ring_out[b % RING].sem, 16)
                    for r in range(RING):
                        sp.wait_ge(ring_out[r].sem, ring_out[r].at(16 * len(range(r, NB, RING))))
            made.base += 2 * NB
            evac.base += NB
            copied.base += NB
            for r in range(RING):
                ring_out[r].base += 16 * len(range(r, NB, RING))

        relation_table_phase(Xn, A["L2_W1"], A["L2_gnn_Wl1"], A["L2_gnn_b1"])
        aggregate_phase(table8, None, root=Wl, row=brow[:, :])
        with nc.Block() as block:
            @block.scalar
            def _(act):
                act.activation(Hn[:, :, :].rearrange("p b f -> p (b f)"), accf[:, 0:NP], ACT.Relu)
        relation_table_phase(Hn, A["L2_W2"], A["L2_gnn_Wl2"], A["L2_gnn_b2"])
        aggregate_phase(table8, None, root=Wl, row=brow[:, :])
        residual_norm_phase(lambda ch, dve: ch(dve.tensor_tensor(Xn[:, :, :], Xn[:, :, :], acc_nodes, ALU.add)))


        LINKS = GSTEPS * P
        Qn = arena[:, 0:NP].rearrange("p (b f) -> p b f", f=H)
        type_w = arena[:, 3200:3200 + NT * 3 * H]
        by_node = arena[:, 9600:9600 + NB * 3 * H]
        sorted_ring = XT[:, 0:8 * H].rearrange("p (r c f) -> p r c f", r=2, c=4)
        sorted_T = XT[:, 8 * H:16 * H].rearrange("p (r c n) -> p r c n", r=2, c=4)
        product_ring = G[:, 0:12, :].rearrange("p a b -> p (a b)")
        block_k = arena[:, 3200:7296].rearrange("p (t c) -> p t c", t=T32)
        block_v = arena[:, 7296:11392].rearrange("p (t c) -> p t c", t=T32)
        raw = arena[:, 11392:12416].rearrange("p (a t o) -> p a t o", a=2, t=T32)
        pri = arena[:, 12416:12448]
        rows32 = arena[:, 12480:12480 + 4 * 2048].rearrange("p (q t c) -> p q t c", q=4, t=8)
        node_cols = G[:, 0, :].rearrange("p (a n) -> p a n", a=2)
        score = arena[:, 3200:3200 + STEPS * HEADS].rearrange("p (s h) -> p s h", h=HEADS)
        onehotT = arena[:, 6528:6528 + 8 * P].rearrange("p (r e) -> p r e", r=2)
        prod = arena[:, 7552:7552 + 8 * H].rearrange("p (r s f) -> p r s f", r=2, s=4)
        scan_in = arena[:, 7600:7600 + LINKS]
        ahead = arena[:, 10928:10928 + LINKS]
        behind = arena[:, 14256:14256 + LINKS]
        rows = arena[0:1, 17600:17600 + 8 * P].rearrange("p (r x) -> p r x", r=8)
        carry = arena[:, 18700:18702]
        gsum = arena[:, 18704:18706]
        rs8 = arena[:, 18720:18720 + NB * HEADS]
        alpha = arena[:, 18940:18940 + NB]
        types_n = arena[:, 18980:18980 + NB].bitcast(I32)
        skip_bc = arena[:, 19010:19010 + NT]
        eq_types = arena[:, 19040:19040 + NB * NT].rearrange("p (b t) -> p b t", t=NT)
        grow = arena[0:1, 20700:20700 + 2 * P].rearrange("p (r x) -> p r x", r=2)
        link = arena[:, 24500 - LINKS - 1:24500]
        vals = arena[:, 7600:7600 + U * H].rearrange("p (r f) -> p r f", r=U)
        msgs = arena[:, 9648:9648 + HALF * H].rearrange("p (r f) -> p r f", r=HALF)
        quad_weights = wts[:, 0, 0:8 * HEADS].rearrange("p (r x) -> p r x", r=2)
        keep = w_s
        g_bc, b_bc = bc[:, 0, :], bc[:, 1, :]
        ff_w = wts[:, 4, :]

        def sort_phase():
            Z = NT * NB
            own = arena[:, 0:Z].rearrange("p (t b) -> p t b", b=NB)
            before = arena[:, 512:512 + Z].rearrange("p (t b) -> p t b", b=NB)
            total, scanned = arena[:, 1024:1024 + Z], arena[:, 1536:1536 + Z]
            tri = arena[:, 2048:2048 + P]
            count, tiles, ends, offset = (arena[:, 2200 + NT * r:2200 + NT * r + NT] for r in range(4))
            whole_i = arena[:, 2300:2300 + NT].bitcast(I32)
            past = arena[:, 2400:2400 + SORT_TILES * NT].rearrange("p (j t) -> p j t", t=NT)
            place = arena[:, 3100:3100 + NB]
            tile_f = arena[:, 3150:3150 + SORT_TILES]
            types = arena[:, 3200:3200 + NB].bitcast(I32)
            with nc.Block() as block:
                @block.sync
                def _(sp):
                    sp.dma_start(types, A["node_type_rows"]).then_inc(loaded.sem, 16)
                    for j in range(SORT_TILES // 4):
                        sp.dma_start(sorted_x[4 * j * P:4 * (j + 1) * P, :].rearrange("(p a) f -> p (a f)", a=4), zeros[:, :]).then_inc(stored.sem, 16)
                    sp.wait_ge(stored.sem, stored.at(16 * (SORT_TILES // 4)))

                @block.gpsimd
                def _(pool):
                    ch = Chain(pool, pdone)
                    ch(pool.memset(tri, 1.0))
                    pool.affine_select(out=tri, in_=tri, compare_op=ALU.is_ge, fill=0.0, base=-1, pattern=[[1, P]],
                                       channel_multiplier=-1).then_inc(go.sem, 1)
                    ch.close()

                @block.tensor
                def _(pe):
                    pe.wait_ge(go.sem, go.at(1))
                    pe.wait_ge(mixed.sem, mixed.at(1))
                    flat = own.rearrange("p t b -> p (t b)")
                    pe.matmul(accf[:, 0:Z], tri, flat, start=True, stop=True)
                    pe.matmul(misc[:, 0:Z], ones[:, :], flat, start=True, stop=True).then_inc(made.sem, 1)

                @block.vector
                def _(dve):
                    ch = Chain(dve, vdone)
                    dve.wait_ge(loaded.sem, loaded.at(16))
                    dve.tensor_tensor(own, types.unsqueeze(1).to_broadcast([P, NT, NB]),
                                      iota_row[:, 0:NT].unsqueeze(2).to_broadcast([P, NT, NB]), ALU.is_equal).then_inc(mixed.sem, 1)
                    dve.wait_ge(mixed.sem, mixed.at(1))
                    dve.wait_ge(made.sem, made.at(1))
                    ch(dve.tensor_copy(before.rearrange("p t b -> p (t b)"), accf[:, 0:Z]))
                    ch(dve.tensor_copy(total, misc[:, 0:Z]))
                    ch(dve.tensor_tensor_scan(scanned, total, zeros[:, 0:Z], 0.0, ALU.add, ALU.add))
                    ch(dve.tensor_tensor(scanned, scanned, total, ALU.subtract))
                    ch(dve.tensor_reduce(count, total.rearrange("p (t b) -> p t b", b=NB), AX.X, ALU.add))
                    ch(dve.tensor_scalar(tiles, count, float(P - 1), None, ALU.add))
                    ch(dve.tensor_copy(whole_i, tiles))
                    ch(dve.tensor_scalar(whole_i, whole_i, 7, None, ALU.arith_shift_right))
                    ch(dve.tensor_copy(tiles, whole_i))
                    ch(dve.tensor_tensor_scan(ends, tiles, zeros[:, 0:NT], 0.0, ALU.add, ALU.add))
                    ch(dve.tensor_tensor(offset, ends, tiles, ALU.subtract))
                    ch(dve.tensor_scalar(offset, offset, float(P), None, ALU.mult))
                    per_type = scanned.rearrange("p (t b) -> p t b", b=NB)
                    ch(dve.tensor_tensor(offset, offset, per_type[:, :, 0], ALU.subtract))
                    ch(dve.tensor_tensor(before, before, per_type, ALU.add))
                    ch(dve.tensor_tensor(before, before, offset.unsqueeze(2).to_broadcast([P, NT, NB]), ALU.add))
                    ch(dve.tensor_tensor(before, before, own, ALU.mult))
                    ch(dve.tensor_reduce(place, before.rearrange("p t b -> p b t"), AX.X, ALU.add))
                    ch(dve.tensor_copy(pos_i[:, :], place))
                    ch(dve.tensor_tensor(past, ends.unsqueeze(1).to_broadcast([P, SORT_TILES, NT]),
                                         iota_row[:, 0:SORT_TILES].unsqueeze(2).to_broadcast([P, SORT_TILES, NT]), ALU.is_le))
                    ch(dve.tensor_reduce(tile_f, past, AX.X, ALU.add))
                    ch(dve.tensor_scalar(tile_f, tile_f, float(NT - 1), None, ALU.min))
                    ch(dve.tensor_copy(tile_type[:, :], tile_f))
                    ch.close()
            loaded.base += 16
            stored.base += 16 * (SORT_TILES // 4)
            go.base += 1
            mixed.base += 1
            made.base += 1

        def by_type_phase(src, weights, sorted_y, dst):
            C = len(weights) * H
            wall = type_w[:, 0:NT * C].rearrange("p (t c) -> p t c", t=NT)
            out_ring = product_ring[:, 0:8 * C].rearrange("p (r c f) -> p r c f", r=2, c=4)
            groups = SORT_TILES // 4
            n_trips = groups // 2
            with nc.Block() as block:
                @block.gpsimd
                def _(pool):
                    for b in range(NB):
                        pool.indirect_dma_start(sorted_x, bass.IndirectOffsetOnAxis(ap=pos_i[:, b:b + 1], axis=0),
                                                src[:, b, :], None).then_inc(placed.sem, 16)
                    for r in range(2):
                        pool.wait_ge(ring_out[r].sem, ring_out[r].at(16 * n_trips))
                    for b in range(NB):
                        pool.indirect_dma_start(dst[:, b * C:(b + 1) * C], None, sorted_y,
                                                bass.IndirectOffsetOnAxis(ap=pos_i[:, b:b + 1], axis=0)).then_inc(fetched.sem, 16)
                    pool.wait_ge(fetched.sem, fetched.at(16 * NB))

                @block.sync
                def _(sp):
                    for w, W in enumerate(weights):
                        sp.dma_start(wall[:, :, w * H:(w + 1) * H], W.rearrange("t f o -> f t o")).then_inc(loaded.sem, 16)
                    sp.wait_ge(placed.sem, placed.at(16 * NB))

                    def load(g, r):
                        sp.dma_start(sorted_ring[:, r, :, :], sorted_x[ds(g * 4 * P, 4 * P), :].rearrange("(c p) f -> p c f", p=P)).then_inc(ring_in[r].sem, 16)

                    def store(g, r):
                        sp.wait_ge(copied.sem, copied.at(4 * g + 4))
                        sp.dma_start(sorted_y[ds(g * 4 * P, 4 * P), :].rearrange("(c p) f -> p c f", p=P), out_ring[:, r, :, :]).then_inc(ring_out[r].sem, 16)
                    load(0, 0)
                    load(1, 1)
                    with sp.Fori(0, n_trips - 1) as i:
                        for r in range(2):
                            store(2 * i + r, r)
                            load(2 * i + 2 + r, r)
                    for r in range(2):
                        store(2 * (n_trips - 1) + r, r)

                @block.tensor
                def _(pe):
                    pe.wait_ge(loaded.sem, loaded.at(16 * len(weights)))

                    def body(i, first):
                        for r in range(2):
                            g = 2 * i + r
                            pe.wait_ge(ring_in[r].sem, ring_in[r].at(16 * (i + 1)))
                            if not first:
                                pe.wait_ge(evac.sem, evac.at(g - 1))
                            for c in range(4):
                                mm = pe.transpose(ps[:, r, c * P:(c + 1) * P], sorted_ring[:, r, c, :], ident[:, :])
                            mm.then_inc(turned.sem, 1)
                        for r in range(2):
                            g = 2 * i + r
                            pe.wait_ge(evac.sem, evac.at(g + 1))
                            for c in range(4):
                                t = nc.values_load(tile_type[0:1, ds(4 * g + c, 1)], engines=(pe.engine,), min_val=0, max_val=NT - 1,
                                                   skip_runtime_bounds_check_because="a node type by construction")
                                if not (first and r == 0):
                                    pe.wait_ge(copied.sem, copied.at(4 * g + c - 3))
                                pe.matmul(ps[:, 2 + c, 0:C], sorted_T[:, r, c, :], type_w[:, ds(t * C, C)],
                                          start=True, stop=True).then_inc(made.sem, 1)
                    trips(pe, body, n_trips)

                @block.scalar
                def _(act):
                    def body(i, first):
                        for r in range(2):
                            g = 2 * i + r
                            act.wait_ge(turned.sem, turned.at(g + 1))
                            if not first:
                                act.wait_ge(made.sem, made.at(4 * g - 4))
                            act.activation(sorted_T[:, r, :, :].rearrange("p c n -> p (c n)"), ps[:, r, :], ACT.Copy).then_inc(evac.sem, 1)
                    trips(act, body, n_trips)

                @block.vector
                def _(dve):
                    def body(i, first):
                        for r in range(2):
                            g = 2 * i + r
                            if not first:
                                dve.wait_ge(ring_out[r].sem, ring_out[r].at(16 * i))
                            for c in range(4):
                                dve.wait_ge(made.sem, made.at(4 * g + c + 1))
                                dve.tensor_copy(out_ring[:, r, c, :], ps[:, 2 + c, 0:C]).then_inc(copied.sem, 1)
                    trips(dve, body, n_trips)
            loaded.base += 16 * len(weights)
            placed.base += 16 * NB
            fetched.base += 16 * NB
            turned.base += groups
            evac.base += groups
            made.base += SORT_TILES
            copied.base += SORT_TILES
            for r in range(2):
                ring_in[r].base += 16 * n_trips
                ring_out[r].base += 16 * n_trips

        def turn_keys_values_phase():
            kvq = by_node.rearrange("p (b w f) -> p b w f", w=3, f=H)
            with nc.Block() as block:
                @block.tensor
                def _(pe):
                    turn_nodes(pe, kvq[:, :, 0, :], lambda k: None)
                    turn_nodes(pe, kvq[:, :, 1, :], lambda k: pe.wait_ge(evac.sem, evac.at(k + 1)))

                @block.scalar
                def _(act):
                    for k in range(BANKS):
                        a, b, _ = span(k)
                        act.wait_ge(turned.sem, turned.at(k + 1))
                        act.activation(HF[:, a:b], accf[:, a:b], ACT.Copy).then_inc(evac.sem, 1)

                @block.vector
                def _(dve):
                    dve.tensor_copy(Qn, kvq[:, :, 2, :])
                    for k in range(BANKS):
                        a, b, _ = span(k)
                        dve.wait_ge(turned.sem, turned.at(BANKS + k + 1))
                        dve.tensor_copy(Hn[:, :, :].rearrange("p b f -> p (b f)")[:, a:b], accf[:, a:b])
            turned.base += 2 * BANKS
            evac.base += BANKS

        def key_value_table_phase(l):
            kT, vT = HF[:, :], Hn[:, :, :].rearrange("p b f -> p (b f)")
            with nc.Block() as block:
                @block.sync
                def _(sp):
                    sp.dma_start(raw[:, 0, :, :].rearrange("p t o -> p (t o)"), A["L3_Watt"][l]).then_inc(loaded.sem, 16)
                    sp.dma_start(raw[:, 1, :, :].rearrange("p t o -> p (t o)"), A["L3_Wmsg"][l]).then_inc(loaded.sem, 16)
                    for h in range(HEADS):
                        sp.dma_start(pri[h * HS:(h + 1) * HS, :], A["L3_gnn_pri"][l, h].partition_broadcast(HS)).then_inc(loaded.sem, 16)

                    def body(i, first):
                        for q in range(4):
                            sp.wait_ge(copied.sem, copied.at(4 * i + q + 1))
                            sp.dma_start(table32.rearrange("(n t) f -> n t f", t=T32)[ds(i * P, P), q * 8:(q + 1) * 8, :],
                                         rows32[:, q, :, :]).then_inc(ring_out[q].sem, 16)
                    trips(sp, body, NB)
                    for q in range(4):
                        sp.wait_ge(ring_out[q].sem, ring_out[q].at(16 * NB))

                @block.gpsimd
                def _(pool):
                    def body(i, first):
                        if not first:
                            pool.wait_ge(made.sem, made.at(4 * i))
                        pool.tensor_copy(node_cols[:, 0, :], kT[:, ds(i * P, P)]).then_inc(idx_ready.sem, 1)
                        if not first:
                            pool.wait_ge(turned.sem, turned.at(4 * i))
                        pool.tensor_copy(node_cols[:, 1, :], vT[:, ds(i * P, P)]).then_inc(go.sem, 1)
                    trips(pool, body, NB)

                @block.tensor
                def _(pe):
                    pe.wait_ge(centred.sem, centred.at(2))

                    def body(i, first):
                        for q in range(4):
                            n = 4 * i + q
                            s = 4 * (q % 2)
                            if q == 0:
                                pe.wait_ge(idx_ready.sem, idx_ready.at(i + 1))
                            if not (first and q < 2):
                                pe.wait_ge(evac.sem, evac.at(n - 1))
                            for c in range(2):
                                mm = pe.matmul(ps[:, s + c, :], node_cols[:, 0, :],
                                               block_k[:, 8 * q + 4 * c:8 * q + 4 * c + 4, :].rearrange("p t c -> p (t c)"), start=True, stop=True)
                            mm.then_inc(made.sem, 1)
                            if q == 0:
                                pe.wait_ge(go.sem, go.at(i + 1))
                            if not (first and q < 2):
                                pe.wait_ge(copied.sem, copied.at(n - 1))
                            for c in range(2):
                                mm = pe.matmul(ps[:, s + 2 + c, :], node_cols[:, 1, :],
                                               block_v[:, 8 * q + 4 * c:8 * q + 4 * c + 4, :].rearrange("p t c -> p (t c)"), start=True, stop=True)
                            mm.then_inc(turned.sem, 1)
                    trips(pe, body, NB)

                @block.scalar
                def _(act):
                    def body(i, first):
                        for q in range(4):
                            act.wait_ge(made.sem, made.at(4 * i + q + 1))
                            if not first:
                                act.wait_ge(ring_out[q].sem, ring_out[q].at(16 * i))
                            act.activation(rows32[:, q, :, 0:H], ps[:, 4 * (q % 2):4 * (q % 2) + 2, :].rearrange("p a (t f) -> p (a t) f", f=H),
                                           ACT.Copy).then_inc(evac.sem, 1)
                    trips(act, body, NB)

                @block.vector
                def _(dve):
                    ch = Chain(dve, vdone)
                    dve.wait_ge(loaded.sem, loaded.at(16 * (2 + HEADS)))
                    ch(dve.tensor_tensor(raw[:, 0, :, :], raw[:, 0, :, :], pri.unsqueeze(2).to_broadcast([P, T32, HS]), ALU.mult))
                    ch(dve.tensor_scalar(raw[:, 0, :, :], raw[:, 0, :, :], 1.0 / HS ** 0.5, None, ALU.mult))
                    for n, blk in enumerate((block_k, block_v)):
                        dve.tensor_tensor(blk.rearrange("p t (h o) -> p t h o", o=HS),
                                          raw[:, n, :, :].unsqueeze(2).to_broadcast([P, T32, HEADS, HS]),
                                          head_mask[:, :].unsqueeze(1).unsqueeze(3).to_broadcast([P, T32, HEADS, HS]),
                                          ALU.mult).then_inc(centred.sem, 1)

                    def body(i, first):
                        for q in range(4):
                            dve.wait_ge(turned.sem, turned.at(4 * i + q + 1))
                            dve.wait_ge(evac.sem, evac.at(4 * i + q + 1))
                            if not first:
                                dve.wait_ge(ring_out[q].sem, ring_out[q].at(16 * i))
                            dve.tensor_copy(rows32[:, q, :, H:2 * H],
                                            ps[:, 4 * (q % 2) + 2:4 * (q % 2) + 4, :].rearrange("p a (t f) -> p (a t) f", f=H)).then_inc(copied.sem, 1)
                    trips(dve, body, NB)
                    ch.close()
            loaded.base += 16 * (2 + HEADS)
            idx_ready.base += NB
            go.base += NB
            centred.base += 2
            for s in (made, turned, evac, copied):
                s.base += 4 * NB
            for q in range(4):
                ring_out[q].base += 16 * NB

        def score_phase():
            with nc.Block() as block:
                @block.gpsimd
                def _(pool):
                    def free(pool, i, h):
                        pool.wait_ge(mixed.sem, mixed.at(i * QUADS - QUADS + 2 * h + 2))
                        for q in range(2 * h, 2 * h + 2):
                            pool.wait_ge(ring_out[q].sem, ring_out[q].at(16 * i))
                    gathers(pool, table32, 2 * H, free)

                @block.sync
                def _(sp):
                    def body(i, first):
                        for q in range(QUADS):
                            for u in range(4 * q, 4 * q + 4):
                                sp.wait_ge(gathered[u].sem, gathered[u].at(16 * (i + 1)))
                            sp.dma_start(values[ds(i * U + 4 * q, 4), :, :].rearrange("a e f -> e a f"),
                                         G[:, 4 * q:4 * q + 4, H:2 * H]).then_inc(ring_out[q].sem, 16)
                    trips(sp, body)
                    for q in range(QUADS):
                        sp.wait_ge(ring_out[q].sem, ring_out[q].at(16 * TRIPS))

                @block.vector
                def _(dve):
                    def multiply(i, q, first):
                        n = i * QUADS + q
                        for u in range(4 * q, 4 * q + 4):
                            dve.wait_ge(gathered[u].sem, gathered[u].at(16 * (i + 1)))
                        dve.wait_ge(made.sem, made.at(n + 1))
                        if not (first and q < 2):
                            dve.wait_ge(copied.sem, copied.at(n - 1))
                        dve.tensor_tensor(prod[:, q % 2, :, :], G[:, 4 * q:4 * q + 4, 0:H],
                                          ps[:, 4 + q, :].rearrange("p (s f) -> p s f", f=H), ALU.mult).then_inc(mixed.sem, 1)

                    def reduce(i, q):
                        n = i * QUADS + q
                        dve.wait_ge(mixed.sem, mixed.at(n + 1))
                        dve.tensor_reduce(score[:, ds(i * U + 4 * q, 4), :].rearrange("p s h -> p (s h)"),
                                          prod[:, q % 2, :, :].rearrange("p s (h o) -> p (s h) o", o=HS), AX.X, ALU.add).then_inc(copied.sem, 1)

                    def lagged(i, q, first):
                        if not (first and q < 2):
                            multiply(i if q >= 2 else i - 1, (q - 2) % QUADS, first)
                        if not (first and q < 3):
                            reduce(i if q >= 3 else i - 1, (q - 3) % QUADS)
                    onehots(dve, None, lagged)
                    for q in range(QUADS - 2, QUADS):
                        multiply(TRIPS - 1, q, False)
                        reduce(TRIPS - 1, q - 1)
                    reduce(TRIPS - 1, QUADS - 1)

                @block.scalar
                def _(act):
                    def body(i, first):
                        for q in range(QUADS):
                            n = i * QUADS + q
                            act.wait_ge(quad_done.sem, quad_done.at(n + 1))
                            if not (first and q < 2):
                                act.wait_ge(made.sem, made.at(n - 1))
                            act.activation(onehotT[:, q % 2, :], ps[:, q, :], ACT.Copy).then_inc(evac.sem, 1)
                    trips(act, body)

                @block.tensor
                def _(pe):
                    def turn(i, q, fresh):
                        n = i * QUADS + q
                        pe.wait_ge(onehot_ready.sem, onehot_ready.at(n + 1))
                        if not fresh:
                            pe.wait_ge(evac.sem, evac.at(n - 3))
                        for c in range(4):
                            mm = pe.transpose(ps[:, q, c * P:(c + 1) * P], onehot[:, 4 * (q % 2) + c, :], ident[:, :])
                        mm.then_inc(quad_done.sem, 1)

                    def query(i, q, fresh):
                        n = i * QUADS + q
                        blocks = quad_blocks(pe, i * QUADS + q)
                        pe.wait_ge(evac.sem, evac.at(n + 1))
                        if not fresh:
                            pe.wait_ge(mixed.sem, mixed.at(n - 3))
                        for c, b in enumerate(blocks):
                            mm = pe.matmul(ps[:, 4 + q, c * P:(c + 1) * P], onehotT[:, q % 2, c * P:(c + 1) * P],
                                           Qn_flat[:, ds(b * P, P)], start=True, stop=True)
                        mm.then_inc(made.sem, 1)

                    def body(i, first):
                        for q in range(QUADS):
                            turn(i, q, first)
                            if not (first and q < 1):
                                query(i if q >= 1 else i - 1, (q - 1) % QUADS, first)
                    Qn_flat = Qn.rearrange("p b f -> p (b f)")
                    body(0, True)
                    with pe.Fori(1, TRIPS) as i:
                        body(i, False)
                    query(TRIPS - 1, QUADS - 1, False)
            gather_pass_over()
            for s in (mixed, made, copied, evac):
                s.base += ALL_QUADS
            for s in ring_out[0:QUADS]:
                s.base += 16 * TRIPS

        def turn_steps(pe, t):
            for k in range(7):
                for g in range(4 * k, min(GSTEPS, 4 * k + 4)):
                    mm = pe.transpose(accf[:, g * P:(g + 1) * P], t[:, g, :], ident[:, :])
                mm.then_inc(turned.sem, 1)

        def link_phase():
            D = arena[:, 0:LINKS + 1]
            wide = arena[:, 3400:3400 + STEPS * HEADS].rearrange("p (g x) -> p g x", g=GSTEPS)
            with nc.Block() as block:
                @block.vector
                def _(dve):
                    ch = Chain(dve, vdone)
                    dve.tensor_copy(wide.rearrange("p g (c h) -> p g c h", h=HEADS),
                                    dv_s[:, :].rearrange("p (c g) -> p g c", g=GSTEPS).unsqueeze(3).to_broadcast([P, GSTEPS, CHUNKS, HEADS])).then_inc(mixed.sem, 1)
                    ch(dve.tensor_scalar(keep[:, :], dv_s[:, :], 0.0, 2 * BIG, ALU.is_gt, ALU.mult))
                    ch(dve.tensor_scalar(keep[:, :], keep[:, :], BIG, None, ALU.subtract))
                    dve.wait_ge(turned.sem, turned.at(7))
                    dve.tensor_copy(D[:, 1:LINKS + 1], accf[:, 0:LINKS]).then_inc(copied.sem, 1)
                    dve.wait_ge(made.sem, made.at(1))
                    ch(dve.tensor_copy(D[:, 0:1], misc[:, 0:1]))
                    dve.wait_ge(copied.sem, copied.at(1))
                    ch(dve.tensor_tensor(link[:, 0:LINKS], D[:, 1:LINKS + 1], D[:, 0:LINKS], ALU.is_equal))
                    dve.scalar_tensor_tensor(link[:, 0:LINKS], D[:, 1:LINKS + 1], 0.0, link[:, 0:LINKS], ALU.is_equal, ALU.max).then_inc(copied.sem, 1)
                    dve.wait_ge(made.sem, made.at(2))
                    ch(dve.tensor_copy(link[:, LINKS:LINKS + 1], misc[:, 1:2]))
                    ch(dve.tensor_scalar(link, link, 2 * BIG, -BIG, ALU.mult, ALU.add))
                    ch(dve.tensor_reduce(gsum[:, 0:1], link[:, 0:LINKS], AX.X, ALU.min))
                    dve.tensor_reduce(gsum[:, 1:2], link[:, 1:LINKS + 1], AX.X, ALU.min).then_inc(copied.sem, 1)
                    dve.wait_ge(turned.sem, turned.at(8))
                    ch(dve.tensor_copy(grow[:, 0, :].rearrange("p (h c) -> p h c", h=HEADS), ps[0:1, 0, 0:P].rearrange("p (c h) -> p h c", h=HEADS)))
                    ch(dve.tensor_copy(grow[:, 1, :].rearrange("p (h c) -> p h c", h=HEADS),
                                       ps[0:1, 1, 0:P].rearrange("p (c h) -> p h c", h=HEADS)[:, :, ::-1]))
                    ch.close()

                @block.tensor
                def _(pe):
                    pe.wait_ge(mixed.sem, mixed.at(1))
                    turn_steps(pe, wide)
                    pe.wait_ge(copied.sem, copied.at(1))
                    pe.matmul(misc[:, 0:1], shift[:, 0, :], D[:, LINKS:LINKS + 1], start=True, stop=True).then_inc(made.sem, 1)
                    pe.wait_ge(copied.sem, copied.at(2))
                    pe.matmul(misc[:, 1:2], shift[:, 1, :], link[:, 0:1], start=True, stop=True).then_inc(made.sem, 1)
                    pe.wait_ge(copied.sem, copied.at(3))
                    pe.transpose(ps[0:1, 0, 0:P], gsum[:, 0:1], ident[:, :])
                    pe.transpose(ps[0:1, 1, 0:P], gsum[:, 1:2], ident[:, :]).then_inc(turned.sem, 1)
            mixed.base += 1
            turned.base += 8
            copied.base += 3
            made.base += 2

        def softmax_phase():
            wide = arena[:, 14256:14256 + STEPS * HEADS].rearrange("p (g x) -> p g x", g=GSTEPS)
            with nc.Block() as block:
                @block.vector
                def _(dve):
                    ch = Chain(dve, vdone)
                    dve.tensor_tensor(wide.rearrange("p g (c h) -> p g c h", h=HEADS),
                                      score.rearrange("p (c g) h -> p g c h", g=GSTEPS),
                                      keep[:, :].rearrange("p (c g) -> p g c", g=GSTEPS).unsqueeze(3).to_broadcast([P, GSTEPS, CHUNKS, HEADS]),
                                      ALU.min).then_inc(mixed.sem, 1)
                    dve.wait_ge(turned.sem, turned.at(7))
                    ch(dve.tensor_copy(scan_in, accf[:, 0:LINKS]))
                    rev = slice(None, None, -1)

                    def scans(first_f, first_b):
                        ch(dve.tensor_tensor_scan(ahead, link[:, 0:LINKS], scan_in, first_f, ALU.min, ALU.max))
                        return dve.tensor_tensor_scan(behind[:, rev], link[:, 1:LINKS + 1][:, rev], scan_in[:, rev], first_b, ALU.min, ALU.max)
                    scans(-BIG, -BIG).then_inc(copied.sem, 1)
                    dve.wait_ge(turned.sem, turned.at(8))
                    ch(dve.tensor_copy(rows[:, 0, :].rearrange("p (h c) -> p h c", h=HEADS), ps[0:1, 0, 0:P].rearrange("p (c h) -> p h c", h=HEADS)))
                    ch(dve.tensor_copy(rows[:, 1, :].rearrange("p (h c) -> p h c", h=HEADS),
                                       ps[0:1, 1, 0:P].rearrange("p (c h) -> p h c", h=HEADS)[:, :, rev]))
                    for r in range(2):
                        ch(dve.tensor_tensor_scan(rows[:, 2 + r, :], grow[:, r, :], rows[:, r, :], -BIG, ALU.min, ALU.max))
                        ch(dve.memset(rows[:, 4 + r, :], -BIG))
                    out_f = rows[:, 4, :].rearrange("p (c h) -> p h c", h=HEADS)
                    out_b = rows[:, 5, :].rearrange("p (c h) -> p h c", h=HEADS)
                    in_f = rows[:, 2, :].rearrange("p (h c) -> p h c", h=HEADS)
                    in_b = rows[:, 3, :].rearrange("p (h c) -> p h c", h=HEADS)
                    ch(dve.tensor_copy(out_f[:, :, 1:CHUNKS], in_f[:, :, 0:CHUNKS - 1]))
                    dve.tensor_copy(out_b[:, :, rev][:, :, 1:CHUNKS], in_b[:, :, 0:CHUNKS - 1]).then_inc(copied.sem, 1)
                    dve.wait_ge(turned.sem, turned.at(9))
                    ch(dve.tensor_copy(carry, misc[:, 0:2]))
                    ch(scans(carry[:, 0:1], carry[:, 1:2]))
                    ch(dve.tensor_tensor(ahead, ahead, behind, ALU.max))
                    dve.tensor_tensor(scan_in, scan_in, ahead, ALU.subtract).then_inc(copied.sem, 1)
                    for k in range(7):
                        g0, g1 = 4 * k, min(GSTEPS, 4 * k + 4)
                        dve.wait_ge(turned.sem, turned.at(10 + k))
                        dve.tensor_copy(score.rearrange("p (c g) h -> p g c h", g=GSTEPS)[:, g0:g1, :, :],
                                        accf[:, g0 * P:g1 * P].rearrange("p (g c h) -> p g c h", c=CHUNKS, h=HEADS))
                    ch.close()

                @block.scalar
                def _(act):
                    act.wait_ge(copied.sem, copied.at(3))
                    act.activation(scan_in, scan_in, ACT.Exp).then_inc(evac.sem, 1)

                @block.tensor
                def _(pe):
                    pe.wait_ge(mixed.sem, mixed.at(1))
                    turn_steps(pe, wide)
                    pe.wait_ge(copied.sem, copied.at(1))
                    pe.transpose(ps[0:1, 0, 0:P], ahead[:, LINKS - 1:LINKS], ident[:, :])
                    pe.transpose(ps[0:1, 1, 0:P], behind[:, 0:1], ident[:, :]).then_inc(turned.sem, 1)
                    pe.wait_ge(copied.sem, copied.at(2))
                    pe.transpose(misc[:, 0:1], rows[:, 4, :], ident[0:1, 0:1])
                    pe.transpose(misc[:, 1:2], rows[:, 5, :], ident[0:1, 0:1]).then_inc(turned.sem, 1)
                    pe.wait_ge(evac.sem, evac.at(1))
                    turn_steps(pe, scan_in.rearrange("p (g e) -> p g e", e=P))
            mixed.base += 1
            turned.base += 16
            copied.base += 3
            evac.base += 1

        def message_phase():
            with nc.Block() as block:
                @block.sync
                def _(sp):
                    def body(i, first):
                        for q in range(QUADS):
                            if not first:
                                sp.wait_ge(mixed.sem, mixed.at(i * QUADS + q - 3))
                            sp.dma_start(vals[:, 4 * q:4 * q + 4, :],
                                         values[ds(i * U + 4 * q, 4), :, :].rearrange("a e f -> e a f")).then_inc(ring_in[q].sem, 16)
                    trips(sp, body)

                @block.vector
                def _(dve):
                    def weigh(i, q, first):
                        dve.wait_ge(ring_in[q].sem, ring_in[q].at(16 * (i + 1)))
                        r = 4 * (q % 2)
                        dve.tensor_tensor(msgs[:, r:r + 4, :].rearrange("p s (h o) -> p (s h) o", o=HS),
                                          vals[:, 4 * q:4 * q + 4, :].rearrange("p s (h o) -> p (s h) o", o=HS),
                                          score[:, ds(i * U + 4 * q, 4), :].rearrange("p s h -> p (s h)").unsqueeze(2).to_broadcast([P, 4 * HEADS, HS]),
                                          ALU.mult).then_inc(mixed.sem, 1)
                    onehots(dve, None, weigh)

                @block.gpsimd
                def _(pool):
                    def body(i, first):
                        for q in range(QUADS):
                            n = i * QUADS + q
                            if not (first and q < 2):
                                pool.wait_ge(quad_done.sem, quad_done.at(n - 1))
                            pool.tensor_copy(quad_weights[:, q % 2, :],
                                             score[:, ds(i * U + 4 * q, 4), :].rearrange("p s h -> p (s h)")).then_inc(idx_ready.sem, 1)
                    trips(pool, body)

                @block.tensor
                def _(pe):
                    fill_rows(pe, None)
                    pe.matmul(misc[:, 0:NB * HEADS], ident[:, :], zeros[:, 0:NB * HEADS], start=True, stop=False, skip_group_check=True)

                    def body(i, first):
                        for q in range(QUADS):
                            blocks = quad_blocks(pe, i * QUADS + q)
                            pe.wait_ge(mixed.sem, mixed.at(i * QUADS + q + 1))
                            pe.wait_ge(idx_ready.sem, idx_ready.at(i * QUADS + q + 1))
                            for c, b in enumerate(blocks):
                                o = onehot[:, 4 * (q % 2) + c, :]
                                pe.matmul(misc[:, ds(b * HEADS, HEADS)], o, quad_weights[:, q % 2, c * HEADS:(c + 1) * HEADS],
                                          start=False, stop=False, skip_group_check=True)
                                mm = pe.matmul(accf[:, ds(b * P, P)], o, msgs[:, 4 * (q % 2) + c, :],
                                               start=False, stop=False, skip_group_check=True)
                            mm.then_inc(quad_done.sem, 1)
                    trips(pe, body)
            quad_pass_over()
            idx_ready.base += ALL_QUADS
            mixed.base += ALL_QUADS
            for s in ring_in[0:QUADS]:
                s.base += 16 * TRIPS

        for l in range(2):
            if l == 0:
                with nc.Block() as block:
                    @block.gpsimd
                    def _(pool):
                        pool.tensor_copy(Lx[:, :, :], Xn[:, :, :])

                    @block.vector
                    def _(dve):
                        ch = Chain(dve, vdone)
                        ch(dve.scalar_tensor_tensor(w1_f, src_s[:, :], float(T32), t32_s[:, :], ALU.mult, ALU.add))
                        ch(dve.tensor_copy(idx_s[:, :], w1_f))
                        ch.close()
                link_phase()
                sort_phase()
            by_type_phase(Lx, [A["L3_gnn_Wk"][l], A["L3_gnn_Wv"][l], A["L3_gnn_Wq"][l]], sorted_kvq, by_node)
            turn_keys_values_phase()
            key_value_table_phase(l)
            score_phase()
            softmax_phase()
            message_phase()
            with nc.Block() as block:
                @block.vector
                def _(dve):
                    ch = Chain(dve, vdone)
                    ch(dve.tensor_scalar(rs8, misc[:, 0:NB * HEADS], 1e-20, None, ALU.max))
                    ch(dve.reciprocal(rs8, rs8))
                    ch(dve.tensor_tensor(Hn[:, :, :].rearrange("p b (h o) -> p (b h) o", o=HS),
                                         accf[:, 0:NP].rearrange("p (x o) -> p x o", o=HS),
                                         rs8.unsqueeze(2).to_broadcast([P, NB * HEADS, HS]), ALU.mult))
                    ch.close()
            by_type_phase(Hn, [A["L3_gnn_Wa"][l]], sorted_a, HF[:, :])
            with nc.Block() as block:
                @block.sync
                def _(sp):
                    sp.dma_start(skip_bc, over_nodes(A["L3_gnn_skip"][l])).then_inc(loaded.sem, 16)
                    sp.dma_start(types_n, A["node_type_rows"]).then_inc(loaded.sem, 16)
                    sp.dma_start(g_bc, over_nodes(A["L3_gnn_ln_g"][l])).then_inc(loaded.sem, 16)
                    sp.dma_start(b_bc, over_nodes(A["L3_gnn_ln_b"][l])).then_inc(loaded.sem, 16)

                @block.scalar
                def _(act):
                    act.activation(Hn[:, :, :].rearrange("p b f -> p (b f)"), HF[:, :], ACT.Sigmoid).then_inc(evac.sem, 1)
                    act.wait_ge(loaded.sem, loaded.at(64))
                    act.activation(skip_bc, skip_bc, ACT.Sigmoid).then_inc(evac.sem, 1)
                    normalise_act(act, Hn[:, :, :])

                @block.vector
                def _(dve):
                    ch = Chain(dve, vdone)
                    dve.wait_ge(loaded.sem, loaded.at(64))
                    dve.wait_ge(evac.sem, evac.at(2))
                    ch(dve.tensor_tensor(eq_types, types_n.unsqueeze(2).to_broadcast([P, NB, NT]),
                                         iota_row[:, 0:NT].unsqueeze(1).to_broadcast([P, NB, NT]), ALU.is_equal))
                    ch(dve.tensor_tensor(eq_types, eq_types, skip_bc.unsqueeze(1).to_broadcast([P, NB, NT]), ALU.mult))
                    ch(dve.tensor_reduce(alpha, eq_types, AX.X, ALU.add))
                    ch(dve.tensor_tensor(Hn[:, :, :], Hn[:, :, :], HF[:, :].rearrange("p (b f) -> p b f", f=H), ALU.mult))
                    ch(dve.tensor_tensor(Hn[:, :, :], Hn[:, :, :], Lx[:, :, :], ALU.subtract))
                    ch(dve.tensor_tensor(Hn[:, :, :], Hn[:, :, :], full(alpha), ALU.mult))
                    ch(dve.tensor_tensor(Hn[:, :, :], Hn[:, :, :], Lx[:, :, :], ALU.add))
                    ch(normalise(ch, dve, Hn[:, :, :], Hn[:, :, :]))
                    ch(dve.tensor_tensor(Hn[:, :, :], Hn[:, :, :], bc[:, 0:1, :].to_broadcast([P, NB, H]), ALU.mult))
                    ch(dve.tensor_tensor(Lx[:, :, :], Hn[:, :, :], bc[:, 1:2, :].to_broadcast([P, NB, H]), ALU.add))
                    ch.close()
            loaded.base += 64
            evac.base += 2
            normalised()

        table_phase(Lx, loads=[(ff_w, A["L3_gnn_ff_w"]), (brow[:, :], one_row(A["L3_gnn_ff_b"]))])
        with nc.Block() as block:
            @block.tensor
            def _(pe):
                fill_rows(pe, brow[:, :])
                for b in range(NB):
                    pe.matmul(accf[:, b * P:(b + 1) * P], XT[:, b * P:(b + 1) * P], ff_w, start=False, stop=False, skip_group_check=True)
        residual_norm_phase(lambda ch, dve: ch(dve.tensor_tensor(Xn[:, :, :], Xn[:, :, :], acc_nodes, ALU.add)))


        with nc.Block() as block:
            @block.sync
            def _(sp):
                sp.dma_start(out[0:(NB - 1) * P, :].rearrange("(b p) f -> p b f", p=P), Xn[:, 0:NB - 1, :]).then_inc(stored.sem, 16)
                sp.dma_start(out[(NB - 1) * P:N, :], Xn[0:LAST, NB - 1, :]).then_inc(stored.sem, 16)
                sp.wait_ge(stored.sem, stored.at(32))

PLAIN = (
    "L0_gnn_lin_root_b",
    "L0_gnn_ln_w",
    "L0_gnn_ln_b",
    "L1_gnn_We1",
    "L1_gnn_be1",
    "L1_gnn_We2",
    "L1_gnn_be2",
    "L1_gnn_Wt",
    "L1_gnn_bt",
    "L1_gnn_Wn1",
    "L1_gnn_bn1",
    "L1_gnn_Wn2",
    "L1_gnn_bn2",
    "L2_gnn_Wl1",
    "L2_gnn_b1",
    "L2_gnn_Wl2",
    "L2_gnn_b2",
    "L3_gnn_Wk",
    "L3_gnn_Wq",
    "L3_gnn_Wv",
    "L3_gnn_Wa",
    "L3_gnn_pri",
    "L3_gnn_skip",
    "L3_gnn_ln_g",
    "L3_gnn_ln_b",
    "L3_gnn_ff_w",
    "L3_gnn_ff_b",
)


def kernel(**inputs):
    import numpy as np
    import concourse.bacc as bacc
    from concourse.bass_utils import run_bass_kernel_spmd

    a = {k: np.asarray(v) for k, v in inputs.items()}
    ints = np.stack([a["src"], a["dst"], a["edge_type_32"], a["edge_type_8"]], axis=1)
    pad = np.full((EP - E, 4), 0, ints.dtype)
    pad[:, 1] = -1
    attr = a["edge_attr_64"]
    types = np.concatenate([a["node_type_16"], np.zeros(NP - N, a["node_type_16"].dtype)])
    arrays = {
        "x": a["x"], "dst": a["dst"],
        "edge_ints": np.ascontiguousarray(np.concatenate([ints, pad])).reshape(TILES, P * 4),
        "edge_w": np.concatenate([a["edge_weight"], np.zeros(EP - E, a["edge_weight"].dtype)]).reshape(TILES, P),
        "edge_attr_T": np.ascontiguousarray(np.concatenate([attr, np.zeros((SHARE_TILES * P - E, EDIM), attr.dtype)]).T),
        "edge_times": np.concatenate([a["edge_weight"], np.zeros(SHARE_TILES * P - E, a["edge_weight"].dtype)]),
        "node_type_rows": np.ascontiguousarray(types.reshape(NB, P).T),
        "L0_neigh": np.ascontiguousarray(a["L0_gnn_lin_neigh_w"].transpose(0, 2, 1)),
        "L0_root": np.ascontiguousarray(a["L0_gnn_lin_root_w"].transpose(0, 2, 1)),
        "L2_W1": np.ascontiguousarray(a["L2_gnn_W1"].transpose(1, 0, 2)),
        "L2_W2": np.ascontiguousarray(a["L2_gnn_W2"].transpose(1, 0, 2)),
        "L3_Watt": np.ascontiguousarray(a["L3_gnn_Watt"].transpose(0, 1, 3, 2, 4)).reshape(2, H, T32 * HS),
        "L3_Wmsg": np.ascontiguousarray(a["L3_gnn_Wmsg"].transpose(0, 1, 3, 2, 4)).reshape(2, H, T32 * HS),
    }
    for name in PLAIN:
        arrays[name] = a[name]

    nc = bacc.Bacc("TRN2", target_bir_lowering=False, num_devices=1)
    aps = {k: nc.dram_tensor(k, v.shape, mybir.dt.from_np(v.dtype), kind="ExternalInput").ap() for k, v in arrays.items()}
    out = nc.dram_tensor("out", (N, H), F32, kind="ExternalOutput").ap()
    build(nc, aps, out)
    r = run_bass_kernel_spmd(nc, [arrays], core_ids=[0])
    return r.results[0]["out"]
```
